# Optimizing a Trainium2 kernel written in Bass

```python
import numpy as np
import jax
import jax.numpy as jnp

def _softmax(x, axis=-1):
    return jax.nn.softmax(x, axis=axis)

def _gelu(x):
    return jax.nn.gelu(x, approximate=True)

def _silu(x):
    return jax.nn.silu(x)

def _sigmoid(x):
    return jax.nn.sigmoid(x)

def _layernorm(x, axis=-1, eps=1e-05):
    m = jnp.mean(x, axis=axis, keepdims=True)
    v = jnp.var(x, axis=axis, keepdims=True)
    return (x - m) / jnp.sqrt(v + eps)

def _scatter_add(tgt, idx, src, axis=0):
    return tgt.at[idx].add(src)

def _segment_sum(src, seg, n):
    return jax.ops.segment_sum(src, seg, n)
kernel_name = 'mk_flamingo_gated_d2_seqx_r8_9461d8'

def setup_inputs(seed: int=0):
    np.random.seed(seed)
    _w = jnp.asarray

    def _rec_inputs():
        import jax
        import jax.numpy as jnp
        _rk = jax.random.key(seed)
        x = 0.002226 + 0.9996 * jax.random.normal(jax.random.fold_in(_rk, 1), (32, 64, 128), jnp.float32)
        _lenS = 64 - jax.random.randint(jax.random.fold_in(_rk, 7), (32,), 0, max(1, 64 // 4) + 1, jnp.int32)
        _lenS2 = 64 - jax.random.randint(jax.random.fold_in(_rk, 8), (32,), 0, max(1, 64 // 4) + 1, jnp.int32)
        _ctx_1024P = jax.random.normal(jax.random.fold_in(_rk, 11), (32, 16, 128), jnp.float32)
        _ctx_1024c = jax.random.dirichlet(jax.random.fold_in(_rk, 511), 0.3 * jnp.ones((16,), jnp.float32), (32, 64))
        _ctx_1024t = jnp.einsum('bsk,bkd->bsd', _ctx_1024c, _ctx_1024P)
        _ctx_1024t = _ctx_1024t * jax.lax.rsqrt(jnp.mean(jnp.square(_ctx_1024t)) + 1e-12) * 0.953939
        ctx_1024 = -7.10856e-05 + 0.999911 * (_ctx_1024t + 0.3 * jax.random.normal(jax.random.fold_in(_rk, 611), (32, 64, 128), jnp.float32))
        _g = jax.random.normal(jax.random.fold_in(_rk, 9001), (2, 2), jnp.float32)
        _g = jnp.sign(_g) * jnp.maximum(jnp.abs(_g), 1.0) + (_g == 0) * 1.0
        g_xattn = _g[0]
        g_ffn = _g[1]
        return (x, ctx_1024, g_xattn, g_ffn)
    x, ctx_1024, g_xattn, g_ffn = _rec_inputs()

    def _L0_xattn_setup():
        import jax, jax.numpy as jnp
        import numpy as np
        DIM = 128
        HEAD_DIM = 64
        NUM_HEADS = 8
        INNER = HEAD_DIM * NUM_HEADS
        ROT_DIM = HEAD_DIM
        ROPE_BASE = 10000.0
        EPS = 1e-05

        def layer_norm(x, g, b):
            mu = jnp.mean(x, axis=-1, keepdims=True)
            var = jnp.var(x, axis=-1, keepdims=True)
            return (x - mu) * jax.lax.rsqrt(var + EPS) * g + b

        def rope_rotate_k(k):
            n = k.shape[1]
            half = ROT_DIM // 2
            inv_freq = 1.0 / ROPE_BASE ** (jnp.arange(0, ROT_DIM, 2, dtype=jnp.float32) / ROT_DIM)
            theta = jnp.arange(n, dtype=jnp.float32)[:, None] * inv_freq[None, :]
            angles = jnp.concatenate([theta, theta], axis=-1)
            cos = jnp.cos(angles)[None, :, None, :].astype(k.dtype)
            sin = jnp.sin(angles)[None, :, None, :].astype(k.dtype)
            k_rope, k_pass = (k[..., :ROT_DIM], k[..., ROT_DIM:])
            neg_half = jnp.concatenate([-k_rope[..., half:], k_rope[..., :half]], axis=-1)
            k_rope = k_rope * cos + neg_half * sin
            return jnp.concatenate([k_rope, k_pass], axis=-1)
        key = jax.random.key(seed)
        ks = jax.random.split(key, 5)
        b, n, m = (8, 1024, 64)
        s = 1.0 / np.sqrt(DIM)
        return {'x': jax.random.normal(ks[0], (b, n, DIM), jnp.float32), 'latents': jax.random.normal(ks[1], (b, m, DIM), jnp.float32), 'gamma_x': jnp.ones((DIM,), jnp.float32), 'beta_x': jnp.zeros((DIM,), jnp.float32), 'gamma_l': jnp.ones((DIM,), jnp.float32), 'beta_l': jnp.zeros((DIM,), jnp.float32), 'Wq': jax.random.normal(ks[2], (DIM, INNER), jnp.float32) * s, 'Wkv': jax.random.normal(ks[3], (DIM, 2 * INNER), jnp.float32) * s, 'Wo': jax.random.normal(ks[4], (INNER, DIM), jnp.float32) * (1.0 / np.sqrt(INNER))}
    _L0_xattn_all = _L0_xattn_setup()
    _L0_xattn_in = {k: v for k, v in _L0_xattn_all.items() if k in ('gamma_x', 'beta_x', 'gamma_l', 'beta_l', 'Wq', 'Wkv', 'Wo')}
    del _L0_xattn_all

    def _L0_ffn_setup():
        import jax, jax.numpy as jnp
        import numpy as np
        DIM = 128

        def _reference_tuple_inner(x, W_r, W_k, W_v, mu_r, mu_k):
            B, T, C = x.shape
            x_prev = jnp.concatenate([jnp.zeros((B, 1, C), x.dtype), x[:, :-1, :]], axis=1)
            xr = mu_r * x + (1.0 - mu_r) * x_prev
            xk = mu_k * x + (1.0 - mu_k) * x_prev
            r = jax.nn.sigmoid(jnp.einsum('btc,dc->btd', xr, W_r))
            k = jnp.einsum('btc,dc->btd', xk, W_k)
            k_act = jnp.square(jax.nn.relu(k))
            out = r * jnp.einsum('btc,dc->btd', k_act, W_v)
            new_state = x[:, -1, :]
            return (out, new_state)
        key = jax.random.key(seed)
        ks = jax.random.split(key, 6)
        B, T, C = (8, 256, DIM)
        x = jax.random.normal(ks[0], (B, T, C), dtype=jnp.float32)
        s = 1.0 / np.sqrt(C)
        W_r = jax.random.uniform(ks[1], (C, C), jnp.float32, -s, s)
        W_k = jax.random.uniform(ks[2], (C, C), jnp.float32, -s, s)
        W_v = jax.random.uniform(ks[3], (C, C), jnp.float32, -s, s)
        mu_r = jax.random.uniform(ks[4], (C,), jnp.float32)
        mu_k = jax.random.uniform(ks[5], (C,), jnp.float32)
        return {'x': x, 'W_r': W_r, 'W_k': W_k, 'W_v': W_v, 'mu_r': mu_r, 'mu_k': mu_k}
    _L0_ffn_all = _L0_ffn_setup()
    _L0_ffn_in = {k: v for k, v in _L0_ffn_all.items() if k in ('W_r', 'W_k', 'W_v', 'mu_r', 'mu_k')}
    del _L0_ffn_all

    def _L1_xattn_setup():
        import jax, jax.numpy as jnp
        import numpy as np
        ROPE_BASE = 10000.0

        def rotate_half(x):
            d = x.shape[-1] // 2
            return jnp.concatenate([-x[..., d:], x[..., :d]], axis=-1)

        def rope_cos_sin(seq_len, head_dim, dtype=jnp.float32):
            inv_freq = 1.0 / ROPE_BASE ** (jnp.arange(0, head_dim, 2, dtype=jnp.float32) / head_dim)
            t = jnp.arange(seq_len, dtype=jnp.float32)
            freqs = jnp.outer(t, inv_freq)
            emb = jnp.concatenate([freqs, freqs], axis=-1)
            return (jnp.cos(emb).astype(dtype), jnp.sin(emb).astype(dtype))

        def alibi_slopes(num_heads):
            return jnp.asarray([2.0 ** (-8.0 * i / num_heads) for i in range(1, num_heads + 1)], dtype=jnp.float32)
        key = jax.random.key(seed)
        k1, k2, k3 = jax.random.split(key, 3)
        B, T, H = (2, 256, 128)
        return {'q': jax.random.normal(k1, (B, T, H), dtype=jnp.float32), 'k': jax.random.normal(k2, (B, T, H), dtype=jnp.float32), 'v': jax.random.normal(k3, (B, T, H), dtype=jnp.float32), 'num_heads': 16}
    _L1_xattn_all = _L1_xattn_setup()
    _L1_xattn_in = {k: v for k, v in _L1_xattn_all.items() if k in ()}
    del _L1_xattn_all

    def _L1_ffn_setup():
        import jax, jax.numpy as jnp
        import numpy as np
        TOP_K = 2
        key = jax.random.key(seed)
        ks = jax.random.split(key, 6)
        B, T, H, E, F = (2, 256, 128, 8, 512)
        s = 0.02
        return {'hidden_states': jax.random.normal(ks[0], (B, T, H), dtype=jnp.float32), 'router_w': jax.random.normal(ks[1], (E, H), dtype=jnp.float32) * s, 'w1': jax.random.normal(ks[2], (E, F, H), dtype=jnp.float32) * s, 'b1': jax.random.normal(ks[3], (E, F), dtype=jnp.float32) * s, 'w2': jax.random.normal(ks[4], (E, H, F), dtype=jnp.float32) * s, 'b2': jax.random.normal(ks[5], (E, H), dtype=jnp.float32) * s}
    _L1_ffn_all = _L1_ffn_setup()
    _L1_ffn_in = {k: v for k, v in _L1_ffn_all.items() if k in ('router_w', 'w1', 'b1', 'w2', 'b2')}
    del _L1_ffn_all
    return {'x': x, 'ctx_1024': ctx_1024, 'g_xattn': g_xattn, 'g_ffn': g_ffn, 'L0_xattn_gamma_x': _L0_xattn_in['gamma_x'], 'L0_xattn_beta_x': _L0_xattn_in['beta_x'], 'L0_xattn_gamma_l': _L0_xattn_in['gamma_l'], 'L0_xattn_beta_l': _L0_xattn_in['beta_l'], 'L0_xattn_Wq': _L0_xattn_in['Wq'], 'L0_xattn_Wkv': _L0_xattn_in['Wkv'], 'L0_xattn_Wo': _L0_xattn_in['Wo'], 'L0_ffn_W_r': _L0_ffn_in['W_r'], 'L0_ffn_W_k': _L0_ffn_in['W_k'], 'L0_ffn_W_v': _L0_ffn_in['W_v'], 'L0_ffn_mu_r': _L0_ffn_in['mu_r'], 'L0_ffn_mu_k': _L0_ffn_in['mu_k'], 'L1_ffn_router_w': _L1_ffn_in['router_w'], 'L1_ffn_w1': _L1_ffn_in['w1'], 'L1_ffn_b1': _L1_ffn_in['b1'], 'L1_ffn_w2': _L1_ffn_in['w2'], 'L1_ffn_b2': _L1_ffn_in['b2']}

def reference(x, ctx_1024, g_xattn, g_ffn, L0_xattn_gamma_x, L0_xattn_beta_x, L0_xattn_gamma_l, L0_xattn_beta_l, L0_xattn_Wq, L0_xattn_Wkv, L0_xattn_Wo, L0_ffn_W_r, L0_ffn_W_k, L0_ffn_W_v, L0_ffn_mu_r, L0_ffn_mu_k, L1_ffn_router_w, L1_ffn_w1, L1_ffn_b1, L1_ffn_w2, L1_ffn_b2):
    import jax
    import jax.numpy as jnp

    def _L0_xattn_ref(x, latents, gamma_x, beta_x, gamma_l, beta_l, Wq, Wkv, Wo):
        import jax, jax.numpy as jnp
        import numpy as np
        DIM = 128
        HEAD_DIM = 64
        NUM_HEADS = 8
        INNER = HEAD_DIM * NUM_HEADS
        ROT_DIM = HEAD_DIM
        ROPE_BASE = 10000.0
        EPS = 1e-05

        def layer_norm(x, g, b):
            mu = jnp.mean(x, axis=-1, keepdims=True)
            var = jnp.var(x, axis=-1, keepdims=True)
            return (x - mu) * jax.lax.rsqrt(var + EPS) * g + b

        def rope_rotate_k(k):
            n = k.shape[1]
            half = ROT_DIM // 2
            inv_freq = 1.0 / ROPE_BASE ** (jnp.arange(0, ROT_DIM, 2, dtype=jnp.float32) / ROT_DIM)
            theta = jnp.arange(n, dtype=jnp.float32)[:, None] * inv_freq[None, :]
            angles = jnp.concatenate([theta, theta], axis=-1)
            cos = jnp.cos(angles)[None, :, None, :].astype(k.dtype)
            sin = jnp.sin(angles)[None, :, None, :].astype(k.dtype)
            k_rope, k_pass = (k[..., :ROT_DIM], k[..., ROT_DIM:])
            neg_half = jnp.concatenate([-k_rope[..., half:], k_rope[..., :half]], axis=-1)
            k_rope = k_rope * cos + neg_half * sin
            return jnp.concatenate([k_rope, k_pass], axis=-1)
        b, n, _ = x.shape
        m = latents.shape[1]
        h, d = (NUM_HEADS, HEAD_DIM)
        scale = d ** (-0.5)
        xn = layer_norm(x, gamma_x, beta_x)
        ln = layer_norm(latents, gamma_l, beta_l)
        q = (ln @ Wq).reshape(b, m, h, d)
        kv_x = xn @ Wkv
        k_x, v_x = (kv_x[..., :INNER], kv_x[..., INNER:])
        kv_l = ln @ Wkv
        k_l, v_l = (kv_l[..., :INNER], kv_l[..., INNER:])
        k_x = k_x.reshape(b, n, h, d)
        v_x = v_x.reshape(b, n, h, d)
        k_x = rope_rotate_k(k_x)
        q = jnp.transpose(q, (0, 2, 1, 3)) * scale
        k_x = jnp.transpose(k_x, (0, 2, 1, 3))
        v_x = jnp.transpose(v_x, (0, 2, 1, 3))
        k_l = jnp.transpose(k_l.reshape(b, m, h, d), (0, 2, 1, 3))
        v_l = jnp.transpose(v_l.reshape(b, m, h, d), (0, 2, 1, 3))
        k = jnp.concatenate([k_x, k_l], axis=2)
        v = jnp.concatenate([v_x, v_l], axis=2)
        sim = jnp.einsum('bhid,bhjd->bhij', q, k)
        attn = jax.nn.softmax(sim, axis=-1)
        out = jnp.einsum('bhij,bhjd->bhid', attn, v)
        out = jnp.transpose(out, (0, 2, 1, 3)).reshape(b, m, INNER)
        return out @ Wo

    def _L0_ffn_ref(x, W_r, W_k, W_v, mu_r, mu_k):
        import jax, jax.numpy as jnp
        import numpy as np
        DIM = 128

        def _reference_tuple_inner(x, W_r, W_k, W_v, mu_r, mu_k):
            B, T, C = x.shape
            x_prev = jnp.concatenate([jnp.zeros((B, 1, C), x.dtype), x[:, :-1, :]], axis=1)
            xr = mu_r * x + (1.0 - mu_r) * x_prev
            xk = mu_k * x + (1.0 - mu_k) * x_prev
            r = jax.nn.sigmoid(jnp.einsum('btc,dc->btd', xr, W_r))
            k = jnp.einsum('btc,dc->btd', xk, W_k)
            k_act = jnp.square(jax.nn.relu(k))
            out = r * jnp.einsum('btc,dc->btd', k_act, W_v)
            new_state = x[:, -1, :]
            return (out, new_state)
        return _reference_tuple_inner(x, W_r, W_k, W_v, mu_r, mu_k)[0]

    def _L1_xattn_ref(q, k, v, num_heads):
        import jax, jax.numpy as jnp
        import numpy as np
        ROPE_BASE = 10000.0

        def rotate_half(x):
            d = x.shape[-1] // 2
            return jnp.concatenate([-x[..., d:], x[..., :d]], axis=-1)

        def rope_cos_sin(seq_len, head_dim, dtype=jnp.float32):
            inv_freq = 1.0 / ROPE_BASE ** (jnp.arange(0, head_dim, 2, dtype=jnp.float32) / head_dim)
            t = jnp.arange(seq_len, dtype=jnp.float32)
            freqs = jnp.outer(t, inv_freq)
            emb = jnp.concatenate([freqs, freqs], axis=-1)
            return (jnp.cos(emb).astype(dtype), jnp.sin(emb).astype(dtype))

        def alibi_slopes(num_heads):
            return jnp.asarray([2.0 ** (-8.0 * i / num_heads) for i in range(1, num_heads + 1)], dtype=jnp.float32)
        B, T, H = q.shape
        nh = num_heads
        hd = H // nh
        q = q.reshape(B, T, nh, hd)
        k = k.reshape(B, T, nh, hd)
        v = v.reshape(B, T, nh, hd)
        cos, sin = rope_cos_sin(T, hd, q.dtype)
        cos = cos[None, :, None, :]
        sin = sin[None, :, None, :]
        q = q * cos + rotate_half(q) * sin
        k = k * cos + rotate_half(k) * sin
        rel = jnp.arange(T)[None, :] - jnp.arange(T)[:, None]
        bias = alibi_slopes(nh)[:, None, None] * rel.astype(q.dtype)
        scale = 1.0 / jnp.sqrt(jnp.asarray(hd, dtype=q.dtype))
        scores = jnp.einsum('bqhd,bkhd->bhqk', q, k) * scale + bias[None]
        attn = jax.nn.softmax(scores, axis=-1)
        out = jnp.einsum('bhqk,bkhd->bqhd', attn, v)
        return out.reshape(B, T, H)

    def _L1_ffn_ref(hidden_states, router_w, w1, b1, w2, b2):
        import jax, jax.numpy as jnp
        import numpy as np
        TOP_K = 2
        x = hidden_states
        router_logits = jnp.einsum('bth,eh->bte', x, router_w)
        topk_values, topk_indices = jax.lax.top_k(router_logits, TOP_K)
        topk_weights = jax.nn.softmax(topk_values.astype(jnp.float32), axis=-1).astype(x.dtype)
        h1 = jnp.einsum('bth,efh->btef', x, w1) + b1
        h1 = jax.nn.gelu(h1, approximate=False)
        expert_outputs = jnp.einsum('btef,ehf->bteh', h1, w2) + b2
        gather_idx = topk_indices[..., None]
        topk_expert_outputs = jnp.take_along_axis(expert_outputs, gather_idx, axis=2)
        mixed_output = jnp.sum(topk_expert_outputs * topk_weights[..., None], axis=2)
        return mixed_output
    x = x + jnp.tanh(g_xattn[0]) * _L0_xattn_ref(ctx_1024, _layernorm(x, axis=-1), L0_xattn_gamma_x, L0_xattn_beta_x, L0_xattn_gamma_l, L0_xattn_beta_l, L0_xattn_Wq, L0_xattn_Wkv, L0_xattn_Wo)
    x = x + jnp.tanh(g_ffn[0]) * _L0_ffn_ref(_layernorm(x, axis=-1), L0_ffn_W_r, L0_ffn_W_k, L0_ffn_W_v, L0_ffn_mu_r, L0_ffn_mu_k)
    x = x + jnp.tanh(g_xattn[1]) * _L1_xattn_ref(_layernorm(x, axis=-1), ctx_1024, ctx_1024, 16)
    x = x + jnp.tanh(g_ffn[1]) * _L1_ffn_ref(_layernorm(x, axis=-1), L1_ffn_router_w, L1_ffn_w1, L1_ffn_b1, L1_ffn_w2, L1_ffn_b2)
    return x

_drawn_inputs = setup_inputs


def setup_inputs(seed=0):
    import zlib

    import numpy as np

    out = dict(_drawn_inputs(seed))
    spreads = {'g_ffn': (-1.0, 0.6),
     'L0_xattn_gamma_x': (1.0, 0.2),
     'L0_xattn_beta_x': (0.0, 0.1),
     'L0_xattn_gamma_l': (1.0, 0.2),
     'L0_xattn_beta_l': (0.0, 0.1)}
    factors = {'L0_ffn_W_r': 4.626, 'L0_ffn_mu_r': 8.0, 'L1_ffn_b1': 8.0, 'L1_ffn_b2': 5.215}
    for name, (base, spread) in spreads.items():
        noise = np.random.default_rng([zlib.crc32(name.encode()), seed]).standard_normal(out[name].shape)
        drawn = base * np.exp(spread * noise) if base else spread * noise
        out[name] = jnp.asarray(drawn.astype(out[name].dtype))
    for name, factor in factors.items():
        out[name] = (out[name] * factor).astype(out[name].dtype)
    return out
```

```python
from contextlib import ExitStack

import numpy as np

import concourse.bass as bass
from concourse import mybir

FP32, FP16, BF16, I32 = mybir.dt.float32, mybir.dt.float16, mybir.dt.bfloat16, mybir.dt.int32
ALU, ACT, AXL = mybir.AluOpType, mybir.ActivationFunctionType, mybir.AxisListType

B, T, D = 32, 64, 128
TB = 2
NT = B // TB
EPS = 1e-5
H0, HD0 = 8, 64
NP = H0 // 2
INNER = H0 * HD0
H1, HD1 = 16, 8
E, F = 8, 512
FC = F // 128
GT = 4
NG = NT // GT
RSQRT_MAGIC = 0x5F3759DF


class Steps:

    def __init__(self, eng, sem):
        self.eng, self.sem, self.base, self.n = eng, sem, 0, 0

    def at(self, base):
        self.base, self.n = base, 0

    def done(self, instruction):
        self.n += 1
        return instruction.then_inc(self.sem, 1)

    def wait(self):
        self.eng.wait_ge(self.sem, self.base + self.n)


def steady(eng, body, last):
    body(0, 0)
    body(1, 1)
    with eng.Fori(1, last // 2) as i:
        body(2 * i, 0)
        body(2 * i + 1, 1)


def program(nc, a, out, phases=4):
    ctx = ExitStack()
    with ctx:
        def sb(name, shape, dt=FP32):
            return ctx.enter_context(nc.sbuf_tensor(name, shape, dt))

        def sem(name):
            return ctx.enter_context(nc.semaphore(name))

        joint = sb("joint", [128, B * D])
        x_res = sb("x_res", [128, NT * D])
        gates = sb("gates", [128, 4])
        tanh_g = sb("tanh_g", [128, 4])
        gamma_j = sb("gamma_j", [128, D])
        beta_j = sb("beta_j", [128, D])
        wq_raw = sb("wq_raw", [128, INNER])
        wkv_raw = sb("wkv_raw", [128, 2 * INNER])
        wo_sb = sb("wo_sb", [128, NP, D])
        ident = sb("ident", [128, 128])
        ident_h = sb("ident_h", [128, 128], FP16)
        ident_b = sb("ident_b", [128, 128], BF16)
        ones_f = sb("ones_f", [128, 1])
        ones_h = sb("ones_h", [128, 1], FP16)
        select = sb("select", [8, 8, 128], BF16)
        cos0 = sb("cos0", [128, T])
        sin0 = sb("sin0", [128, T])
        wq_s = sb("wq_s", [128, 2, INNER], FP16)
        wk_s = sb("wk_s", [128, 2, INNER], FP16)
        wkr_s = sb("wkr_s", [128, 2, INNER], FP16)
        wvT = sb("wvT", [128, NP, D])
        wvo = sb("wvo", [128, H0, D])
        stat = sb("stat", [128, B, 6])
        mv = sb("mv", [128, B, 2])
        nwt = sb("nwt", [128, 6, B])
        scale_j = sb("scale_j", [128, B])
        bias_j = sb("bias_j", [128, B])
        xn = sb("xn", [128, 2, TB, D])
        x_s = sb("x_s", [128, 2, 2, TB, D], FP16)
        xT = sb("xT", [128, 2, 2, TB, 128], FP16)
        stat4 = sb("stat4", [128, 2, NT, 6])
        mv4 = sb("mv4", [128, 2, NT, 2])
        nwt4 = sb("nwt4", [128, 2, 5, NT])
        mix_w = sb("mix_w", [128, 4])
        ffn_raw = sb("ffn_raw", [128, 3, D])
        ffn_wT = sb("ffn_wT", [128, 3, D])
        half_g = sb("half_g", [128, 1])
        z = sb("z", [128, 2, GT * D])
        zT = sb("zT", [128, 2, GT * TB, T + 1])
        mixed = sb("mixed", [128, 2, 2, GT * TB, T])
        act_k = sb("act_k", [128, 2, GT * D])
        recept = sb("recept", [128, 2, GT * D])
        own_row = sb("own_row", [128, TB], FP16)
        cos1 = sb("cos1", [128, 8])
        sin1 = sb("sin1", [128, 8])
        q_ext = sb("q_ext", [128, H1, 8], FP16)
        k_ext = sb("k_ext", [128, H1, 8], FP16)
        ctx_tok = sb("ctx_tok", [128, NT * D])
        k1_s = sb("k1_s", [128, 2, NT * D], FP16)
        v1_s = sb("v1_s", [128, 2, NT * D], FP16)
        z1 = joint[:, 0:NT * D]
        kv_tmp = joint[:, NT * D:2 * NT * D]
        w1_raw = sb("w1_raw", [128, E * FC, D])
        w2_raw = sb("w2_raw", [128, E, F])
        b1_raw = sb("b1_raw", [E * FC, 128])
        b1T = sb("b1T", [128, E * FC])
        b2_sb = sb("b2_sb", [E, D])
        rw_raw = sb("rw_raw", [E, D])
        rwT = sb("rwT", [128, E])
        logit = sb("logit", [128, 2, GT, E])
        top = sb("top", [128, 2, GT, 8])
        gt_ = sb("gt_", [128, 8, GT, E])
        gate = sb("gate", [128, 2, GT, E])
        gateT = sb("gateT", [E, 2, GT * 128])

        early = ExitStack()

        def sb0(name, shape, dt=FP32):
            return early.enter_context(nc.sbuf_tensor(name, shape, dt))

        kT = sb0("kT", [128, 2, NP, TB, 128])
        kT_b = sb0("kT_b", [128, 2, NP, TB, 128], BF16)
        qT = sb0("qT", [128, 2, NP, TB, 2, T])
        qT_b = sb0("qT_b", [128, 2, NP, TB, 2, T], BF16)
        kcos = sb0("kcos", [128, 2, NP, TB, T])
        ksin = sb0("ksin", [128, 2, NP, TB, T])
        nmax = sb0("nmax", [128, 2, TB, NP], BF16)
        nmaxT = sb0("nmaxT", [8, 2, 128], BF16)
        prob = sb0("prob", [128, 2, H0, TB, T])
        prob_s = sb0("prob_s", [128, 2, 2, H0, TB, T], FP16)
        rden = sb0("rden", [128, 2, H0])
        ax = sb0("ax", [128, 2, H0, TB, T])

        early.close()
        early = ExitStack()
        qr = sb0("qr", [128, 2, 2, D])
        q_st = sb0("q_st", [128, 2, H1, 4, 8], FP16)
        k_st = sb0("k_st", [128, 2, H1, 4, 8], FP16)
        v_bd = sb0("v_bd", [128, 2, 2, H1 // 2, TB, 17], FP16)
        qT1 = sb0("qT1", [128, 2, 4, 128], FP16)
        qT2 = sb0("qT2", [128, 2, 4, 128], FP16)
        kT1 = sb0("kT1", [128, 2, 4, 128], FP16)
        q_bd = sb0("q_bd", [128, 2, 4, TB, 4, T], FP16)
        k_bd = sb0("k_bd", [128, 2, 4, TB, 4, T], FP16)
        p1 = sb0("p1", [128, 2, H1 * T])
        p1_s = sb0("p1_s", [128, 2, 2, H1 * T], FP16)
        rden1 = sb0("rden1", [128, 2, H1 // 2, TB])
        o1 = sb0("o1", [128, 2, D])
        early.close()
        w1_s = sb("w1_s", [128, 2, E * FC, 128], FP16)
        w2T = sb("w2T", [128, E * FC, D])
        zTd = sb("zTd", [128, 2, GT * D])
        zTd_s = sb("zTd_s", [128, 2, 2, GT * D], FP16)
        hid = sb("hid", [128, 2, FC, GT * 128])

        bank = [ctx.enter_context(nc.psum_tensor(f"bank{i}", [128, 512], FP32)) for i in range(8)]

        s = {}
        for name in (
            "consts_in weights_in x_in0 x_in1 x_in2 x_in3 x_res_in out_done ident_up select_up vec_step pool_step q_zero tanh_ready "
            "w_split wv_turned wv_copied wvo_mm wvo_up stats_up "
            "a_norm a_split a_turn a_xT a_proj a_projq a_q a_qk a_rope a_k a_kb a_qb a_s a_nmax a_nturn a_nmaxT "
            "a_sT a_exp a_ph a_pl a_den a_rden a_ax a_axs a_y a_x1 "
            "ffn_in ffn_turned ffn_wT_up zT_zero half_up b_z b_zT b_zTs b_mix b_k b_r b_tanh b_relu b_sq b_v b_x2 "
            "c_consts kv_in c_kv c_ext c_zero c_z c_q c_st c_turn c_k_out c_q1_out c_kbd c_s c_max c_turn2 c_q2_out c_qbd c_sT "
            "c_exp c_ph c_pl c_pv c_o c_x3 "
            "moe_in moe_in2 d_w d_wl d_ws d_small d_smalls d_z d_zT d_zTs d_zTl d_log d_ex d_pick d_gate d_gT d_gTs d_b2 d_b2s d_h d_hid d_y d_acc"
        ).split():
            s[name] = sem(name)

        block = ctx.enter_context(nc.Block())

        @block.sync
        def _(sp):
            ctx_rows = a["ctx_1024"].rearrange("b t d -> t b d")
            x_rows = a["x"].rearrange("b t d -> t b d")
            jt = joint[:, :].rearrange("p (b d) -> p b d", d=D)
            for c in range(4):
                bs = slice(c * 8, c * 8 + 8)
                sp.dma_start(jt[0:64, bs, :], ctx_rows[:, bs, :]).then_inc(s[f"x_in{c}"], 16)
                sp.dma_start(jt[64:128, bs, :], x_rows[:, bs, :]).then_inc(s[f"x_in{c}"], 16)
            for t, dst in ((a["L0_xattn_gamma_x"], gamma_j[0:64, :]), (a["L0_xattn_gamma_l"], gamma_j[64:128, :]),
                           (a["L0_xattn_beta_x"], beta_j[0:64, :]), (a["L0_xattn_beta_l"], beta_j[64:128, :])):
                sp.dma_start(dst, t.partition_broadcast(64)).then_inc(s["consts_in"], 16)
            sp.dma_start(cos0[:, :], a["cos0"]).then_inc(s["consts_in"], 16)
            sp.dma_start(sin0[:, :], a["sin0"]).then_inc(s["consts_in"], 16)
            sp.dma_start(gates[:, 0:2], a["g_xattn"].partition_broadcast(128)).then_inc(s["consts_in"], 16)
            sp.dma_start(gates[:, 2:4], a["g_ffn"].partition_broadcast(128)).then_inc(s["consts_in"], 16)
            tok = a["x"].rearrange("(n b) t d -> (b t) n d", b=TB)
            sp.dma_start(x_res[:, :].rearrange("p (n d) -> p n d", d=D), tok).then_inc(s["x_res_in"], 16)
            for n, name in enumerate(("L0_ffn_W_r", "L0_ffn_W_k", "L0_ffn_W_v")):
                sp.dma_start(ffn_raw[:, n, :], a[name]).then_inc(s["ffn_in"], 16)
            for n, name in enumerate(("L0_ffn_mu_r", "L0_ffn_mu_k")):
                sp.dma_start(mix_w[:, n:n + 1], a[name].rearrange("(d a) -> d a", a=1)).then_inc(s["ffn_in"], 16)
            for t, dst in (("cos1", cos1[:, :]), ("sin1", sin1[:, :]), ("q_ext", q_ext[:, :, :]), ("k_ext", k_ext[:, :, :])):
                sp.dma_start(dst, a[t]).then_inc(s["c_consts"], 16)
            sp.dma_start(ctx_tok[:, :].rearrange("p (n d) -> p n d", d=D),
                         a["ctx_1024"].rearrange("(n b) t d -> (b t) n d", b=TB)).then_inc(s["kv_in"], 16)
            sp.dma_start(b1_raw[:, :], a["L1_ffn_b1"].rearrange("e (c f) -> (e c) f", f=128)).then_inc(s["moe_in"], 16)
            sp.dma_start(b2_sb[:, :], a["L1_ffn_b2"]).then_inc(s["moe_in"], 16)
            sp.dma_start(rw_raw[:, :], a["L1_ffn_router_w"]).then_inc(s["moe_in"], 16)
            sp.dma_start(w1_raw[:, :, :], a["L1_ffn_w1"].rearrange("e (c f) h -> f (e c) h", f=128)).then_inc(s["moe_in2"], 16)
            sp.dma_start(w2_raw[:, :, :], a["L1_ffn_w2"].rearrange("e h f -> h e f")).then_inc(s["moe_in2"], 16)
            if phases == 1:
                sp.wait_ge(s["a_x1"], NT)
            elif phases == 2:
                sp.wait_ge(s["b_x2"], NG)
            elif phases == 3:
                sp.wait_ge(s["c_x3"], NT)
            else:
                sp.wait_ge(s["d_acc"], NG * E * GT)
            sp.dma_start(out.rearrange("(n b) t d -> (b t) n d", b=TB),
                         x_res[:, :].rearrange("p (n d) -> p n d", d=D)).then_inc(s["out_done"], 16)
            sp.wait_ge(s["out_done"], 16)
            if phases < 4:
                for nm, v in (("moe_in", 48), ("moe_in2", 32), ("c_consts", 64), ("kv_in", 16), ("ffn_in", 80)):
                    sp.wait_ge(s[nm], v)

        @block.gpsimd
        def _(pool):
            g = nc.gpsimd
            st = Steps(pool, s["pool_step"])
            st.done(g.memset(ident[:, :], 0.0))
            st.done(g.memset(qT[:, :, :, :, :, :], 0.0))
            st.done(g.memset(ones_f[:, :], 1.0))
            g.memset(ones_h[:, :], 1.0).then_inc(s["q_zero"], 1)
            st.wait()
            g.affine_select(out=ident[:, :], in_=ident[:, :], compare_op=ALU.not_equal, fill=1.0,
                            base=0, pattern=[[-1, 128]], channel_multiplier=1).then_inc(s["ident_up"], 1)
            pool.wait_ge(s["ident_up"], 1)
            g.tensor_copy(ident_h[:, :], ident[:, :]).then_inc(s["ident_up"], 1)
            g.tensor_copy(ident_b[:, :], ident[:, :]).then_inc(s["ident_up"], 1)
            for r in range(8):
                i = g.tensor_copy(select[:, r, :], ident[0:8, r:r + 1].to_broadcast([8, 128]))
            i.then_inc(s["select_up"], 1)
            pool.wait_ge(s["consts_in"], 8 * 16)

            def cast(dst, src, shape):
                one = ones_f[:, :]
                for _ in range(len(shape) - 2):
                    one = one.unsqueeze(1)
                return g.tensor_tensor(out=dst, in0=src, in1=one.to_broadcast(shape), op=ALU.mult)

            def split(t, u):
                pool.wait_ge(s["a_norm"], t + 1)
                x = xn[:, u, :, :]
                st.done(g.tensor_tensor(out=x, in0=x, in1=gamma_j[:, :].unsqueeze(1).to_broadcast([128, TB, D]), op=ALU.mult))
                st.wait()
                st.done(g.tensor_tensor(out=x, in0=x, in1=beta_j[:, :].unsqueeze(1).to_broadcast([128, TB, D]), op=ALU.add))
                st.wait()
                st.done(cast(x_s[:, u, 0], x, [128, TB, D]))
                st.wait()
                g.tensor_tensor(out=x_s[:, u, 1], in0=x, in1=x_s[:, u, 0], op=ALU.subtract).then_inc(s["a_split"], 1)

            def prob_high(t, u):
                for b in range(TB):
                    pool.wait_ge(s["a_exp"], TB * t + b + 1)
                    cast(prob_s[:, u, 0, :, b, :], prob[:, u, :, b, :], [128, H0, T]).then_inc(s["a_ph"], 1)

            def k_low(t, u):
                pool.wait_ge(s["a_k"], t + 1)
                pool.wait_ge(s["a_qk"], NP * (t + 1))
                cast(kT_b[:, u].rearrange("p a b k -> p (a b k)"), kT[:, u].rearrange("p a b k -> p (a b k)"), [128, NP * TB * 128]).then_inc(s["a_kb"], 1)

            n0 = st.n
            split(0, 0)
            split(1, 1)
            k_low(0, 0)
            per = 3

            def turn(t, u, more=True):
                st.at(n0 + 2 * per + per * t)
                if not (isinstance(t, int) and t < 2):
                    pool.wait_ge(s["a_ax"], TB * (t - 1))
                prob_high(t, u)
                if more is not None:
                    k_low(t + 1, 1 - u)
                if more:
                    pool.wait_ge(s["a_ax"], TB * (t + 1))
                    split(t + 2, u)

            turn(0, 0)
            turn(1, 1)
            with pool.Fori(1, NT // 2 - 1) as i:
                turn(2 * i, 0)
                turn(2 * i + 1, 1)
            turn(NT - 2, 0, False)
            turn(NT - 1, 1, None)
            if phases < 2:
                return
            for gi in range(NG):
                u = gi % 2
                pool.wait_ge(s["b_relu"], gi + 1)
                g.tensor_tensor(out=act_k[:, u], in0=act_k[:, u], in1=act_k[:, u], op=ALU.mult).then_inc(s["b_sq"], 1)
            if phases < 3:
                return
            st.at(0)
            pool.wait_ge(s["c_consts"], 64)
            for u in range(2):
                g.tensor_copy(q_st[:, u, :, 3, :], q_ext[:, :, :])
                i = g.tensor_copy(k_st[:, u, :, 3, :], k_ext[:, :, :])
            i.then_inc(s["c_ext"], 1)
            g.memset(q_bd[:, :, :, :, :, :], 0.0)
            g.memset(k_bd[:, :, :, :, :, :], 0.0)
            g.memset(v_bd[:, :, :, :, :, :], 0.0).then_inc(s["c_zero"], 1)
            pool.wait_ge(s["c_zero"], 1)
            pool.wait_ge(s["c_kv"], 1)

            def stack(t, u):
                if not (isinstance(t, int) and t < 2):
                    pool.wait_ge(s["c_pv"], t - 1)
                kh, kl = (k1_s[:, j, bass.ds(t * D, D)].rearrange("p (h e) -> p h e", e=8) for j in range(2))
                g.tensor_copy(k_st[:, u, :, 0, :], kh)
                g.tensor_copy(k_st[:, u, :, 1, :], kh)
                g.tensor_copy(k_st[:, u, :, 2, :], kl)
                for b in range(TB):
                    own = own_row[:, b:b + 1].unsqueeze(1).to_broadcast([128, H1 // 2, 16])
                    for j in range(2):
                        i = g.tensor_tensor(out=v_bd[:, u, j, :, b, 0:16], in0=v1_s[:, j, bass.ds(t * D, D)].rearrange("p (h e) -> p h e", e=16),
                                            in1=own, op=ALU.mult)
                i.then_inc(s["c_st"], 1)

            steady(pool, stack, NT)

        @block.scalar
        def _(act):
            g = nc.scalar
            act.dma_start(wq_raw[:, :], a["L0_xattn_Wq"]).then_inc(s["weights_in"], 16)
            act.dma_start(wkv_raw[:, :], a["L0_xattn_Wkv"]).then_inc(s["weights_in"], 16)
            act.dma_start(wo_sb[:, :, :], a["L0_xattn_Wo"].rearrange("(p r) n -> r p n", r=128)).then_inc(s["weights_in"], 16)
            act.wait_ge(s["consts_in"], 8 * 16)
            g.activation(tanh_g[:, :], gates[:, :], ACT.Tanh).then_inc(s["tanh_ready"], 1)
            act.wait_ge(s["wv_turned"], 1)
            g.activation(wvT[:, :, :], bank[6][:, :].rearrange("p (a d) -> p a d", d=D), ACT.Copy).then_inc(s["wv_copied"], 1)
            for half in range(2):
                act.wait_ge(s["wvo_mm"], half + 1)
                g.activation(wvo[:, half:H0:2, :], bank[4 + half][:, :].rearrange("p (a d) -> p a d", d=D),
                             ACT.Copy).then_inc(s["wvo_up"], 1)
            act.wait_ge(s["q_zero"], 1)

            def x_turned(t, u):
                act.wait_ge(s["a_turn"], t + 1)
                g.activation(xT[:, u], bank[2][:, 0:256].bitcast(FP16).rearrange("p (h b k) -> p h b k", h=2, b=TB),
                             ACT.Copy).then_inc(s["a_xT"], 1)

            def qk(t, u):
                act.wait_ge(s["a_projq"], t + 1)
                qq = bank[2][:, :].rearrange("p (a b q) -> p a b q", a=NP, b=TB)
                for h in range(2):
                    r = slice(64 * h, 64 * h + 64)
                    i = g.activation(qT[r, u, :, :, h, :], qq[r], ACT.Copy)
                i.then_inc(s["a_q"], 1)
                for p in range(NP):
                    act.wait_ge(s["a_rope"], NP * t + p + 1)
                    kk = bank[p % 2][:, 0:256].rearrange("p (b k) -> p b k", b=TB)
                    g.activation(kT[:, u, p, :, 64:128], kk[:, :, 64:128], ACT.Copy).then_inc(s["a_qk"], 1)

            def exps(t, u):
                for b in range(TB):
                    act.wait_ge(s["a_sT"], TB * t + b + 1)
                    g.activation(prob[:, u, :, b, :], bank[6 + b][:, :].rearrange("p (h q) -> p h q", h=H0), ACT.Exp,
                                 scale=HD0 ** -0.5).then_inc(s["a_exp"], 1)

            def ax_out(t, u):
                for b in range(TB):
                    act.wait_ge(s["a_ax"], TB * t + b + 1)
                    g.activation(ax[:, u, :, b, :], bank[6 + b][:, :].rearrange("p (h q) -> p h q", h=H0), ACT.Copy).then_inc(s["a_axs"], 1)

            def nmax_out(t, u):
                act.wait_ge(s["a_nturn"], t + 1)
                g.activation(nmaxT[:, u, :], bank[3][0:8, 64:128].bitcast(BF16), ACT.Copy).then_inc(s["a_nmaxT"], 1)

            x_turned(0, 0)
            qk(0, 0)
            nmax_out(0, 0)

            def turn(t, u, more=True):
                if more:
                    x_turned(t + 1, 1 - u)
                if not (isinstance(t, int) and t < 2):
                    act.wait_ge(s["a_ph"], TB * (t - 1))
                    act.wait_ge(s["a_pl"], TB * (t - 1))
                exps(t, u)
                if more:
                    if not (isinstance(t, int) and t < 1):
                        act.wait_ge(s["a_sT"], TB * t)
                        act.wait_ge(s["a_kb"], t)
                        act.wait_ge(s["a_qb"], t)
                    qk(t + 1, 1 - u)
                if not (isinstance(t, int) and t < 2):
                    act.wait_ge(s["a_y"], t - 1)
                ax_out(t, u)
                if more:
                    nmax_out(t + 1, 1 - u)

            turn(0, 0)
            turn(1, 1)
            with act.Fori(1, NT // 2 - 1) as i:
                turn(2 * i, 0)
                turn(2 * i + 1, 1)
            turn(NT - 2, 0)
            turn(NT - 1, 1, False)
            if phases < 2:
                return
            act.wait_ge(s["ffn_turned"], 1)
            g.activation(ffn_wT[:, :, :], bank[3][:, 0:384].rearrange("p (a d) -> p a d", d=D), ACT.Copy).then_inc(s["ffn_wT_up"], 1)
            for gi in range(NG):
                u = gi % 2
                act.wait_ge(s["b_zT"], gi + 1)
                if gi >= 2:
                    act.wait_ge(s["b_mix"], gi - 1)
                g.activation(zT[:, u, :, 1:T + 1], bank[2][:, :].rearrange("p (b q) -> p b q", q=T), ACT.Copy).then_inc(s["b_zTs"], 1)
                act.wait_ge(s["b_k"], gi + 1)
                if gi >= 2:
                    act.wait_ge(s["b_v"], gi - 1)
                g.activation(act_k[:, u], bank[4][:, :], ACT.Relu).then_inc(s["b_relu"], 1)
                act.wait_ge(s["b_r"], gi + 1)
                if gi >= 2:
                    act.wait_ge(s["b_x2"], gi - 1)
                g.activation(recept[:, u], bank[5][:, :], ACT.Tanh, scale=0.5).then_inc(s["b_tanh"], 1)
            if phases < 3:
                return

            def half_banks(t, u, ks):
                pass

            def k_q1_out(t, u):
                act.wait_ge(s["c_turn"], t + 1)
                pt = bank[0][:, :].bitcast(FP16).rearrange("p (a g k) -> p a g k", a=2, g=4)
                if not (isinstance(t, int) and t < 2):
                    act.wait_ge(s["c_sT"], t - 1)
                    act.wait_ge(s["c_kbd"], t - 1)
                g.activation(kT1[:, u], pt[:, 0], ACT.Copy).then_inc(s["c_k_out"], 1)
                g.activation(qT1[:, u], pt[:, 1], ACT.Copy).then_inc(s["c_q1_out"], 1)

            def q2_out(t, u):
                act.wait_ge(s["c_turn2"], t + 1)
                if not (isinstance(t, int) and t < 2):
                    act.wait_ge(s["c_qbd"], t - 1)
                g.activation(qT2[:, u], bank[1][:, 0:256].bitcast(FP16).rearrange("p (g k) -> p g k", g=4), ACT.Copy).then_inc(s["c_q2_out"], 1)

            def exp1(t, u):
                act.wait_ge(s["c_sT"], t + 1)
                if not (isinstance(t, int) and t < 2):
                    act.wait_ge(s["c_pl"], t - 1)
                    act.wait_ge(s["c_pv"], t - 1)
                for half in range(2):
                    c = slice(512 * half, 512 * half + 512)
                    i = g.activation(p1[:, u, c], bank[4 + half][:, :], ACT.Exp, scale=HD1 ** -0.5)
                i.then_inc(s["c_exp"], 1)
                act.wait_ge(s["c_exp"], t + 1)
                g.activation(p1_s[:, u, 0], p1[:, u], ACT.Copy).then_inc(s["c_ph"], 1)

            k_q1_out(0, 0)
            q2_out(0, 0)

            def turn1(t, u, more=True):
                if more:
                    k_q1_out(t + 1, 1 - u)
                exp1(t, u)
                if more:
                    q2_out(t + 1, 1 - u)

            turn1(0, 0)
            turn1(1, 1)
            with act.Fori(1, NT // 2 - 1) as i:
                turn1(2 * i, 0)
                turn1(2 * i + 1, 1)
            turn1(NT - 2, 0)
            turn1(NT - 1, 1, False)
            if phases < 4:
                return
            for k in range(2 * E):
                act.wait_ge(s["d_w"], k + 1)
                src = bank[k % 2][:, :].rearrange("p (c f) -> p c f", f=128)
                if k < E:
                    g.activation(w1_s[:, 0, FC * k:FC * k + FC, :], src, ACT.Copy).then_inc(s["d_ws"], 1)
                else:
                    g.activation(w2T[:, FC * (k - E):FC * (k - E) + FC, :], src, ACT.Copy).then_inc(s["d_ws"], 1)
            act.wait_ge(s["d_small"], 1)
            g.activation(b1T[:, :], bank[2][:, 0:E * FC], ACT.Copy)
            g.activation(rwT[:, :], bank[2][:, 32:32 + E], ACT.Copy).then_inc(s["d_smalls"], 1)

            act.wait_ge(s["d_smalls"], 1)

            def moe_in(gi, u):
                act.wait_ge(s["d_zT"], gi + 1)
                g.activation(zTd[:, u], bank[2][:, :], ACT.Copy)
                g.activation(zTd_s[:, u, 0], bank[2][:, :], ACT.Copy).then_inc(s["d_zTs"], 1)
                act.wait_ge(s["d_pick"], gi + 1)
                g.activation(gt_[:, 5], gt_[:, 5], ACT.Exp).then_inc(s["d_ex"], 1)
                act.wait_ge(s["d_gT"], gi + 1)
                g.activation(gateT[:, u, :], bank[3][0:E, :], ACT.Copy).then_inc(s["d_gTs"], 1)

            def gelus(gi, u):
                n = E * gi
                for e in range(E):
                    if not (isinstance(gi, int) and gi == 0 and e < 2):
                        act.wait_ge(s["d_y"], GT * (n + e - 1))
                    for c in range(FC):
                        act.wait_ge(s["d_h"], FC * (n + e) + c + 1)
                        g.activation(hid[:, e % 2, c], bank[4 + c % 2][:, :], ACT.Gelu,
                                     bias=b1T[:, e * FC + c:e * FC + c + 1]).then_inc(s["d_hid"], 1)

            def moe(gi, u):
                moe_in(gi, u)
                gelus(gi, u)

            for gi in range(NG):
                moe(gi, gi % 2)

        @block.vector
        def _(vec):
            g = nc.vector
            st = Steps(vec, s["vec_step"])

            def rsqrt(y, v, tmp, out_sem=None):
                half, sq, bits = tmp
                st.wait()
                st.done(g.tensor_scalar(out=half, in0=v, scalar1=-0.5, scalar2=None, op0=ALU.mult))
                st.done(g.tensor_scalar(out=bits.bitcast(I32), in0=v.bitcast(I32), scalar1=1, scalar2=None, op0=ALU.logical_shift_right))
                st.wait()
                st.done(g.tensor_scalar(out=y.bitcast(I32), in0=bits.bitcast(I32), scalar1=-1.0, scalar2=float(RSQRT_MAGIC),
                                        op0=ALU.mult, op1=ALU.add))
                for k in range(3):
                    st.wait()
                    st.done(g.tensor_tensor(out=sq, in0=y, in1=y, op=ALU.mult))
                    st.wait()
                    st.done(g.tensor_tensor(out=sq, in0=sq, in1=half, op=ALU.mult))
                    st.wait()
                    st.done(g.scalar_tensor_tensor(out=y, in0=sq, scalar=1.5, in1=y, op0=ALU.add, op1=ALU.mult))

            for c in range(4):
                vec.wait_ge(s[f"x_in{c}"], 32)
                for b in range(8 * c, 8 * c + 8):
                    st.done(g.bn_stats(stat[:, b, :], joint[:, b * D:(b + 1) * D]))
            st.wait()
            for b in range(B):
                st.done(g.bn_aggr(mv[:, b, :], stat[:, b, :]))
            st.wait()
            var, y, h, sq, bits, w = (nwt[:, i, :] for i in range(6))
            st.done(g.tensor_scalar(out=var, in0=mv[:, :, 1], scalar1=EPS, scalar2=None, op0=ALU.add))
            rsqrt(y, var, (h, sq, bits))
            st.wait()
            st.done(g.tensor_copy(scale_j[:, :], y))
            hi = slice(64, 128)
            st.wait()
            st.done(g.tensor_tensor(out=w[hi], in0=y[hi], in1=y[hi], op=ALU.mult))
            st.wait()
            st.done(g.tensor_tensor(out=w[hi], in0=w[hi], in1=mv[hi, :, 1], op=ALU.mult))
            st.wait()
            st.done(g.tensor_scalar(out=w[hi], in0=w[hi], scalar1=EPS, scalar2=None, op0=ALU.add))
            rsqrt(y[hi], w[hi], (h[hi], sq[hi], bits[hi]))
            st.wait()
            st.done(g.tensor_tensor(out=scale_j[hi, :], in0=scale_j[hi, :], in1=y[hi], op=ALU.mult))
            st.wait()
            st.done(g.scalar_tensor_tensor(out=bias_j[:, :], in0=mv[:, :, 0], scalar=-1.0, in1=scale_j[:, :],
                                           op0=ALU.mult, op1=ALU.mult))
            st.wait()

            def norm(t, u):
                for b in range(TB):
                    i = g.tensor_scalar(out=xn[:, u, b, :], in0=joint[:, bass.ds((TB * t + b) * D, D)],
                                        scalar1=scale_j[:, bass.ds(TB * t + b, 1)], scalar2=bias_j[:, bass.ds(TB * t + b, 1)],
                                        op0=ALU.mult, op1=ALU.add)
                i.then_inc(s["a_norm"], 1)

            norm(0, 0)
            norm(1, 1)
            vec.wait_ge(s["weights_in"], 48)
            wk_raw = wkv_raw[:, 0:INNER]
            for raw, split in ((wq_raw[:, :], wq_s), (wk_raw, wk_s)):
                st.done(g.tensor_copy(split[:, 0, :], raw))
                st.wait()
                st.done(g.tensor_tensor(out=split[:, 1, :], in0=raw, in1=split[:, 0, :], op=ALU.subtract))
            st.wait()
            for hl in range(2):
                src = wk_s[:, hl, :].rearrange("p (h a d) -> p h a d", a=2, d=HD0 // 2)
                dst = wkr_s[:, hl, :].rearrange("p (h a d) -> p h a d", a=2, d=HD0 // 2)
                for half in range(2):
                    i = g.tensor_copy(dst[:, :, half, :], src[:, :, 1 - half, :])
            i.then_inc(s["w_split"], 1)
            vec.wait_ge(s["consts_in"], 8 * 16)
            vec.wait_ge(s["x_res_in"], 16)
            vec.wait_ge(s["tanh_ready"], 1)

            def rope(t, u, p):
                vec.wait_ge(s["a_proj"], NP * t + p + 1)
                kk = bank[p % 2][:, 0:256].rearrange("p (b k) -> p b k", b=TB)[:, :, 0:64]
                kr = bank[p % 2][:, 256:384].rearrange("p (b k) -> p b k", b=TB)
                g.tensor_tensor(out=kcos[:, u, p], in0=kk, in1=cos0[:, :].unsqueeze(1).to_broadcast([128, TB, T]), op=ALU.mult)
                g.tensor_tensor(out=ksin[:, u, p], in0=kr, in1=sin0[:, :].unsqueeze(1).to_broadcast([128, TB, T]), op=ALU.mult).then_inc(s["a_rope"], 1)

            def rope_sum(t, u):
                vec.wait_ge(s["a_rope"], NP * (t + 1))
                g.tensor_tensor(out=kT[:, u, :, :, 0:64].rearrange("p a b k -> p (a b) k"), in0=kcos[:, u].rearrange("p a b k -> p (a b) k"),
                                in1=ksin[:, u].rearrange("p a b k -> p (a b) k"), op=ALU.add).then_inc(s["a_k"], 1)
                vec.wait_ge(s["a_q"], t + 1)
                g.tensor_copy(qT_b[:, u].rearrange("p a b h q -> p (a b h q)"),
                              qT[:, u].rearrange("p a b h q -> p (a b h q)")).then_inc(s["a_qb"], 1)

            def prob_low(t, u, b):
                vec.wait_ge(s["a_ph"], TB * t + b + 1)
                g.tensor_tensor(out=prob_s[:, u, 1, :, b, :], in0=prob[:, u, :, b, :], in1=prob_s[:, u, 0, :, b, :],
                                op=ALU.subtract).then_inc(s["a_pl"], 1)

            def maxima(t, u):
                for b in range(TB):
                    vec.wait_ge(s["a_s"], TB * t + b + 1)
                    g.tensor_reduce(out=nmax[:, u, b, :], in_=bank[4 + b][:, :].rearrange("p (a k) -> p a k", a=NP), axis=AXL.X,
                                    op=ALU.max, negate=True).then_inc(s["a_nmax"], 1)

            def denominators(t, u):
                vec.wait_ge(s["a_den"], t + 1)
                st.done(g.reciprocal(rden[:, u, :], bank[3][:, 0:H0]))
                st.wait()
                g.tensor_scalar(out=rden[:, u, :], in0=rden[:, u, :], scalar1=tanh_g[:, 0:1], scalar2=None, op0=ALU.mult).then_inc(s["a_rden"], 1)

            def residual(t, u):
                vec.wait_ge(s["a_y"], t + 1)
                vec.wait_ge(s["a_rden"], t + 1)
                xr = x_res[:, bass.ds(t * D, D)]
                for h in range(H0):
                    if h:
                        st.wait()
                    i = g.scalar_tensor_tensor(out=xr, in0=bank[h // 4][:, (h % 4) * D:(h % 4 + 1) * D], scalar=rden[:, u, h:h + 1],
                                               in1=xr, op0=ALU.mult, op1=ALU.add)
                    if h < H0 - 1:
                        st.done(i)
                    else:
                        i.then_inc(s["a_x1"], 1)

            n0 = st.n
            for p in range(NP):
                rope(0, 0, p)
            rope_sum(0, 0)
            maxima(0, 0)
            per = H0

            def turn(t, u, more=2):
                st.at(n0 + per * t)
                if more == 2:
                    vec.wait_ge(s["a_split"], t + 1)
                    norm(t + 2, u)
                v = 1 - u
                if more and not (isinstance(t, int) and t < 1):
                    vec.wait_ge(s["a_sT"], TB * t)
                    vec.wait_ge(s["a_kb"], t)
                for p in range(NP):
                    if more:
                        rope(t + 1, v, p)
                    if p % 2 == 1:
                        prob_low(t, u, p // 2)
                if more:
                    rope_sum(t + 1, v)
                denominators(t, u)
                if more:
                    if not (isinstance(t, int) and t < 1):
                        vec.wait_ge(s["a_nturn"], t)
                    maxima(t + 1, v)
                residual(t, u)

            turn(0, 0)
            turn(1, 1)
            with vec.Fori(1, NT // 2 - 1) as i:
                turn(2 * i, 0)
                turn(2 * i + 1, 1)
            turn(NT - 2, 0, 1)
            turn(NT - 1, 1, 0)
            if phases < 2:
                return
            st.at(n0 + per * NT)

            def layer_norm(first, count, dst, u, ready):
                st.wait()
                for j in range(count):
                    st.done(g.bn_stats(stat4[:, u, j, :], x_res[:, bass.ds((first + j) * D, D)]))
                st.wait()
                for j in range(count):
                    st.done(g.bn_aggr(mv4[:, u, j, :], stat4[:, u, j, :]))
                st.wait()
                var, y, h, sq, bits = (nwt4[:, u, k, 0:count] for k in range(5))
                st.done(g.tensor_scalar(out=var, in0=mv4[:, u, 0:count, 1], scalar1=EPS, scalar2=None, op0=ALU.add))
                rsqrt(y, var, (h, sq, bits))
                st.wait()
                for j in range(count):
                    i = g.tensor_scalar(out=dst[:, j * D:(j + 1) * D], in0=x_res[:, bass.ds((first + j) * D, D)],
                                        scalar1=mv4[:, u, j, 0:1], scalar2=y[:, j:j + 1], op0=ALU.subtract, op1=ALU.mult)
                i.then_inc(ready, 1)

            vec.wait_ge(s["ffn_in"], 80)
            st.done(g.tensor_scalar(out=mix_w[:, 2:4], in0=mix_w[:, 0:2], scalar1=-1.0, scalar2=1.0, op0=ALU.mult, op1=ALU.add))
            st.done(g.tensor_scalar(out=half_g[:, :], in0=tanh_g[:, 2:3], scalar1=0.5, scalar2=None, op0=ALU.mult))
            st.done(g.memset(zT[:, :, :, 0:1], 0.0))
            vec.wait_ge(s["a_x1"], NT)

            def ffn_head(gi, u):
                if gi >= 2:
                    vec.wait_ge(s["b_zT"], gi - 1)
                layer_norm(GT * gi, GT, z[:, u], u, s["b_z"])

            def ffn_mix(gi, u):
                vec.wait_ge(s["b_zTs"], gi + 1)
                if gi >= 2:
                    vec.wait_ge(s["b_r"], gi - 1)
                now, prev = zT[:, u, :, 1:T + 1], zT[:, u, :, 0:T]
                for j in range(2):
                    st.done(g.tensor_scalar(out=mixed[:, u, j], in0=prev, scalar1=mix_w[:, 2 + j:3 + j], scalar2=None, op0=ALU.mult))
                st.wait()
                for j in range(2):
                    i = g.scalar_tensor_tensor(out=mixed[:, u, j], in0=now, scalar=mix_w[:, j:j + 1], in1=mixed[:, u, j],
                                               op0=ALU.mult, op1=ALU.add)
                i.then_inc(s["b_mix"], 1)

            def ffn_tail(gi, u):
                vec.wait_ge(s["b_v"], gi + 1)
                vec.wait_ge(s["b_tanh"], gi + 1)
                st.done(g.scalar_tensor_tensor(out=recept[:, u], in0=recept[:, u], scalar=1.0, in1=bank[6][:, :], op0=ALU.add, op1=ALU.mult))
                st.wait()
                xr = x_res[:, gi * GT * D:(gi + 1) * GT * D]
                g.scalar_tensor_tensor(out=xr, in0=recept[:, u], scalar=half_g[:, 0:1], in1=xr, op0=ALU.mult, op1=ALU.add).then_inc(s["b_x2"], 1)

            ffn_head(0, 0)
            for gi in range(NG):
                if gi + 1 < NG:
                    ffn_head(gi + 1, (gi + 1) % 2)
                ffn_mix(gi, gi % 2)
                if gi:
                    ffn_tail(gi - 1, (gi - 1) % 2)
            ffn_tail(NG - 1, (NG - 1) % 2)
            if phases < 3:
                return

            def rotate(src, tmp, dst, n):
                hs, ht, hd = (x.rearrange("p (h e) -> p h e", e=8) for x in (src, tmp, dst))
                for half in range(2):
                    o, i = slice(4 * half, 4 * half + 4), slice(4 - 4 * half, 8 - 4 * half)
                    st.done(g.tensor_tensor(out=ht[:, :, o], in0=hs[:, :, i], in1=sin1[:, o].unsqueeze(1).to_broadcast([128, n, 4]), op=ALU.mult))
                st.done(g.tensor_tensor(out=hd, in0=hs, in1=cos1[:, :].unsqueeze(1).to_broadcast([128, n, 8]), op=ALU.mult))
                st.wait()
                st.done(g.tensor_tensor(out=dst, in0=dst, in1=tmp, op=ALU.add))
                st.wait()

            vec.wait_ge(s["c_consts"], 64)
            vec.wait_ge(s["kv_in"], 16)
            vec.wait_ge(s["c_zero"], 1)
            st.done(g.memset(own_row[:, :], 0.0))
            st.wait()
            for b in range(TB):
                r = slice(64 * b, 64 * b + 64)
                st.done(g.memset(own_row[r, b:b + 1], 1.0))
                for u in range(2):
                    st.done(g.memset(v_bd[r, u, 0, :, b, 16], 1.0))
            rotate(ctx_tok[:, :], kv_tmp, z1, NT * H1)
            st.done(g.tensor_copy(k1_s[:, 0], z1))
            st.done(g.tensor_copy(v1_s[:, 0], ctx_tok[:, :]))
            st.wait()
            g.tensor_tensor(out=k1_s[:, 1], in0=z1, in1=k1_s[:, 0], op=ALU.subtract)
            g.tensor_tensor(out=v1_s[:, 1], in0=ctx_tok[:, :], in1=v1_s[:, 0], op=ALU.subtract).then_inc(s["c_kv"], 1)
            vec.wait_ge(s["b_x2"], NG)
            vec.wait_ge(s["c_kv"], 1)
            layer_norm(0, NT, z1, 0, s["c_z"])
            vec.wait_ge(s["c_z"], 1)
            vec.wait_ge(s["c_ext"], 1)

            def queries(t, u):
                if not (isinstance(t, int) and t < 2):
                    vec.wait_ge(s["c_turn2"], t - 1)
                src = z1[:, bass.ds(t * D, D)]
                rotate(src, qr[:, u, 0], qr[:, u, 1], H1)
                qf = qr[:, u, 1].rearrange("p (h e) -> p h e", e=8)
                st.done(g.tensor_copy(q_st[:, u, :, 0, :], qf))
                st.done(g.tensor_copy(q_st[:, u, :, 2, :], qf))
                st.done(g.memset(q_st[:, u, :, 3, 4:5], 0.0))
                st.wait()
                g.tensor_tensor(out=q_st[:, u, :, 1, :], in0=qf, in1=q_st[:, u, :, 0, :], op=ALU.subtract).then_inc(s["c_q"], 1)

            def blocks(t, u, src, dst, ready):
                for i in range(4):
                    r = slice(32 * i, 32 * i + 32)
                    last = g.tensor_copy(dst[r, u, :, :, i, :].rearrange("p g b k -> p (g b) k"),
                                         src[r, u].rearrange("p g (b k) -> p (g b) k", b=TB))
                last.then_inc(ready, 1)

            def k_blocks(t, u):
                vec.wait_ge(s["c_k_out"], t + 1)
                blocks(t, u, kT1, k_bd, s["c_kbd"])

            def max1(t, u):
                vec.wait_ge(s["c_s"], t + 1)
                vec.wait_ge(s["c_turn"], t + 1)
                for half in range(2):
                    i = g.tensor_reduce(out=q_st[:, u, 8 * half:8 * half + 8, 3, 4], in_=bank[2 + half][:, :].rearrange("p (h k) -> p h k", k=T),
                                        axis=AXL.X, op=ALU.max, negate=True)
                i.then_inc(s["c_max"], 1)

            def q_blocks(t, u):
                vec.wait_ge(s["c_q2_out"], t + 1)
                if not (isinstance(t, int) and t < 2):
                    vec.wait_ge(s["c_sT"], t - 1)
                blocks(t, u, qT2, q_bd, s["c_qbd"])

            def p_low(t, u):
                vec.wait_ge(s["c_ph"], t + 1)
                g.tensor_tensor(out=p1_s[:, u, 1], in0=p1[:, u], in1=p1_s[:, u, 0], op=ALU.subtract).then_inc(s["c_pl"], 1)

            def output1(t, u):
                vec.wait_ge(s["c_pv"], t + 1)
                pv = bank[6][:, 0:272].rearrange("p (a b e) -> p a b e", a=H1 // 2, b=TB)
                st.done(g.reciprocal(rden1[:, u], pv[:, :, :, 16]))
                st.wait()
                for hh in range(2):
                    for b in range(TB):
                        r = slice(64 * hh, 64 * hh + 64)
                        st.done(g.tensor_tensor(out=o1[64 * b:64 * b + 64, u].rearrange("p (a h e) -> p a h e", a=8, h=2)[:, :, hh, :],
                                                in0=pv[r, :, b, 8 * hh:8 * hh + 8],
                                                in1=rden1[r, u, :, b:b + 1].to_broadcast([64, 8, 8]), op=ALU.mult))
                st.wait()
                xr = x_res[:, bass.ds(t * D, D)]
                g.scalar_tensor_tensor(out=xr, in0=o1[:, u], scalar=tanh_g[:, 1:2], in1=xr, op0=ALU.mult, op1=ALU.add).then_inc(s["c_x3"], 1)

            queries(0, 0)
            queries(1, 1)
            k_blocks(0, 0)
            max1(0, 0)
            q_blocks(0, 0)
            n1 = st.base + st.n - 2 * 7
            per1 = 7 + 5

            def turn1(t, u, more=2):
                st.at(n1 + 14 + per1 * t)
                if more:
                    k_blocks(t + 1, 1 - u)
                    max1(t + 1, 1 - u)
                p_low(t, u)
                if more:
                    q_blocks(t + 1, 1 - u)
                if more == 2:
                    queries(t + 2, u)
                output1(t, u)

            turn1(0, 0)
            turn1(1, 1)
            with vec.Fori(1, NT // 2 - 1) as i:
                turn1(2 * i, 0)
                turn1(2 * i + 1, 1)
            turn1(NT - 2, 0, 1)
            st.at(n1 + 14 + per1 * (NT - 2) + 5)
            nt = st.base
            turn_last = NT - 1
            p_low(NT - 1, 1)
            output1(NT - 1, 1)
            if phases < 4:
                return

            for k in range(E):
                vec.wait_ge(s["d_ws"], k + 1)
                g.tensor_tensor(out=w1_s[:, 1, FC * k:FC * k + FC, :], in0=bank[k % 2][:, :].rearrange("p (c f) -> p c f", f=128),
                                in1=w1_s[:, 0, FC * k:FC * k + FC, :], op=ALU.subtract).then_inc(s["d_wl"], 1)
            vec.wait_ge(s["c_x3"], NT)

            def moe_norm(gi, u):
                if gi >= 2:
                    vec.wait_ge(s["d_zT"], gi - 1)
                layer_norm(GT * gi, GT, z[:, u], u, s["d_z"])

            def moe_gates(gi, u):
                vec.wait_ge(s["d_zTs"], gi + 1)
                g.tensor_tensor(out=zTd_s[:, u, 1], in0=bank[2][:, :], in1=zTd_s[:, u, 0], op=ALU.subtract).then_inc(s["d_zTl"], 1)
                vec.wait_ge(s["d_log"], gi + 1)
                lg = logit[:, u]
                st.done(g.tensor_copy(lg, bank[3][:, 0:GT * E].rearrange("p (j e) -> p j e", e=E)))
                st.wait()
                for j in range(GT):
                    st.done(g.max(top[:, u, j], lg[:, j]))
                st.wait()
                m1 = top[:, u, :, 0:1].to_broadcast([128, GT, E])
                m2 = top[:, u, :, 1:2].to_broadcast([128, GT, E])
                above, equal, run, run2, want, ex = (gt_[:, k] for k in range(6))
                st.done(g.tensor_tensor(out=above, in0=lg, in1=m2, op=ALU.is_gt))
                st.done(g.tensor_tensor(out=equal, in0=lg, in1=m2, op=ALU.is_equal))
                st.done(g.tensor_tensor(out=ex, in0=lg, in1=m1, op=ALU.subtract))
                st.wait()
                src, dst = equal, run
                for step in (1, 2, 4):
                    st.done(g.tensor_copy(dst[:, :, 0:step], src[:, :, 0:step]))
                    st.done(g.tensor_tensor(out=dst[:, :, step:E], in0=src[:, :, step:E], in1=src[:, :, 0:E - step], op=ALU.add))
                    st.wait()
                    src, dst = dst, (run2 if dst is run else run)
                counted = src
                st.done(g.tensor_reduce(out=want[:, :, 0], in_=above, axis=AXL.X, op=ALU.add))
                st.wait()
                st.done(g.tensor_scalar(out=want[:, :, 0], in0=want[:, :, 0], scalar1=-1.0, scalar2=2.0, op0=ALU.mult, op1=ALU.add))
                st.wait()
                st.done(g.tensor_tensor(out=counted, in0=counted, in1=want[:, :, 0:1].to_broadcast([128, GT, E]), op=ALU.is_le))
                st.wait()
                st.done(g.tensor_tensor(out=equal, in0=equal, in1=counted, op=ALU.mult))
                st.wait()
                g.tensor_tensor(out=above, in0=above, in1=equal, op=ALU.add).then_inc(s["d_pick"], 1)
                vec.wait_ge(s["d_ex"], gi + 1)
                vec.wait_ge(s["d_pick"], gi + 1)
                st.done(g.tensor_tensor(out=ex, in0=ex, in1=above, op=ALU.mult))
                st.wait()
                st.done(g.tensor_reduce(out=want[:, :, 1], in_=ex, axis=AXL.X, op=ALU.add))
                st.wait()
                st.done(g.reciprocal(want[:, :, 2], want[:, :, 1]))
                st.wait()
                st.done(g.tensor_scalar(out=want[:, :, 2], in0=want[:, :, 2], scalar1=tanh_g[:, 3:4], scalar2=None, op0=ALU.mult))
                st.wait()
                g.tensor_tensor(out=gate[:, u], in0=ex, in1=want[:, :, 2:3].to_broadcast([128, GT, E]), op=ALU.mult).then_inc(s["d_gate"], 1)
                xr = x_res[:, gi * GT * D:(gi + 1) * GT * D]
                vec.wait_ge(s["d_b2"], gi + 1)
                st.done(g.tensor_tensor(out=xr, in0=xr, in1=bank[3][:, :], op=ALU.add))
                st.wait()

            def moe_sum(gi, e):
                for j in range(GT):
                    vec.wait_ge(s["d_y"], GT * (E * gi + e) + j + 1)
                    if e:
                        vec.wait_ge(s["d_acc"], GT * (E * gi + e - 1) + j + 1)
                    xr = x_res[:, (gi * GT + j) * D:(gi * GT + j + 1) * D]
                    g.scalar_tensor_tensor(out=xr, in0=bank[(6, 7, 0, 1)[j]][:, 0:D], scalar=gate[:, gi % 2, j, e:e + 1], in1=xr,
                                           op0=ALU.mult, op1=ALU.add).then_inc(s["d_acc"], 1)

            vec.wait_ge(s["d_wl"], E)
            for gi in range(NG):
                moe_norm(gi, gi % 2)
                moe_gates(gi, gi % 2)
                for e in range(E):
                    moe_sum(gi, e)

        @block.tensor
        def _(pe):
            g = nc.tensor
            pe.wait_ge(s["ident_up"], 3)
            pe.wait_ge(s["weights_in"], 48)
            for p in range(NP):
                i = g.transpose(bank[6][:, p * D:(p + 1) * D], wkv_raw[:, INNER + p * 128:INNER + (p + 1) * 128], ident[:, :])
            i.then_inc(s["wv_turned"], 1)
            pe.wait_ge(s["wv_copied"], 1)
            for h in range(H0):
                r = slice(64 * (h % 2), 64 * (h % 2) + 64)
                i = g.matmul(bank[4 + h % 2][:, (h // 2) * D:(h // 2 + 1) * D], wvT[r, h // 2, :], wo_sb[r, h // 2, :], start=True, stop=True)
                if h >= H0 - 2:
                    i.then_inc(s["wvo_mm"], 1)
            pe.wait_ge(s["w_split"], 1)
            pe.wait_ge(s["q_zero"], 1)
            pe.wait_ge(s["select_up"], 1)

            def turn_x(t, u):
                pe.wait_ge(s["a_split"], t + 1)
                for hl in range(2):
                    for b in range(TB):
                        i = g.transpose(bank[2][:, 0:256].bitcast(FP16)[:, (hl * TB + b) * 128:(hl * TB + b + 1) * 128],
                                        x_s[:, u, hl, b, :], ident_h[:, :])
                i.then_inc(s["a_turn"], 1)

            def product(dst, w, x, cols):
                for n, (i, j) in enumerate(((0, 0), (0, 1), (1, 0))):
                    last = g.matmul(dst, w[:, i, cols], x[j], start=n == 0, stop=n == 2)
                return last

            def project(t, u):
                pe.wait_ge(s["a_xT"], t + 1)
                for p in range(NP):
                    i = product(bank[2][:, p * 128:(p + 1) * 128], wq_s, [xT[:, u, j, :, 64:128] for j in range(2)],
                                slice(p * 128, (p + 1) * 128))
                i.then_inc(s["a_projq"], 1)
                for p in range(NP):
                    if not (isinstance(t, int) and t == 0 and p < 2):
                        pe.wait_ge(s["a_qk"], NP * t + p - 1)
                    cols = slice(p * 128, (p + 1) * 128)
                    product(bank[p % 2][:, 0:256], wk_s, [xT[:, u, j].rearrange("p b k -> p (b k)") for j in range(2)], cols)
                    product(bank[p % 2][:, 256:384], wkr_s, [xT[:, u, j, :, 0:64] for j in range(2)], cols).then_inc(s["a_proj"], 1)

            def scores(t, u):
                pe.wait_ge(s["a_qb"], t + 1)
                pe.wait_ge(s["a_kb"], t + 1)
                for b in range(TB):
                    for p in range(NP):
                        i = g.matmul(bank[4 + b][:, p * 128:(p + 1) * 128], qT_b[:, u, p, b].rearrange("p h q -> p (h q)"),
                                     kT_b[:, u, p, b, :], start=True, stop=True)
                    i.then_inc(s["a_s"], 1)

            def turn_max(t, u):
                pe.wait_ge(s["a_nmax"], TB * (t + 1))
                g.transpose(bank[3][0:8, 64:128].bitcast(BF16), nmax[:, u].rearrange("p b a -> p (b a)"), ident_b[:, :]).then_inc(s["a_nturn"], 1)

            def scores_t(t, u):
                pe.wait_ge(s["a_nmaxT"], t + 1)
                pe.wait_ge(s["a_k"], t + 1)
                pe.wait_ge(s["a_q"], t + 1)
                pe.wait_ge(s["a_qk"], NP * (t + 1))
                if not (isinstance(t, int) and t == 0):
                    pe.wait_ge(s["a_axs"], TB * t)
                for b in range(TB):
                    for p in range(NP):
                        d = bank[6 + b][:, p * 128:(p + 1) * 128]
                        g.matmul(d, kT[:, u, p, b, :], qT[:, u, p, b].rearrange("p h q -> p (h q)"), start=True, stop=False)
                        i = g.matmul(d, select[:, b * NP + p, :], nmaxT[:, u, :], start=False, stop=True)
                    i.then_inc(s["a_sT"], 1)

            def attend(t, u):
                pe.wait_ge(s["a_pl"], TB * (t + 1))
                pe.wait_ge(s["a_nmaxT"], t + 1)
                for h in range(H0):
                    for hl in range(2):
                        i = g.matmul(bank[3][:, h:h + 1], prob_s[:, u, hl, h].rearrange("p b q -> p (b q)"), ones_h[:, :],
                                     start=hl == 0, stop=hl == 1)
                i.then_inc(s["a_den"], 1)
                for b in range(TB):
                    for n, (i, j) in enumerate(((0, 0), (0, 1), (1, 0))):
                        last = g.matmul(bank[6 + b][:, :], x_s[:, u, i, b, :], prob_s[:, u, j, :, b, :], start=n == 0, stop=n == 2)
                    last.then_inc(s["a_ax"], 1)

            def project_out(t, u):
                pe.wait_ge(s["a_axs"], TB * (t + 1))
                for h in range(H0):
                    i = g.matmul(bank[h // 4][:, (h % 4) * D:(h % 4 + 1) * D], ax[:, u, h].rearrange("p b q -> p (b q)"),
                                 wvo[:, h, :], start=True, stop=True)
                i.then_inc(s["a_y"], 1)

            pe.wait_ge(s["wvo_up"], 2)
            turn_x(0, 0)
            project(0, 0)
            scores(0, 0)
            turn_max(0, 0)

            def turn(t, u, more=True):
                v = 1 - u
                if more:
                    pe.wait_ge(s["a_q"], t + 1)
                    turn_x(t + 1, v)
                scores_t(t, u)
                if more:
                    if not (isinstance(t, int) and t == 0):
                        pe.wait_ge(s["a_x1"], t)
                    project(t + 1, v)
                attend(t, u)
                if more:
                    pe.wait_ge(s["a_nmax"], TB * (t + 1))
                    scores(t + 1, v)
                project_out(t, u)
                if more:
                    pe.wait_ge(s["a_rden"], t + 1)
                    turn_max(t + 1, v)

            turn(0, 0)
            turn(1, 1)
            with pe.Fori(1, NT // 2 - 1) as i:
                turn(2 * i, 0)
                turn(2 * i + 1, 1)
            turn(NT - 2, 0)
            turn(NT - 1, 1, False)
            if phases < 2:
                return
            pe.wait_ge(s["ffn_in"], 80)
            pe.wait_ge(s["a_rden"], NT)
            for n in range(3):
                i = g.transpose(bank[3][:, n * D:(n + 1) * D], ffn_raw[:, n, :], ident[:, :])
            i.then_inc(s["ffn_turned"], 1)
            pe.wait_ge(s["ffn_wT_up"], 1)

            def z_turn(gi, u):
                pe.wait_ge(s["b_z"], gi + 1)
                if gi:
                    pe.wait_ge(s["b_zTs"], gi)
                for j in range(GT):
                    i = g.transpose(bank[2][:, j * D:(j + 1) * D], z[:, u, j * D:(j + 1) * D], ident[:, :])
                i.then_inc(s["b_zT"], 1)

            def keys_receptance(gi, u):
                pe.wait_ge(s["b_mix"], gi + 1)
                if gi:
                    pe.wait_ge(s["b_relu"], gi)
                    pe.wait_ge(s["b_tanh"], gi)
                g.matmul(bank[4][:, :], ffn_wT[:, 1, :], mixed[:, u, 1].rearrange("p b q -> p (b q)"), start=True, stop=True).then_inc(s["b_k"], 1)
                for j in range(GT):
                    i = g.matmul(bank[5][:, j * D:(j + 1) * D], mixed[:, u, 0].rearrange("p b q -> p (b q)")[:, j * D:(j + 1) * D],
                                 ffn_wT[:, 0, :], start=True, stop=True)
                i.then_inc(s["b_r"], 1)

            def values(gi, u):
                pe.wait_ge(s["b_sq"], gi + 1)
                if gi:
                    pe.wait_ge(s["b_x2"], gi)
                else:
                    pe.wait_ge(s["a_axs"], TB * NT)
                for j in range(GT):
                    i = g.matmul(bank[6][:, j * D:(j + 1) * D], act_k[:, u, j * D:(j + 1) * D], ffn_wT[:, 2, :], start=True, stop=True)
                i.then_inc(s["b_v"], 1)

            z_turn(0, 0)
            for gi in range(NG):
                if gi + 1 < NG:
                    z_turn(gi + 1, (gi + 1) % 2)
                keys_receptance(gi, gi % 2)
                values(gi, gi % 2)
            if phases < 3:
                return

            def turn_kq(t, u):
                pe.wait_ge(s["c_st"], t + 1)
                pe.wait_ge(s["c_q"], t + 1)
                if not (isinstance(t, int) and t == 0):
                    pe.wait_ge(s["c_q1_out"], t)
                pt = bank[0][:, :].bitcast(FP16)
                for a_, x in enumerate((k_st, q_st)):
                    for k in range(4):
                        i = g.transpose(pt[:, (4 * a_ + k) * 128:(4 * a_ + k + 1) * 128],
                                        x[:, u, 4 * k:4 * k + 4].rearrange("p h c e -> p (h c e)"), ident_h[:, :])
                i.then_inc(s["c_turn"], 1)

            def scores1(t, u):
                pe.wait_ge(s["c_kbd"], t + 1)
                pe.wait_ge(s["c_q1_out"], t + 1)
                if not (isinstance(t, int) and t == 0):
                    pe.wait_ge(s["c_max"], t)
                for b in range(TB):
                    for k in range(4):
                        i = g.matmul(bank[2 + k // 2][64 * b:64 * b + 64, (k % 2) * 256:(k % 2) * 256 + 256],
                                     qT1[:, u, k, 64 * b:64 * b + 64], k_bd[:, u, k, b].rearrange("p i k -> p (i k)"), start=True, stop=True)
                i.then_inc(s["c_s"], 1)

            def turn_q2(t, u):
                pe.wait_ge(s["c_max"], t + 1)
                if not (isinstance(t, int) and t == 0):
                    pe.wait_ge(s["c_q2_out"], t)
                for k in range(4):
                    i = g.transpose(bank[1][:, 0:256].bitcast(FP16)[:, k * 128:(k + 1) * 128],
                                    q_st[:, u, 4 * k:4 * k + 4].rearrange("p h c e -> p (h c e)"), ident_h[:, :])
                i.then_inc(s["c_turn2"], 1)

            def scores1_t(t, u):
                pe.wait_ge(s["c_qbd"], t + 1)
                if not (isinstance(t, int) and t == 0):
                    pe.wait_ge(s["c_exp"], t)
                for b in range(TB):
                    for k in range(4):
                        i = g.matmul(bank[4 + k // 2][64 * b:64 * b + 64, (k % 2) * 256:(k % 2) * 256 + 256],
                                     kT1[:, u, k, 64 * b:64 * b + 64], q_bd[:, u, k, b].rearrange("p i k -> p (i k)"), start=True, stop=True)
                i.then_inc(s["c_sT"], 1)

            def attend1(t, u):
                pe.wait_ge(s["c_pl"], t + 1)
                if not (isinstance(t, int) and t == 0):
                    pe.wait_ge(s["c_x3"], t)
                for p in range(H1 // 2):
                    for n, (i, j) in enumerate(((0, 0), (0, 1), (1, 0))):
                        last = g.matmul(bank[6][:, p * 34:p * 34 + 34], p1_s[:, u, i, p * 128:(p + 1) * 128],
                                        v_bd[:, u, j, p].rearrange("p b e -> p (b e)"), start=n == 0, stop=n == 2)
                last.then_inc(s["c_pv"], 1)

            pe.wait_ge(s["b_x2"], NG)
            turn_kq(0, 0)
            scores1(0, 0)
            turn_q2(0, 0)

            def turn1(t, u, more=True):
                if more:
                    turn_kq(t + 1, 1 - u)
                scores1_t(t, u)
                if more:
                    scores1(t + 1, 1 - u)
                    turn_q2(t + 1, 1 - u)
                attend1(t, u)

            turn1(0, 0)
            turn1(1, 1)
            with pe.Fori(1, NT // 2 - 1) as i:
                turn1(2 * i, 0)
                turn1(2 * i + 1, 1)
            turn1(NT - 2, 0)
            turn1(NT - 1, 1, False)
            if phases < 4:
                return

            pe.wait_ge(s["moe_in"], 48)
            pe.wait_ge(s["moe_in2"], 32)
            pe.wait_ge(s["c_x3"], NT)
            for k in range(2 * E):
                if k >= 2:
                    pe.wait_ge(s["d_ws"], k - 1)
                    if k - 2 < E:
                        pe.wait_ge(s["d_wl"], k - 1)
                for c in range(FC):
                    src = w1_raw[:, FC * k + c, :] if k < E else w2_raw[:, k - E, c * 128:(c + 1) * 128]
                    i = g.transpose(bank[k % 2][:, c * 128:(c + 1) * 128], src, ident[:, :])
                i.then_inc(s["d_w"], 1)
            g.transpose(bank[2][:, 0:E * FC], b1_raw[:, :], ident[0:E * FC, 0:E * FC])
            g.transpose(bank[2][:, 32:32 + E], rw_raw[:, :], ident[0:E, 0:E]).then_inc(s["d_small"], 1)
            pe.wait_ge(s["d_smalls"], 1)

            def moe_head(gi, u):
                pe.wait_ge(s["d_z"], gi + 1)
                if gi:
                    pe.wait_ge(s["d_zTl"], gi)
                for j in range(GT):
                    i = g.transpose(bank[2][:, j * D:(j + 1) * D], z[:, u, j * D:(j + 1) * D], ident[:, :])
                i.then_inc(s["d_zT"], 1)
                pe.wait_ge(s["d_zTs"], gi + 1)
                if gi:
                    pe.wait_ge(s["d_acc"], GT * E * (gi - 1) + 1)
                for j in range(GT):
                    i = g.matmul(bank[3][:, j * E:(j + 1) * E], zTd[:, u, j * D:(j + 1) * D], rwT[:, :], start=True, stop=True)
                i.then_inc(s["d_log"], 1)
                pe.wait_ge(s["d_gate"], gi + 1)
                for j in range(GT):
                    i = g.transpose(bank[3][0:E, j * 128:(j + 1) * 128], gate[:, u, j, :], ident[:, :])
                i.then_inc(s["d_gT"], 1)
                pe.wait_ge(s["d_gTs"], gi + 1)
                for j in range(GT):
                    i = g.matmul(bank[3][:, j * D:(j + 1) * D], gateT[:, u, j * 128:(j + 1) * 128], b2_sb[:, :], start=True, stop=True)
                i.then_inc(s["d_b2"], 1)

            def up(gi, u, e):
                n = E * gi + e
                if e == 0:
                    pe.wait_ge(s["d_zTl"], gi + 1)
                for c in range(FC):
                    k = FC * n + c
                    if k >= 2:
                        pe.wait_ge(s["d_hid"], k - 1)
                    for m, (i, j) in enumerate(((0, 0), (0, 1), (1, 0))):
                        last = g.matmul(bank[4 + c % 2][:, :], w1_s[:, i, e * FC + c, :], zTd_s[:, u, j], start=m == 0, stop=m == 2)
                    last.then_inc(s["d_h"], 1)

            def down(gi, u, e):
                n = E * gi + e
                pe.wait_ge(s["d_hid"], FC * (n + 1))
                for j in range(GT):
                    if n:
                        pe.wait_ge(s["d_acc"], GT * (n - 1) + j + 1)
                    for c in range(FC):
                        i = g.matmul(bank[(6, 7, 0, 1)[j]][:, 0:D], hid[:, e % 2, c, j * 128:(j + 1) * 128],
                                     w2T[:, e * FC + c, :], start=c == 0, stop=c == FC - 1)
                    i.then_inc(s["d_y"], 1)

            for gi in range(NG):
                moe_head(gi, gi % 2)
                for e in range(E):
                    up(gi, gi % 2, e)
                    if e:
                        down(gi, gi % 2, e - 1)
                down(gi, gi % 2, E - 1)


_INS = ["x", "ctx_1024", "g_xattn", "g_ffn", "L0_xattn_gamma_x", "L0_xattn_beta_x", "L0_xattn_gamma_l", "L0_xattn_beta_l",
        "L0_xattn_Wq", "L0_xattn_Wkv", "L0_xattn_Wo", "L0_ffn_W_r", "L0_ffn_W_k", "L0_ffn_W_v", "L0_ffn_mu_r", "L0_ffn_mu_k",
        "L1_ffn_router_w", "L1_ffn_w1", "L1_ffn_b1", "L1_ffn_w2", "L1_ffn_b2"]


def _constants():
    f32 = np.float32

    def angles(width):
        inv = (1.0 / f32(10000.0) ** (np.arange(0, width, 2, dtype=f32) / f32(width))).astype(f32)
        return (np.arange(T, dtype=f32)[:, None] * inv[None, :]).astype(f32)

    th = angles(HD0)
    cos, sin = np.cos(th).astype(f32).T, np.sin(th).astype(f32).T
    cos0 = np.ascontiguousarray(np.concatenate([cos, cos, cos, cos], 0))
    sin0 = np.ascontiguousarray(np.concatenate([-sin, sin, -sin, sin], 0))
    th = angles(HD1)
    cos, sin = np.cos(th).astype(f32), np.sin(th).astype(f32)
    cos1 = np.tile(np.concatenate([cos, cos], 1), (2, 1))
    sin1 = np.tile(np.concatenate([-sin, sin], 1), (2, 1))
    slope = np.array([2.0 ** (-8.0 * i / H1) for i in range(1, H1 + 1)]).astype(f32).astype(np.float64) * HD1 ** 0.5
    pos = np.tile(np.arange(T, dtype=np.float64), 2)
    q_ext, k_ext = np.zeros((128, H1, 8), np.float16), np.zeros((128, H1, 8), np.float16)
    shift = -slope[None, :] * pos[:, None]
    q_ext[:, :, 0] = slope
    q_ext[:, :, 1] = slope - slope.astype(np.float16)
    q_ext[:, :, 2] = shift
    q_ext[:, :, 3] = shift - shift.astype(np.float16)
    k_ext[:, :, 0] = k_ext[:, :, 1] = pos[:, None]
    k_ext[:, :, 2:5] = 1.0
    return {"cos0": cos0, "sin0": sin0, "cos1": cos1, "sin1": sin1, "q_ext": q_ext, "k_ext": k_ext}


def kernel(**inputs):
    import numpy as _np
    import concourse.bacc as _bacc
    from concourse import mybir as _mybir
    from concourse.bass_utils import run_bass_kernel_spmd as _run

    nc = _bacc.Bacc("TRN2", target_bir_lowering=False, num_devices=1)
    arrays, args = {}, {}
    held = {n: _np.ascontiguousarray(inputs[n]) for n in _INS}
    held.update(_constants())
    for name, v in held.items():
        arrays[f"in_{name}"] = v
        args[name] = nc.dram_tensor(f"in_{name}", v.shape, _mybir.dt.from_np(v.dtype), kind="ExternalInput").ap()
    out = nc.dram_tensor("out_0", (B, T, D), _mybir.dt.float32, kind="ExternalOutput").ap()
    program(nc, args, out)
    r = _run(nc, [arrays], core_ids=[0])
    return r.results[0]["out_0"]
```

```python
from contextlib import ExitStack

import numpy as np

import concourse.bass as bass
from concourse import mybir

FP32, FP16, BF16, I32 = mybir.dt.float32, mybir.dt.float16, mybir.dt.bfloat16, mybir.dt.int32
ALU, ACT, AXL = mybir.AluOpType, mybir.ActivationFunctionType, mybir.AxisListType

B, T, D = 32, 64, 128
TB = 2
NT = B // TB
EPS = 1e-5
H0, HD0 = 8, 64
NP = H0 // 2
INNER = H0 * HD0
H1, HD1 = 16, 8
E, F = 8, 512
FC = F // 128
REG = B * T + 128
NULL = E * REG
TOK = B * T
DIGITS = 6
SLOTS = 40
ROW = D + 2
ROUTED = ((0, 6), (6, 6), (12, 4))
RT = 6
GT = 4
NG = NT // GT
K_PAIRS = ((2, 4), (3, 5), (0, 0), (1, 1))
UP_BANKS = (2, 3, 6, 7)
RSQRT_MAGIC = 0x5F3759DF


class Steps:

    def __init__(self, eng, sem):
        self.eng, self.sem, self.base, self.n = eng, sem, 0, 0

    def at(self, base):
        self.base, self.n = base, 0

    def done(self, instruction):
        self.n += 1
        return instruction.then_inc(self.sem, 1)

    def wait(self, but=0):
        self.eng.wait_ge(self.sem, self.base + self.n - but)


def steady(eng, body, last):
    body(0, 0)
    body(1, 1)
    with eng.Fori(1, last // 2) as i:
        body(2 * i, 0)
        body(2 * i + 1, 1)


def rotate(g, st, src, tmp, dst, sin, cos):
    hs, ht, hd = (x.rearrange("p (h e) -> p h e", e=HD1) for x in (src, tmp, dst))
    n, half_d = hs.shape[1], HD1 // 2
    for half in range(2):
        o, i = slice(half_d * half, half_d * (half + 1)), slice(half_d * (1 - half), half_d * (2 - half))
        st.done(g.tensor_tensor(out=ht[:, :, o], in0=hs[:, :, i], in1=sin[:, o].unsqueeze(1).to_broadcast([128, n, half_d]), op=ALU.mult))
    st.wait()
    st.done(g.tensor_tensor(out=hd, in0=hs, in1=cos[:, :].unsqueeze(1).to_broadcast([128, n, HD1]), op=ALU.mult))
    st.wait()
    st.done(g.tensor_tensor(out=dst, in0=dst, in1=tmp, op=ALU.add))
    st.wait()


def slots(eng, body, table=None, ahead=0):
    def four(i, last=False):
        experts = None
        if table is not None:
            digits = eng.value_load(table[0:1, bass.ds(i, 1)], min_val=0, max_val=E ** DIGITS - 1)
            experts = [(digits // E ** n) % E for n in range(4 if last else 4 + ahead)]
        for j in range(4):
            body(4 * i + j, j, experts)

    four(0)
    with eng.Fori(1, SLOTS // 4 - 1) as i:
        four(i)
    four(SLOTS // 4 - 1, True)


def turns_and_routes(eng, turn, routes):
    turn(0, 0)
    turn(1, 1)
    with eng.Fori(1, 3) as i:
        turn(2 * i, 0)
        turn(2 * i + 1, 1)
    for t in range(6, NT):
        if t in routes:
            routes[t]()
        turn(t, t % 2)


def after(k, n):
    return not isinstance(k, int) or k >= n


def program(nc, a, out):
    ctx = ExitStack()
    with ctx:
        def sb(name, shape, dt=FP32):
            return ctx.enter_context(nc.sbuf_tensor(name, shape, dt))

        def sem(name):
            return ctx.enter_context(nc.semaphore(name))

        joint = sb("joint", [128, B * D])
        x_res = sb("x_res", [128, NT * D])
        gates = sb("gates", [128, 4])
        tanh_g = sb("tanh_g", [128, 4])
        ident = sb("ident", [128, 128])
        ident_h = sb("ident_h", [128, 128], FP16)
        ident_b = sb("ident_b", [128, 128], BF16)
        ones_f = sb("ones_f", [128, 1])
        ones_h = sb("ones_h", [128, 1], FP16)
        stat4 = sb("stat4", [128, 2, NT, 6])
        mv4 = sb("mv4", [128, 2, NT, 2])
        nwt4 = sb("nwt4", [128, 2, 5, NT])
        mix_w = sb("mix_w", [128, 4])
        ffn_raw = sb("ffn_raw", [128, 3, D])
        ffn_wT = sb("ffn_wT", [128, 3, D])
        half_g = sb("half_g", [128, 1])
        z = sb("z", [128, 2, GT * D])
        own_row = sb("own_row", [128, TB], FP16)
        cos1 = sb("cos1", [128, 8])
        sin1 = sb("sin1", [128, 8])
        q_ext = sb("q_ext", [128, H1, 8], FP16)
        k_ext = sb("k_ext", [128, H1, 8], FP16)
        ctx_tok = sb("ctx_tok", [128, NT * D])
        half_w = NT // 2 * D
        k_f, k_tmp, q_f, q_tmp = (joint[:, k * half_w:(k + 1) * half_w] for k in range(4))
        w1_raw = sb("w1_raw", [128, E * FC, D])
        w2_raw = sb("w2_raw", [128, E, F])
        b1_raw = sb("b1_raw", [E * FC, 128])
        b1T = sb("b1T", [128, E * FC])
        b2_row = sb("b2_row", [1, E * D])
        ones_row = sb("ones_row", [1, 128])
        tri = sb("tri", [128, 128], FP16)
        ones_sq = sb("ones_sq", [128, 128], FP16)
        tile_no = sb("tile_no", [128, SLOTS])
        region = sb("region", [128, E])
        tok_id = sb("tok_id", [128, NT])
        pad_rows = sb("pad_rows", [128, E + 1, ROW])
        pad_at = sb("pad_at", [128, E + 1])
        rw_raw = sb("rw_raw", [E, D])
        rwT = sb("rwT", [128, E])

        early = ExitStack()

        def sb0(name, shape, dt=FP32):
            return early.enter_context(nc.sbuf_tensor(name, shape, dt))

        gamma_j = sb0("gamma_j", [128, D])
        beta_j = sb0("beta_j", [128, D])
        wq_raw = sb0("wq_raw", [128, INNER])
        wkv_raw = sb0("wkv_raw", [128, 2 * INNER])
        wo_sb = sb0("wo_sb", [128, NP, D])
        select = sb0("select", [8, 8, 128], BF16)
        cos0 = sb0("cos0", [128, T])
        sin0 = sb0("sin0", [128, T])
        wq_s = sb0("wq_s", [128, 2, INNER], FP16)
        wk_s = sb0("wk_s", [128, 2, INNER], FP16)
        wkr_s = sb0("wkr_s", [128, 2, INNER], FP16)
        wvT = sb0("wvT", [128, NP, D])
        wvo = sb0("wvo", [128, H0, D])
        stat = sb0("stat", [128, B, 6])
        mv = sb0("mv", [128, B, 2])
        nwt = sb0("nwt", [128, 6, B])
        scale_j = sb0("scale_j", [128, B])
        bias_j = sb0("bias_j", [128, B])
        xn = sb0("xn", [128, 2, TB, D])
        x_s = sb0("x_s", [128, 2, 2, TB, D], FP16)
        xT = sb0("xT", [128, 2, 2, TB, 128], FP16)
        kT = sb0("kT", [128, 2, NP, TB, 128])
        kT_b = sb0("kT_b", [128, 2, NP, TB, 128], BF16)
        qT = sb0("qT", [128, 2, NP, TB, 2, T])
        qT_b = sb0("qT_b", [128, 2, NP, TB, 2, T], BF16)
        kcos = sb0("kcos", [128, 2, NP, TB, T])
        ksin = sb0("ksin", [128, 2, NP, TB, T])
        nmax = sb0("nmax", [128, 2, TB, NP], BF16)
        nmaxT = sb0("nmaxT", [8, 2, 128], BF16)
        prob = sb0("prob", [128, 2, H0, TB, T])
        prob_s = sb0("prob_s", [128, 2, 2, H0, TB, T], FP16)
        y_odd = sb0("y_odd", [128, D])
        rden = sb0("rden", [128, 2, H0])
        ax = sb0("ax", [128, 2, H0, TB, T])

        early.close()
        early = ExitStack()
        zT = sb0("zT", [128, 2, GT * TB, T + 1])
        mixed = sb0("mixed", [128, 2, 2, GT * TB, T])
        act_k = sb0("act_k", [128, 2, GT * D])
        recept = sb0("recept", [128, 2, GT * D])
        k1_s = sb0("k1_s", [128, 2, NT * D], FP16)
        v1_s = sb0("v1_s", [128, 2, NT * D], FP16)
        q1_s = sb0("q1_s", [128, 2, NT * D], FP16)
        q_st = sb0("q_st", [128, 2, H1, 4, 8], FP16)
        k_st = sb0("k_st", [128, 2, H1, 4, 8], FP16)
        v_bd = sb0("v_bd", [128, 2, 2, H1 // 2, TB, 17], FP16)
        qT1 = sb0("qT1", [128, 2, 4, 128], FP16)
        qT2 = sb0("qT2", [128, 2, 4, 128], FP16)
        kT1 = sb0("kT1", [128, 2, 4, 128], FP16)
        q_bd = sb0("q_bd", [128, 2, 4, TB, 4, T], FP16)
        k_bd = sb0("k_bd", [128, 2, 4, TB, 4, T], FP16)
        p1 = mixed[:, :, :, :, :].rearrange("p u a b q -> p u (a b q)")
        p1_s = sb0("p1_s", [128, 2, 2, H1 * T], FP16)
        rden1 = sb0("rden1", [128, 2, H1 // 2, TB])
        o1 = sb0("o1", [128, 2, D])
        w1_s = sb0("w1_s", [128, 2, E * FC * 128], FP16)
        w2T = sb0("w2T", [128, E * FC * D])
        top = sb0("top", [128, RT, 8])
        rs = sb0("rs", [128, 8, RT])
        picked = sb0("picked", [128, RT, E], FP16)
        slot_at = sb0("slot_at", [128, 2, NT], I32)
        count = sb0("count", [128, 2, E])
        per_e = sb0("per_e", [128, 6, E])
        per_ei = sb0("per_ei", [128, 2, E], I32)
        expert_pad = sb0("expert_pad", [128, SLOTS + DIGITS])
        tab_i = sb0("tab_i", [128, SLOTS], I32)
        experts_i = sb0("experts_i", [128, SLOTS // 4], I32)
        null_off = sb0("null_off", [128, SLOTS])
        rT = sb0("rT", [128, 2, 2, 128], FP16)
        y_row = sb0("y_row", [128, 4])
        y_at = sb0("y_at", [128, 4], I32)
        y_gate = sb0("y_gate", [128, 4])
        early.close()

        spent = [0, 0]

        def over(k, *shape):
            n = int(np.prod(shape))
            at = spent[k]
            spent[k] += n
            assert spent[k] <= E * FC * D
            axes = "abc"[:len(shape)]
            flat = (w1_raw, w2_raw)[k][:, :, :].rearrange("p a b -> p (a b)")[:, at:at + n]
            return flat.rearrange("p (" + " ".join(axes) + ") -> p " + " ".join(axes), **dict(zip(axes[1:], shape[1:])))

        row_buf = [over(r // 2, 2, n, ROW) for r, (_, n) in enumerate(ROUTED)]
        zTr = over(1, RT * D)
        rt = over(1, 14, RT, E)
        big = over(0, 2, SLOTS, E)
        tab = over(0, 3, SLOTS)
        rows = over(1, 4, ROW)
        hid = w1_raw[:, 0:16, :].rearrange("p (j c) f -> p j c f", c=FC)
        y_out = over(1, 4, D)

        rows_d = nc.dram_tensor("rows_by_expert", (NULL + 128, ROW), FP32, kind="Internal").ap()
        y_d = nc.dram_tensor("results", (2 * TOK + (E + 1) * 128 + SLOTS * 128, D), FP32, kind="Internal").ap()

        bank = [ctx.enter_context(nc.psum_tensor(f"bank{i}", [128, 512], FP32)) for i in range(8)]

        s = {}
        for name in (
            "consts_in weights_in x_in0 x_in1 x_in2 x_in3 x_res_in out_done ident_up select_up vec_step pool_step q_zero tanh_ready "
            "w_split wv_turned wv_copied wvo_mm wvo_up stats_up "
            "a_norm a_split a_turn a_xT a_proj a_projq a_q a_qk a_rope a_k a_kb a_s a_nmax a_nturn a_nmaxT "
            "a_sT a_exp a_ph a_pl a_den a_rden a_ax a_axs a_y a_x1 "
            "ffn_in ffn_turned ffn_wT_up zT_zero half_up b_z b_zT b_zTs b_mix b_k b_r b_tanh b_relu b_sq b_v b_x2 "
            "c_consts kv_in c_vh c_kv c_own c_ext c_zero c_ln c_qs c_q c_st c_v c_turn c_k_out c_q1_out c_kbd c_s c_max c_turn2 c_q2_out c_qbd c_sT "
            "c_exp c_ph c_pl c_pv c_o c_x3 "
            "moe_in moe_in2 d_w d_wl d_ws moe_consts pads_up "
            "r_z r_zT r_zTs r_log r_less r_exp r_pick r_rank r_slots r_sent r_tab r_exps r_pad "
            "e_row0 e_row1 e_row2 e_row3 e_turn e_xT e_ex e_gate e_up e_hid e_y e_out e_sent0 e_sent1 e_sent2 e_sent3 "
            "f_y0 f_y1 f_y2 f_y3 f_half f_x"
        ).split():
            s[name] = sem(name)

        block = ctx.enter_context(nc.Block())

        @block.sync
        def _(sp):
            ctx_rows = a["ctx_1024"].rearrange("b t d -> t b d")
            x_rows = a["x"].rearrange("b t d -> t b d")
            jt = joint[:, :].rearrange("p (b d) -> p b d", d=D)
            for c in range(4):
                bs = slice(c * 8, c * 8 + 8)
                sp.dma_start(jt[0:64, bs, :], ctx_rows[:, bs, :]).then_inc(s[f"x_in{c}"], 16)
                sp.dma_start(jt[64:128, bs, :], x_rows[:, bs, :]).then_inc(s[f"x_in{c}"], 16)
            for t, dst in ((a["L0_xattn_gamma_x"], gamma_j[0:64, :]), (a["L0_xattn_gamma_l"], gamma_j[64:128, :]),
                           (a["L0_xattn_beta_x"], beta_j[0:64, :]), (a["L0_xattn_beta_l"], beta_j[64:128, :])):
                sp.dma_start(dst, t.partition_broadcast(64)).then_inc(s["consts_in"], 16)
            sp.dma_start(cos0[:, :], a["cos0"]).then_inc(s["consts_in"], 16)
            sp.dma_start(sin0[:, :], a["sin0"]).then_inc(s["consts_in"], 16)
            sp.dma_start(gates[:, 0:2], a["g_xattn"].partition_broadcast(128)).then_inc(s["consts_in"], 16)
            sp.dma_start(gates[:, 2:4], a["g_ffn"].partition_broadcast(128)).then_inc(s["consts_in"], 16)
            tok = a["x"].rearrange("(n b) t d -> (b t) n d", b=TB)
            sp.dma_start(x_res[:, :].rearrange("p (n d) -> p n d", d=D), tok).then_inc(s["x_res_in"], 16)
            for n, name in enumerate(("L0_ffn_W_r", "L0_ffn_W_k", "L0_ffn_W_v")):
                sp.dma_start(ffn_raw[:, n, :], a[name]).then_inc(s["ffn_in"], 16)
            for n, name in enumerate(("L0_ffn_mu_r", "L0_ffn_mu_k")):
                sp.dma_start(mix_w[:, n:n + 1], a[name].rearrange("(d a) -> d a", a=1)).then_inc(s["ffn_in"], 16)
            for t, dst in (("cos1", cos1[:, :]), ("sin1", sin1[:, :]), ("q_ext", q_ext[:, :, :]), ("k_ext", k_ext[:, :, :])):
                sp.dma_start(dst, a[t]).then_inc(s["c_consts"], 16)
            sp.dma_start(ctx_tok[:, :].rearrange("p (n d) -> p n d", d=D),
                         a["ctx_1024"].rearrange("(n b) t d -> (b t) n d", b=TB)).then_inc(s["kv_in"], 16)
            sp.dma_start(b1_raw[:, :], a["L1_ffn_b1"].rearrange("e (c f) -> (e c) f", f=128)).then_inc(s["moe_in"], 16)
            sp.dma_start(b2_row[:, :], a["L1_ffn_b2"].rearrange("(a e) d -> a (e d)", a=1)).then_inc(s["moe_in"], 16)
            sp.dma_start(rw_raw[:, :], a["L1_ffn_router_w"]).then_inc(s["moe_in"], 16)
            sp.dma_start(w1_raw[:, :, :], a["L1_ffn_w1"].rearrange("e (c f) h -> f (e c) h", f=128)).then_inc(s["moe_in2"], 16)
            sp.dma_start(w2_raw[:, :, :], a["L1_ffn_w2"].rearrange("e h f -> h e f")).then_inc(s["moe_in2"], 16)
            for t, dst in (("tri", tri[:, :]), ("tile_no", tile_no[:, :]), ("region", region[:, :]), ("tok_id", tok_id[:, :]),
                           ("pad_at", pad_at[:, :])):
                sp.dma_start(dst, a[t]).then_inc(s["moe_consts"], 16)
            sp.wait_ge(s["pads_up"], 2)
            sp.dma_start(rows_d[NULL:NULL + 128, :], pad_rows[:, E, :]).then_inc(s["r_pad"], 16)
            sp.wait_ge(s["r_tab"], 1)
            for e in range(E):
                at = sp.value_load(per_ei[0:1, 1, e:e + 1], min_val=0, max_val=NULL - 128)
                sp.dma_start(rows_d[bass.ds(at, 128), :], pad_rows[:, e, :]).then_inc(s["r_pad"], 16)
            sp.wait_ge(s["r_pad"], (E + 1) * 16)
            sp.wait_ge(s["r_sent"], 2 * NT * 16)

            def load_rows(k, j, _):
                at = sp.value_load(tab_i[0:1, bass.ds(k, 1)], min_val=0, max_val=NULL)
                if after(k, 4):
                    sp.wait_ge(s["e_turn"], k - 3)
                    sp.wait_ge(s["e_ex"], k - 3)
                    sp.wait_ge(s["e_gate"], k - 3)
                sp.dma_start(rows[:, j, :], rows_d[bass.ds(at, 128), :]).then_inc(s[f"e_row{j}"], 16)

            slots(sp, load_rows)
            for j in range(4):
                sp.wait_ge(s[f"e_sent{j}"], SLOTS // 4 * 16)
            yv = y_d[0:2 * TOK, :].rearrange("(c n p) d -> p c n d", p=128, n=NT)
            for gi in range(NG):
                for c in range(2):
                    sp.dma_start(joint[:, c * NT * D + gi * GT * D:c * NT * D + (gi + 1) * GT * D].rearrange("p (n d) -> p n d", d=D),
                                 yv[:, c, gi * GT:(gi + 1) * GT, :]).then_inc(s[f"f_y{gi}"], 16)
            ov = out.rearrange("(n b) t d -> (b t) n d", b=TB)
            for gi in range(NG):
                sp.wait_ge(s["f_x"], gi + 1)
                sp.dma_start(ov[:, gi * GT:(gi + 1) * GT, :],
                             x_res[:, gi * GT * D:(gi + 1) * GT * D].rearrange("p (n d) -> p n d", d=D)).then_inc(s["out_done"], 16)
            sp.wait_ge(s["out_done"], NG * 16)

        @block.gpsimd
        def _(pool):
            g = nc.gpsimd
            st = Steps(pool, s["pool_step"])
            st.done(g.memset(ident[:, :], 0.0))
            st.done(g.memset(qT[:, :, :, :, :, :], 0.0))
            st.done(g.memset(qT_b[:, :, :, :, :, :], 0.0))
            st.done(g.memset(ones_f[:, :], 1.0))
            st.done(g.memset(ones_row[:, :], 1.0))
            st.done(g.memset(ones_sq[:, :], 1.0))
            g.memset(pad_rows[:, :, :], 0.0).then_inc(s["pads_up"], 1)
            g.memset(ones_h[:, :], 1.0).then_inc(s["q_zero"], 1)
            st.wait()
            g.affine_select(out=ident[:, :], in_=ident[:, :], compare_op=ALU.not_equal, fill=1.0,
                            base=0, pattern=[[-1, 128]], channel_multiplier=1).then_inc(s["ident_up"], 1)
            pool.wait_ge(s["ident_up"], 1)
            g.tensor_copy(ident_h[:, :], ident[:, :]).then_inc(s["ident_up"], 1)
            g.tensor_copy(ident_b[:, :], ident[:, :]).then_inc(s["ident_up"], 1)
            for r in range(8):
                i = g.tensor_copy(select[:, r, :], ident[0:8, r:r + 1].to_broadcast([8, 128]))
            i.then_inc(s["select_up"], 1)
            pool.wait_ge(s["consts_in"], 8 * 16)

            def cast(dst, src, shape):
                one = ones_f[:, :]
                for _ in range(len(shape) - 2):
                    one = one.unsqueeze(1)
                return g.tensor_tensor(out=dst, in0=src, in1=one.to_broadcast(shape), op=ALU.mult)

            def affine(t, u):
                pool.wait_ge(s["a_norm"], t + 1)
                x = xn[:, u, :, :]
                st.done(g.tensor_tensor(out=x, in0=x, in1=gamma_j[:, :].unsqueeze(1).to_broadcast([128, TB, D]), op=ALU.mult))
                st.wait()
                st.done(g.tensor_tensor(out=x, in0=x, in1=beta_j[:, :].unsqueeze(1).to_broadcast([128, TB, D]), op=ALU.add))

            def split(t, u):
                st.wait()
                st.done(cast(x_s[:, u, 0], xn[:, u, :, :], [128, TB, D]))
                st.wait()
                g.tensor_tensor(out=x_s[:, u, 1], in0=xn[:, u, :, :], in1=x_s[:, u, 0], op=ALU.subtract).then_inc(s["a_split"], 1)

            def prob_high(t, u):
                for b in range(TB):
                    pool.wait_ge(s["a_exp"], TB * t + b + 1)
                    cast(prob_s[:, u, 0, :, b, :], prob[:, u, :, b, :], [128, H0, T]).then_inc(s["a_ph"], 1)

            n0 = st.n
            per = 3
            for t in range(2):
                affine(t, t)
                split(t, t)

            def turn(t, u, more=True):
                st.at(n0 + 2 * per + per * t)
                if more:
                    affine(t + 2, u)
                if not (isinstance(t, int) and t < 2):
                    pool.wait_ge(s["a_den"], t - 1)
                prob_high(t, u)
                if more:
                    pool.wait_ge(s["a_ax"], TB * (t + 1))
                    split(t + 2, u)

            turn(0, 0)
            turn(1, 1)
            with pool.Fori(1, NT // 2 - 1) as i:
                turn(2 * i, 0)
                turn(2 * i + 1, 1)
            turn(NT - 2, 0, False)
            turn(NT - 1, 1, False)
            st.at(n0 + 2 * per + per * (NT - 2))
            pool.wait_ge(s["a_x1"], NT)
            pool.wait_ge(s["c_consts"], 64)
            g.memset(v_bd[:, :, :, :, :, :], 0.0).then_inc(s["c_zero"], 1)
            g.memset(k_bd[:, :, :, :, :, :], 0.0)
            g.memset(q_bd[:, :, :, :, :, :], 0.0).then_inc(s["c_zero"], 1)
            for u in range(2):
                g.tensor_copy(q_st[:, u, :, 3, :], q_ext[:, :, :])
                i = g.tensor_copy(k_st[:, u, :, 3, :], k_ext[:, :, :])
            i.then_inc(s["c_ext"], 1)
            pool.wait_ge(s["kv_in"], 16)
            for half in range(2):
                c = slice(half * half_w, (half + 1) * half_w)
                rotate(g, st, ctx_tok[:, c], k_tmp, k_f, sin1, cos1)
                st.done(cast(k1_s[:, 0, c], k_f, [128, half_w]))
                st.wait()
                st.done(g.tensor_tensor(out=k1_s[:, 1, c], in0=k_f, in1=k1_s[:, 0, c], op=ALU.subtract))
                st.wait()
            pool.wait_ge(s["c_vh"], 1)
            g.tensor_tensor(out=v1_s[:, 1], in0=ctx_tok[:, :], in1=v1_s[:, 0], op=ALU.subtract).then_inc(s["c_kv"], 1)
            pool.wait_ge(s["c_kv"], 1)
            pool.wait_ge(s["c_own"], 1)
            pool.wait_ge(s["c_ext"], 1)

            def heads_of(x, t, j):
                return x[:, j, bass.ds(t * D, D)].rearrange("p (h e) -> p h e", e=8)

            def stack_k(t, u):
                if not (isinstance(t, int) and t < 2):
                    pool.wait_ge(s["c_turn"], t - 1)
                for n, j in enumerate((0, 0, 1)):
                    i = cast(k_st[:, u, :, n, :], heads_of(k1_s, t, j), [128, H1, 8])
                i.then_inc(s["c_st"], 1)

            def stack_q(t, u):
                if not (isinstance(t, int) and t < 2):
                    pool.wait_ge(s["c_turn2"], t - 1)
                for n, j in enumerate((0, 1, 0)):
                    cast(q_st[:, u, :, n, :], heads_of(q1_s, t, j), [128, H1, 8])
                g.memset(q_st[:, u, :, 3, 4:5], 0.0).then_inc(s["c_q"], 1)

            def blocks_v(t, u):
                if not (isinstance(t, int) and t < 2):
                    pool.wait_ge(s["c_pv"], t - 1)
                for b in range(TB):
                    own = own_row[:, b:b + 1].unsqueeze(1).to_broadcast([128, H1 // 2, 16])
                    for j in range(2):
                        i = g.tensor_tensor(out=v_bd[:, u, j, :, b, 0:16], in0=v1_s[:, j, bass.ds(t * D, D)].rearrange("p (h e) -> p h e", e=16),
                                            in1=own, op=ALU.mult)
                i.then_inc(s["c_v"], 1)

            stack_k(0, 0)
            stack_k(1, 1)
            blocks_v(0, 0)
            pool.wait_ge(s["c_qs"], 1)
            stack_q(0, 0)
            stack_q(1, 1)
            stack_k(2, 0)
            stack_q(2, 0)

            def turn1(t, u):
                if not isinstance(t, int) or t + 3 < NT:
                    stack_k(t + 3, 1 - u)
                if not isinstance(t, int) or t + 1 < NT:
                    blocks_v(t + 1, 1 - u)
                if not isinstance(t, int) or t + 3 < NT:
                    stack_q(t + 3, 1 - u)

            def send_rows(r, js):
                pool.wait_ge(s["r_slots"], r + 1)
                for j in js:
                    for c in range(2):
                        g.indirect_dma_start(rows_d, bass.IndirectOffsetOnAxis(ap=slot_at[:, c, ROUTED[r][0] + j:ROUTED[r][0] + j + 1], axis=0),
                                             row_buf[r][:, c, j, :], None).then_inc(s["r_sent"], 16)

            turn1(0, 0)
            turn1(1, 1)
            pool.wait_ge(s["c_qs"], 2)
            with pool.Fori(1, 6) as i:
                turn1(2 * i, 0)
                turn1(2 * i + 1, 1)
            turn1(12, 0)
            send_rows(0, range(0, 2))
            turn1(13, 1)
            send_rows(0, range(2, 4))
            turn1(14, 0)
            send_rows(0, range(4, 6))
            send_rows(1, range(0, 6))
            send_rows(2, range(0, 4))

            def weight_out(k, j):
                g.tensor_tensor(out=y_gate[:, j:j + 1], in0=rows[:, j, D + 1:D + 2], in1=ones_f[:, :], op=ALU.mult).then_inc(s["e_gate"], 1)

            def send(k, j, _):
                pool.wait_ge(s["e_out"], k + 1)
                if not isinstance(k, int) or k + 2 < SLOTS:
                    weight_out(k + 2, (j + 2) % 4)
                g.indirect_dma_start(y_d, bass.IndirectOffsetOnAxis(ap=y_at[:, j:j + 1], axis=0), y_out[:, j, :], None)\
                 .then_inc(s[f"e_sent{j}"], 16)

            for j in range(2):
                pool.wait_ge(s["e_turn"], j + 1)
                weight_out(j, j)
            slots(pool, send)

        @block.scalar
        def _(act):
            g = nc.scalar
            act.dma_start(wq_raw[:, :], a["L0_xattn_Wq"]).then_inc(s["weights_in"], 16)
            act.dma_start(wkv_raw[:, :], a["L0_xattn_Wkv"]).then_inc(s["weights_in"], 16)
            act.dma_start(wo_sb[:, :, :], a["L0_xattn_Wo"].rearrange("(p r) n -> r p n", r=128)).then_inc(s["weights_in"], 16)
            act.wait_ge(s["consts_in"], 8 * 16)
            g.activation(tanh_g[:, :], gates[:, :], ACT.Tanh).then_inc(s["tanh_ready"], 1)
            act.wait_ge(s["wv_turned"], 1)
            g.activation(wvT[:, :, :], bank[6][:, :].rearrange("p (a d) -> p a d", d=D), ACT.Copy).then_inc(s["wv_copied"], 1)
            for half in range(2):
                act.wait_ge(s["wvo_mm"], half + 1)
                g.activation(wvo[:, half:H0:2, :], bank[4 + half][:, :].rearrange("p (a d) -> p a d", d=D),
                             ACT.Copy).then_inc(s["wvo_up"], 1)
            act.wait_ge(s["q_zero"], 1)

            def x_turned(t, u):
                act.wait_ge(s["a_turn"], t + 1)
                g.activation(xT[:, u], bank[2][:, 0:256].bitcast(FP16).rearrange("p (h b k) -> p h b k", h=2, b=TB),
                             ACT.Copy).then_inc(s["a_xT"], 1)

            def queries_out(t, u):
                act.wait_ge(s["a_projq"], t + 1)
                qq = bank[2][:, :].rearrange("p (a b q) -> p a b q", a=NP, b=TB)
                for h in range(2):
                    r = slice(64 * h, 64 * h + 64)
                    g.activation(qT[r, u, :, :, h, :], qq[r], ACT.Copy)
                    i = g.activation(qT_b[r, u, :, :, h, :], qq[r], ACT.Copy)
                i.then_inc(s["a_q"], 1)

            def latent_keys_out(t, u, ns):
                for n in ns:
                    p, k = K_PAIRS[n]
                    act.wait_ge(s["a_rope"], NP * t + n + 1)
                    kk = bank[k][:, 0:256].rearrange("p (b k) -> p b k", b=TB)
                    g.activation(kT[:, u, p, :, 64:128], kk[:, :, 64:128], ACT.Copy)
                    g.activation(kT_b[:, u, p, :, 64:128], kk[:, :, 64:128], ACT.Copy).then_inc(s["a_qk"], 1)

            def exps(t, u, b):
                act.wait_ge(s["a_sT"], TB * t + b + 1)
                g.activation(prob[:, u, :, b, :], bank[6 + b][:, :].rearrange("p (h q) -> p h q", h=H0), ACT.Exp,
                             scale=HD0 ** -0.5).then_inc(s["a_exp"], 1)

            def ax_out(t, u):
                for b in range(TB):
                    act.wait_ge(s["a_ax"], TB * t + b + 1)
                    g.activation(ax[:, u, :, b, :], bank[6 + b][:, :].rearrange("p (h q) -> p h q", h=H0), ACT.Copy).then_inc(s["a_axs"], 1)

            def nmax_out(t, u):
                act.wait_ge(s["a_nturn"], t + 1)
                g.activation(nmaxT[:, u, :], bank[3][0:8, 64:128].bitcast(BF16), ACT.Copy).then_inc(s["a_nmaxT"], 1)

            x_turned(0, 0)
            latent_keys_out(0, 0, (0, 1))
            queries_out(0, 0)
            latent_keys_out(0, 0, (2, 3))
            nmax_out(0, 0)
            x_turned(1, 1)

            def turn(t, u, more=2):
                if not (isinstance(t, int) and t < 2):
                    act.wait_ge(s["a_ph"], TB * (t - 1))
                    act.wait_ge(s["a_pl"], TB * (t - 1))
                exps(t, u, 0)
                if more:
                    if not (isinstance(t, int) and t < 1):
                        act.wait_ge(s["a_sT"], TB * t)
                        act.wait_ge(s["a_s"], TB * t)
                    latent_keys_out(t + 1, 1 - u, (0, 1))
                exps(t, u, 1)
                if more:
                    queries_out(t + 1, 1 - u)
                    latent_keys_out(t + 1, 1 - u, (2, 3))
                if not (isinstance(t, int) and t < 2):
                    act.wait_ge(s["a_y"], t - 1)
                ax_out(t, u)
                if more:
                    nmax_out(t + 1, 1 - u)
                if more == 2:
                    x_turned(t + 2, u)

            turn(0, 0)
            turn(1, 1)
            with act.Fori(1, NT // 2 - 1) as i:
                turn(2 * i, 0)
                turn(2 * i + 1, 1)
            turn(NT - 2, 0, 1)
            turn(NT - 1, 1, 0)
            act.wait_ge(s["ffn_turned"], 1)
            g.activation(ffn_wT[:, :, :], bank[3][:, 0:384].rearrange("p (a d) -> p a d", d=D), ACT.Copy)
            g.activation(b1T[:, :], bank[3][:, 384:384 + E * FC], ACT.Copy)
            g.activation(rwT[:, :], bank[3][:, 416:416 + E], ACT.Copy).then_inc(s["ffn_wT_up"], 1)

            def z_out(gi, u):
                act.wait_ge(s["b_zT"], gi + 1)
                if gi >= 2:
                    act.wait_ge(s["b_mix"], gi - 1)
                g.activation(zT[:, u, :, 1:T + 1], bank[2][:, :].rearrange("p (b q) -> p b q", q=T), ACT.Copy).then_inc(s["b_zTs"], 1)

            def weights_out(k):
                act.wait_ge(s["d_w"], k + 1)
                dst = w1_s[:, 0, :] if k < E else w2T[:, :]
                g.activation(dst[:, F * (k % E):F * (k % E + 1)], bank[k % 2][:, :], ACT.Copy).then_inc(s["d_ws"], 1)

            z_out(0, 0)
            act.wait_ge(s["kv_in"], 16)
            g.activation(v1_s[:, 0], ctx_tok[:, :], ACT.Copy).then_inc(s["c_vh"], 1)
            for gi in range(NG):
                u = gi % 2
                if gi + 1 < NG:
                    z_out(gi + 1, 1 - u)
                weights_out(4 * gi)
                weights_out(4 * gi + 1)
                act.wait_ge(s["b_k"], gi + 1)
                if gi >= 2:
                    act.wait_ge(s["b_v"], gi - 1)
                g.activation(act_k[:, u], bank[4][:, :], ACT.Relu).then_inc(s["b_relu"], 1)
                act.wait_ge(s["b_relu"], gi + 1)
                g.activation(act_k[:, u], act_k[:, u], ACT.Square).then_inc(s["b_sq"], 1)
                act.wait_ge(s["b_r"], gi + 1)
                if gi >= 2:
                    act.wait_ge(s["b_x2"], gi - 1)
                g.activation(recept[:, u], bank[5][:, :], ACT.Tanh, scale=0.5).then_inc(s["b_tanh"], 1)
                weights_out(4 * gi + 2)
                weights_out(4 * gi + 3)

            def k_q1_out(t, u):
                act.wait_ge(s["c_turn"], t + 1)
                pt = bank[0][:, :].bitcast(FP16).rearrange("p (a g k) -> p a g k", a=2, g=4)
                if not (isinstance(t, int) and t < 2):
                    act.wait_ge(s["c_sT"], t - 1)
                    act.wait_ge(s["c_kbd"], t - 1)
                g.activation(kT1[:, u], pt[:, 0], ACT.Copy).then_inc(s["c_k_out"], 1)
                g.activation(qT1[:, u], pt[:, 1], ACT.Copy).then_inc(s["c_q1_out"], 1)

            def q2_out(t, u):
                act.wait_ge(s["c_turn2"], t + 1)
                if not (isinstance(t, int) and t < 2):
                    act.wait_ge(s["c_qbd"], t - 1)
                g.activation(qT2[:, u], bank[1][:, 0:256].bitcast(FP16).rearrange("p (g k) -> p g k", g=4), ACT.Copy).then_inc(s["c_q2_out"], 1)

            def exp1(t, u):
                act.wait_ge(s["c_sT"], t + 1)
                if not (isinstance(t, int) and t < 2):
                    act.wait_ge(s["c_pl"], t - 1)
                    act.wait_ge(s["c_pv"], t - 1)
                for half in range(2):
                    c = slice(512 * half, 512 * half + 512)
                    i = g.activation(p1[:, u, c], bank[4 + half][:, :], ACT.Exp, scale=HD1 ** -0.5)
                i.then_inc(s["c_exp"], 1)
                act.wait_ge(s["c_exp"], t + 1)
                g.activation(p1_s[:, u, 0], p1[:, u], ACT.Copy).then_inc(s["c_ph"], 1)

            k_q1_out(0, 0)
            q2_out(0, 0)
            k_q1_out(1, 1)

            def turn1(t, u):
                exp1(t, u)
                if not isinstance(t, int) or t + 2 < NT:
                    k_q1_out(t + 2, u)
                if not isinstance(t, int) or t + 1 < NT:
                    q2_out(t + 1, 1 - u)

            zT_chunks = [0]

            def route_turned(r):
                for at in range(0, ROUTED[r][1], 4):
                    n = min(4, ROUTED[r][1] - at)
                    zT_chunks[0] += 1
                    act.wait_ge(s["r_zT"], zT_chunks[0])
                    g.activation(zTr[:, at * D:(at + n) * D], bank[7][:, 0:n * D], ACT.Copy).then_inc(s["r_zTs"], 1)

            def route_exp(r):
                act.wait_ge(s["r_less"], r + 1)
                x = rt[:, 5, 0:ROUTED[r][1]]
                g.activation(x, x, ACT.Exp).then_inc(s["r_exp"], 1)

            turns_and_routes(act, turn1, {8: lambda: route_turned(0), 9: lambda: route_exp(0),
                                          14: lambda: route_turned(1), 15: lambda: route_exp(1)})
            route_turned(2)
            route_exp(2)

            def gelus(k, j, expert):
                act.wait_ge(s["e_up"], k + 1)
                if after(k, 4):
                    act.wait_ge(s["e_y"], k - 3)
                for c in range(FC):
                    i = g.activation(hid[:, j, c], bank[UP_BANKS[j]][:, c * 128:(c + 1) * 128], ACT.Gelu,
                                     bias=b1T[:, bass.ds(expert[j] * FC + c, 1)])
                i.then_inc(s["e_hid"], 1)

            act.wait_ge(s["r_exps"], 1)
            slots(act, gelus, experts_i)

        @block.vector
        def _(vec):
            g = nc.vector
            st = Steps(vec, s["vec_step"])

            def rsqrt(y, v, tmp, out_sem=None):
                half, sq, bits = tmp
                st.wait()
                st.done(g.tensor_scalar(out=half, in0=v, scalar1=-0.5, scalar2=None, op0=ALU.mult))
                st.done(g.tensor_scalar(out=bits.bitcast(I32), in0=v.bitcast(I32), scalar1=1, scalar2=None, op0=ALU.logical_shift_right))
                st.wait()
                st.done(g.tensor_scalar(out=y.bitcast(I32), in0=bits.bitcast(I32), scalar1=-1.0, scalar2=float(RSQRT_MAGIC),
                                        op0=ALU.mult, op1=ALU.add))
                for k in range(3):
                    st.wait()
                    st.done(g.tensor_tensor(out=sq, in0=y, in1=y, op=ALU.mult))
                    st.wait()
                    st.done(g.tensor_tensor(out=sq, in0=sq, in1=half, op=ALU.mult))
                    st.wait()
                    st.done(g.scalar_tensor_tensor(out=y, in0=sq, scalar=1.5, in1=y, op0=ALU.add, op1=ALU.mult))

            for c in range(4):
                vec.wait_ge(s[f"x_in{c}"], 32)
                for b in range(8 * c, 8 * c + 8):
                    st.done(g.bn_stats(stat[:, b, :], joint[:, b * D:(b + 1) * D]))
            st.wait()
            for b in range(B):
                st.done(g.bn_aggr(mv[:, b, :], stat[:, b, :]))
            st.wait()
            var, y, h, sq, bits, w = (nwt[:, i, :] for i in range(6))
            st.done(g.tensor_scalar(out=var, in0=mv[:, :, 1], scalar1=EPS, scalar2=None, op0=ALU.add))
            rsqrt(y, var, (h, sq, bits))
            st.wait()
            st.done(g.tensor_copy(scale_j[:, :], y))
            hi = slice(64, 128)
            st.wait()
            st.done(g.tensor_tensor(out=w[hi], in0=y[hi], in1=y[hi], op=ALU.mult))
            st.wait()
            st.done(g.tensor_tensor(out=w[hi], in0=w[hi], in1=mv[hi, :, 1], op=ALU.mult))
            st.wait()
            st.done(g.tensor_scalar(out=w[hi], in0=w[hi], scalar1=EPS, scalar2=None, op0=ALU.add))
            rsqrt(y[hi], w[hi], (h[hi], sq[hi], bits[hi]))
            st.wait()
            st.done(g.tensor_tensor(out=scale_j[hi, :], in0=scale_j[hi, :], in1=y[hi], op=ALU.mult))
            st.wait()
            st.done(g.scalar_tensor_tensor(out=bias_j[:, :], in0=mv[:, :, 0], scalar=-1.0, in1=scale_j[:, :],
                                           op0=ALU.mult, op1=ALU.mult))
            st.wait()

            def norm(t, u):
                for b in range(TB):
                    i = g.tensor_scalar(out=xn[:, u, b, :], in0=joint[:, bass.ds((TB * t + b) * D, D)],
                                        scalar1=scale_j[:, bass.ds(TB * t + b, 1)], scalar2=bias_j[:, bass.ds(TB * t + b, 1)],
                                        op0=ALU.mult, op1=ALU.add)
                i.then_inc(s["a_norm"], 1)

            norm(0, 0)
            norm(1, 1)
            vec.wait_ge(s["weights_in"], 48)
            wk_raw = wkv_raw[:, 0:INNER]
            for raw, split in ((wq_raw[:, :], wq_s), (wk_raw, wk_s)):
                st.done(g.tensor_copy(split[:, 0, :], raw))
                st.wait()
                st.done(g.tensor_tensor(out=split[:, 1, :], in0=raw, in1=split[:, 0, :], op=ALU.subtract))
            st.wait()
            for hl in range(2):
                src = wk_s[:, hl, :].rearrange("p (h a d) -> p h a d", a=2, d=HD0 // 2)
                dst = wkr_s[:, hl, :].rearrange("p (h a d) -> p h a d", a=2, d=HD0 // 2)
                for half in range(2):
                    i = g.tensor_copy(dst[:, :, half, :], src[:, :, 1 - half, :])
            i.then_inc(s["w_split"], 1)
            vec.wait_ge(s["consts_in"], 8 * 16)
            vec.wait_ge(s["x_res_in"], 16)
            vec.wait_ge(s["tanh_ready"], 1)

            def rope(t, u, n):
                p, k = K_PAIRS[n]
                vec.wait_ge(s["a_proj"], NP * t + n + 1)
                kk = bank[k][:, 0:256].rearrange("p (b k) -> p b k", b=TB)[:, :, 0:64]
                kr = bank[k][:, 256:384].rearrange("p (b k) -> p b k", b=TB)
                g.tensor_tensor(out=kcos[:, u, p], in0=kk, in1=cos0[:, :].unsqueeze(1).to_broadcast([128, TB, T]), op=ALU.mult)
                g.tensor_tensor(out=ksin[:, u, p], in0=kr, in1=sin0[:, :].unsqueeze(1).to_broadcast([128, TB, T]), op=ALU.mult).then_inc(s["a_rope"], 1)

            def rope_sum(t, u):
                vec.wait_ge(s["a_rope"], NP * (t + 1))
                kx = kT[:, u, :, :, 0:64].rearrange("p a b k -> p (a b) k")
                g.tensor_tensor(out=kx, in0=kcos[:, u].rearrange("p a b k -> p (a b) k"),
                                in1=ksin[:, u].rearrange("p a b k -> p (a b) k"), op=ALU.add).then_inc(s["a_k"], 1)
                vec.wait_ge(s["a_k"], t + 1)
                g.tensor_copy(kT_b[:, u, :, :, 0:64].rearrange("p a b k -> p (a b) k"), kx).then_inc(s["a_kb"], 1)

            def prob_low(t, u, b):
                vec.wait_ge(s["a_ph"], TB * t + b + 1)
                g.tensor_tensor(out=prob_s[:, u, 1, :, b, :], in0=prob[:, u, :, b, :], in1=prob_s[:, u, 0, :, b, :],
                                op=ALU.subtract).then_inc(s["a_pl"], 1)

            def maxima(t, u):
                for b in range(TB):
                    vec.wait_ge(s["a_s"], TB * t + b + 1)
                    g.tensor_reduce(out=nmax[:, u, b, :], in_=bank[4 + b][:, :].rearrange("p (a k) -> p a k", a=NP), axis=AXL.X,
                                    op=ALU.max, negate=True).then_inc(s["a_nmax"], 1)

            def denominators(t, u):
                vec.wait_ge(s["a_den"], t + 1)
                st.done(g.reciprocal(rden[:, u, :], bank[3][:, 0:H0]))
                st.wait()
                g.tensor_scalar(out=rden[:, u, :], in0=rden[:, u, :], scalar1=tanh_g[:, 0:1], scalar2=None, op0=ALU.mult).then_inc(s["a_rden"], 1)

            def residual(t, u):
                vec.wait_ge(s["a_y"], t + 1)
                vec.wait_ge(s["a_rden"], t + 1)
                xr = x_res[:, bass.ds(t * D, D)]
                for h in range(H0):
                    if h >= 2:
                        st.wait(1)
                    y, r = bank[h // 4][:, (h % 4) * D:(h % 4 + 1) * D], rden[:, u, h:h + 1]
                    dst = y_odd[:, :] if h % 2 else xr
                    if h == 1:
                        st.done(g.tensor_scalar(out=dst, in0=y, scalar1=r, scalar2=None, op0=ALU.mult))
                    else:
                        st.done(g.scalar_tensor_tensor(out=dst, in0=y, scalar=r, in1=dst, op0=ALU.mult, op1=ALU.add))
                st.wait()
                g.tensor_tensor(out=xr, in0=xr, in1=y_odd[:, :], op=ALU.add).then_inc(s["a_x1"], 1)

            n0 = st.n
            for p in range(NP):
                rope(0, 0, p)
            rope_sum(0, 0)
            maxima(0, 0)
            vec.wait_ge(s["a_split"], 1)
            norm(2, 0)
            per = H0 + 1 + 1

            def stats(t, k):
                st.done(g.bn_stats(stat4[:, :, :, :].rearrange("p a n s -> p (a n s)")[:, bass.ds(k * NT * 6 + t * 6, 6)], x_res[:, bass.ds(t * D, D)]))

            def mean_var(first, count, k):
                st.wait()
                for t in range(first, first + count):
                    st.done(g.bn_aggr(mv4[:, k, t, :], stat4[:, k, t, :]))

            def turn(t, u, more=2):
                st.at(n0 + per * t - (0 if isinstance(t, int) and t == 0 else 1))
                v = 1 - u
                if more and not (isinstance(t, int) and t < 1):
                    vec.wait_ge(s["a_sT"], TB * t)
                    vec.wait_ge(s["a_s"], TB * t)
                for n in range(NP):
                    if more:
                        rope(t + 1, v, n)
                    if n % 2:
                        prob_low(t, u, n // 2)
                if more:
                    rope_sum(t + 1, v)
                denominators(t, u)
                if not (isinstance(t, int) and t == 0):
                    vec.wait_ge(s["a_x1"], t)
                    stats(t - 1, 0)
                if more:
                    if not (isinstance(t, int) and t < 1):
                        vec.wait_ge(s["a_nturn"], t)
                    maxima(t + 1, v)
                if more == 2:
                    vec.wait_ge(s["a_split"], t + 2)
                    norm(t + 3, v)
                residual(t, u)

            turn(0, 0)
            turn(1, 1)
            with vec.Fori(1, NT // 2 - 2) as i:
                turn(2 * i, 0)
                turn(2 * i + 1, 1)
            turn(NT - 4, 0)
            turn(NT - 3, 1, 1)
            turn(NT - 2, 0, 1)
            turn(NT - 1, 1, 0)
            st.at(n0 + per * NT - 1)

            def rstd(k, first, count):
                st.wait()
                var, y, h, sq, bits = (nwt4[:, k, n, first:first + count] for n in range(5))
                st.done(g.tensor_scalar(out=var, in0=mv4[:, k, first:first + count, 1], scalar1=EPS, scalar2=None, op0=ALU.add))
                rsqrt(y, var, (h, sq, bits))
                st.wait()

            def normalize(k, first, count, dst):
                for j in range(count):
                    t = first + j
                    i = g.tensor_scalar(out=dst[:, j * D:(j + 1) * D], in0=x_res[:, t * D:(t + 1) * D],
                                        scalar1=mv4[:, k, t, 0:1], scalar2=nwt4[:, k, 1, t:t + 1], op0=ALU.subtract, op1=ALU.mult)
                return i

            vec.wait_ge(s["ffn_in"], 80)
            st.done(g.tensor_scalar(out=mix_w[:, 2:4], in0=mix_w[:, 0:2], scalar1=-1.0, scalar2=1.0, op0=ALU.mult, op1=ALU.add))
            st.done(g.tensor_scalar(out=half_g[:, :], in0=tanh_g[:, 2:3], scalar1=0.5, scalar2=None, op0=ALU.mult))
            st.done(g.memset(zT[:, :, :, 0:1], 0.0))
            vec.wait_ge(s["a_x1"], NT)
            stats(NT - 1, 0)
            mean_var(0, NT, 0)
            rstd(0, 0, NT)

            def ffn_head(gi, u):
                if gi >= 2:
                    vec.wait_ge(s["b_zT"], gi - 1)
                normalize(0, GT * gi, GT, z[:, u]).then_inc(s["b_z"], 1)

            def ffn_mix(gi, u):
                vec.wait_ge(s["b_zTs"], gi + 1)
                if gi >= 2:
                    vec.wait_ge(s["b_r"], gi - 1)
                now, prev = zT[:, u, :, 1:T + 1], zT[:, u, :, 0:T]
                for j in range(2):
                    st.done(g.tensor_scalar(out=mixed[:, u, j], in0=prev, scalar1=mix_w[:, 2 + j:3 + j], scalar2=None, op0=ALU.mult))
                st.wait()
                for j in range(2):
                    i = g.scalar_tensor_tensor(out=mixed[:, u, j], in0=now, scalar=mix_w[:, j:j + 1], in1=mixed[:, u, j],
                                               op0=ALU.mult, op1=ALU.add)
                i.then_inc(s["b_mix"], 1)

            def ffn_tail(gi, u):
                vec.wait_ge(s["b_v"], gi + 1)
                vec.wait_ge(s["b_tanh"], gi + 1)
                st.done(g.scalar_tensor_tensor(out=recept[:, u], in0=recept[:, u], scalar=1.0, in1=bank[6][:, :], op0=ALU.add, op1=ALU.mult))
                st.wait()
                xr = x_res[:, gi * GT * D:(gi + 1) * GT * D]
                g.scalar_tensor_tensor(out=xr, in0=recept[:, u], scalar=half_g[:, 0:1], in1=xr, op0=ALU.mult, op1=ALU.add).then_inc(s["b_x2"], 1)

            def weights_low(k):
                vec.wait_ge(s["d_ws"], k + 1)
                c = slice(F * k, F * (k + 1))
                g.tensor_tensor(out=w1_s[:, 1, c], in0=bank[k % 2][:, :], in1=w1_s[:, 0, c], op=ALU.subtract).then_inc(s["d_wl"], 1)

            def queries_half(half):
                first, c = half * (NT // 2), slice(half * half_w, (half + 1) * half_w)
                vec.wait_ge(s["b_x2"], (half + 1) * NG // 2)
                for t in range(first, first + NT // 2):
                    stats(t, 1)
                mean_var(first, NT // 2, 1)
                rstd(1, first, NT // 2)
                normalize(1, first, NT // 2, q_f).then_inc(s["c_ln"], 1)
                vec.wait_ge(s["c_ln"], half + 1)
                rotate(g, st, q_f, q_tmp, q_f, sin1, cos1)
                st.done(g.tensor_copy(q1_s[:, 0, c], q_f))
                st.wait()
                g.tensor_tensor(out=q1_s[:, 1, c], in0=q_f, in1=q1_s[:, 0, c], op=ALU.subtract).then_inc(s["c_qs"], 1)
                vec.wait_ge(s["c_qs"], half + 1)

            vec.wait_ge(s["c_consts"], 64)
            ffn_head(0, 0)
            for gi in range(NG):
                if gi + 1 < NG:
                    ffn_head(gi + 1, (gi + 1) % 2)
                ffn_mix(gi, gi % 2)
                for k in range(4 * gi, 4 * gi + 4):
                    if k < E:
                        weights_low(k)
                if gi:
                    ffn_tail(gi - 1, (gi - 1) % 2)
                if gi == NG // 2:
                    queries_half(0)
                    vec.wait_ge(s["c_zero"], 1)
                    st.done(g.memset(own_row[:, :], 0.0))
                    st.wait()
                    for b in range(TB):
                        r = slice(64 * b, 64 * b + 64)
                        i = g.memset(own_row[r, b:b + 1], 1.0)
                        for u in range(2):
                            st.done(g.memset(v_bd[r, u, 0, :, b, 16], 1.0))
                    i.then_inc(s["c_own"], 1)
            ffn_tail(NG - 1, (NG - 1) % 2)
            queries_half(1)
            st.wait()

            vec.wait_ge(s["c_zero"], 2)

            def blocks(t, u, src, dst, ready):
                for i in range(4):
                    r = slice(32 * i, 32 * i + 32)
                    last = g.tensor_copy(dst[r, u, :, :, i, :].rearrange("p g b k -> p (g b) k"),
                                         src[r, u].rearrange("p g (b k) -> p (g b) k", b=TB))
                last.then_inc(ready, 1)

            def k_blocks(t, u):
                vec.wait_ge(s["c_k_out"], t + 1)
                blocks(t, u, kT1, k_bd, s["c_kbd"])

            def max1(t, u):
                vec.wait_ge(s["c_s"], t + 1)
                vec.wait_ge(s["c_turn"], t + 1)
                for half in range(2):
                    i = g.tensor_reduce(out=q_st[:, u, 8 * half:8 * half + 8, 3, 4], in_=bank[2 + half][:, :].rearrange("p (h k) -> p h k", k=T),
                                        axis=AXL.X, op=ALU.max, negate=True)
                i.then_inc(s["c_max"], 1)

            def q_blocks(t, u):
                vec.wait_ge(s["c_q2_out"], t + 1)
                if not (isinstance(t, int) and t < 2):
                    vec.wait_ge(s["c_sT"], t - 1)
                blocks(t, u, qT2, q_bd, s["c_qbd"])

            def p_low(t, u):
                vec.wait_ge(s["c_ph"], t + 1)
                g.tensor_tensor(out=p1_s[:, u, 1], in0=p1[:, u], in1=p1_s[:, u, 0], op=ALU.subtract).then_inc(s["c_pl"], 1)

            def output1(t, u):
                vec.wait_ge(s["c_pv"], t + 1)
                pv = bank[6][:, 0:272].rearrange("p (a b e) -> p a b e", a=H1 // 2, b=TB)
                st.done(g.reciprocal(rden1[:, u], pv[:, :, :, 16]))
                st.wait()
                for hh in range(2):
                    for b in range(TB):
                        r = slice(64 * hh, 64 * hh + 64)
                        st.done(g.tensor_tensor(out=o1[64 * b:64 * b + 64, u].rearrange("p (a h e) -> p a h e", a=8, h=2)[:, :, hh, :],
                                                in0=pv[r, :, b, 8 * hh:8 * hh + 8],
                                                in1=rden1[r, u, :, b:b + 1].to_broadcast([64, 8, 8]), op=ALU.mult))
                st.wait()
                xr = x_res[:, bass.ds(t * D, D)]
                g.scalar_tensor_tensor(out=xr, in0=o1[:, u], scalar=tanh_g[:, 1:2], in1=xr, op0=ALU.mult, op1=ALU.add).then_inc(s["c_x3"], 1)

            k_blocks(0, 0)
            max1(0, 0)
            q_blocks(0, 0)
            n1 = st.base + st.n
            per1 = 5 + 1
            extra = [0]

            def before(t):
                return n1 + extra[0] + (per1 * t - per1 if not isinstance(t, int) or t else 0)

            def turn1(t, u):
                st.at(before(t))
                more = not isinstance(t, int) or t + 1 < NT
                if more:
                    k_blocks(t + 1, 1 - u)
                if not isinstance(t, int) or t:
                    output1(t - 1, 1 - u)
                if more:
                    max1(t + 1, 1 - u)
                if not isinstance(t, int) or t:
                    vec.wait_ge(s["c_x3"], t)
                    stats(t - 1, 0)
                p_low(t, u)
                if more:
                    q_blocks(t + 1, 1 - u)

            z_all = z[:, :, :].rearrange("p a b -> p (a b)")

            def piece(t, f, *args):
                def run():
                    st.at(before(t))
                    f(*args)
                    extra[0] += st.n
                return run

            def route_rows(r):
                first, n = ROUTED[r]
                if r:
                    vec.wait_ge(s["r_log"], r)
                mean_var(first, n, 0)
                rstd(0, first, n)
                normalize(0, first, n, z_all).then_inc(s["r_z"], 1)
                vec.wait_ge(s["r_z"], r + 1)
                zz = z_all[:, 0:n * D].rearrange("p (j d) -> p j d", d=D)
                hi, lo = (row_buf[r][:, 0, :, k * (D // 2):(k + 1) * (D // 2)].bitcast(FP16) for k in range(2))
                st.done(g.tensor_copy(hi, zz))
                st.wait()
                st.done(g.tensor_tensor(out=lo, in0=zz, in1=hi, op=ALU.subtract))
                st.wait()
                st.done(g.tensor_copy(row_buf[r][:, 1, :, 0:D], row_buf[r][:, 0, :, 0:D]))

            def prefix(src, spare, n):
                dst, other = spare
                cols = lambda x, lo, hi: x[:, :, lo:hi] if len(x.shape) == 3 else x[:, lo:hi]
                step = 1
                while step < n:
                    st.done(g.tensor_copy(cols(dst, 0, step), cols(src, 0, step)))
                    st.done(g.tensor_tensor(out=cols(dst, step, n), in0=cols(src, step, n), in1=cols(src, 0, n - step), op=ALU.add))
                    st.wait()
                    src, dst, other = dst, other, dst
                    step *= 2
                return src

            def route_gates(r):
                first, n = ROUTED[r]
                vec.wait_ge(s["r_log"], r + 1)
                lg, above, equal, run, run2, ex, gates_ = (rt[:, k, 0:ROUTED[r][1]] for k in range(7))
                st.done(g.tensor_copy(lg, bank[7][:, 0:n * E].rearrange("p (j e) -> p j e", e=E)))
                st.wait()
                for j in range(n):
                    st.done(g.max(top[:, j], lg[:, j]))
                st.wait()
                m1 = top[:, 0:n, 0:1].to_broadcast([128, n, E])
                m2 = top[:, 0:n, 1:2].to_broadcast([128, n, E])
                g.tensor_tensor(out=ex, in0=lg, in1=m1, op=ALU.subtract).then_inc(s["r_less"], 1)
                st.done(g.tensor_tensor(out=above, in0=lg, in1=m2, op=ALU.is_gt))
                st.done(g.tensor_tensor(out=equal, in0=lg, in1=m2, op=ALU.is_equal))
                st.wait()
                counted = prefix(equal, (run, run2), E)
                st.done(g.tensor_reduce(out=rs[:, 0, 0:n], in_=above, axis=AXL.X, op=ALU.add))
                st.wait()
                st.done(g.tensor_scalar(out=rs[:, 0, 0:n], in0=rs[:, 0, 0:n], scalar1=-1.0, scalar2=2.0, op0=ALU.mult, op1=ALU.add))
                st.wait()
                st.done(g.tensor_tensor(out=counted, in0=counted, in1=rs[:, 0, 0:n].unsqueeze(2).to_broadcast([128, n, E]), op=ALU.is_le))
                st.wait()
                st.done(g.tensor_tensor(out=equal, in0=equal, in1=counted, op=ALU.mult))
                st.wait()
                st.done(g.tensor_tensor(out=above, in0=above, in1=equal, op=ALU.add))
                st.wait()
                g.tensor_copy(picked[:, 0:n, :], above).then_inc(s["r_pick"], 1)

            def route_weights(r):
                above, ex, gates_ = (rt[:, k, 0:ROUTED[r][1]] for k in (1, 5, 6))
                n = ROUTED[r][1]
                vec.wait_ge(s["r_pick"], r + 1)
                vec.wait_ge(s["r_exp"], r + 1)
                st.done(g.tensor_tensor(out=ex, in0=ex, in1=above, op=ALU.mult))
                st.wait()
                st.done(g.tensor_reduce(out=rs[:, 1, 0:n], in_=ex, axis=AXL.X, op=ALU.add))
                st.wait()
                st.done(g.reciprocal(rs[:, 2, 0:n], rs[:, 1, 0:n]))
                st.wait()
                st.done(g.tensor_scalar(out=rs[:, 2, 0:n], in0=rs[:, 2, 0:n], scalar1=tanh_g[:, 3:4], scalar2=None, op0=ALU.mult))
                st.wait()
                st.done(g.tensor_tensor(out=gates_, in0=ex, in1=rs[:, 2, 0:n].unsqueeze(2).to_broadcast([128, n, E]), op=ALU.mult))

            def route_slots(r):
                at, n = ROUTED[r]
                vec.wait_ge(s["r_rank"], r + 1)
                above, gates_, pos, is_a, ga, gb = (rt[:, k, 0:ROUTED[r][1]] for k in (1, 6, 7, 8, 9, 10))
                rank = bank[7][:, 0:n * E].rearrange("p (j e) -> p j e", e=E)
                first, total = region[:, :], count[:, (r + 1) % 2]
                here = bank[7][:, RT * E:RT * E + E]
                if r:
                    first = per_e[:, 0]
                    st.done(g.tensor_tensor(out=first, in0=region[:, :], in1=count[:, r % 2], op=ALU.add))
                    st.done(g.tensor_tensor(out=total, in0=count[:, r % 2], in1=here, op=ALU.add))
                else:
                    st.done(g.tensor_copy(total, here))
                st.wait()
                st.done(g.tensor_tensor(out=pos, in0=rank, in1=first.unsqueeze(1).to_broadcast([128, n, E]), op=ALU.add))
                st.wait()
                st.done(g.tensor_tensor(out=pos, in0=pos, in1=above, op=ALU.mult))
                st.wait()
                st.done(g.tensor_reduce(out=rs[:, 3, 0:n], in_=pos, axis=AXL.X, op=ALU.max))
                st.done(g.tensor_reduce(out=rs[:, 4, 0:n], in_=pos, axis=AXL.X, op=ALU.add))
                st.wait()
                st.done(g.tensor_tensor(out=rs[:, 5, 0:n], in0=rs[:, 4, 0:n], in1=rs[:, 3, 0:n], op=ALU.subtract))
                st.done(g.tensor_tensor(out=is_a, in0=pos, in1=rs[:, 3, 0:n].unsqueeze(2).to_broadcast([128, n, E]), op=ALU.is_equal))
                st.wait()
                st.done(g.tensor_tensor(out=ga, in0=gates_, in1=is_a, op=ALU.mult))
                st.wait()
                st.done(g.tensor_tensor(out=gb, in0=gates_, in1=ga, op=ALU.subtract))
                st.wait()
                st.done(g.tensor_reduce(out=row_buf[r][:, 0, :, D + 1], in_=ga, axis=AXL.X, op=ALU.add))
                st.done(g.tensor_reduce(out=row_buf[r][:, 1, :, D + 1], in_=gb, axis=AXL.X, op=ALU.add))
                st.done(g.tensor_copy(row_buf[r][:, 0, :, D], tok_id[:, at:at + n]))
                st.done(g.tensor_scalar(out=row_buf[r][:, 1, :, D], in0=tok_id[:, at:at + n], scalar1=float(TOK), scalar2=None, op0=ALU.add))
                st.done(g.tensor_copy(slot_at[:, 0, at:at + n], rs[:, 3, 0:n]))
                g.tensor_copy(slot_at[:, 1, at:at + n], rs[:, 5, 0:n]).then_inc(s["r_slots"], 1)

            def tables():
                total = count[:, len(ROUTED) % 2]
                n_t, end, spare, start = (per_e[:, k] for k in (1, 2, 3, 4))
                st.wait()
                st.done(g.tensor_scalar(out=per_ei[:, 0], in0=total, scalar1=127.0, scalar2=None, op0=ALU.add))
                st.done(g.tensor_tensor(out=per_ei[:, 1], in0=total, in1=region[:, :], op=ALU.add))
                st.wait()
                st.done(g.tensor_scalar(out=per_ei[:, 0], in0=per_ei[:, 0], scalar1=7, scalar2=None, op0=ALU.logical_shift_right))
                st.wait()
                st.done(g.tensor_copy(n_t, per_ei[:, 0]))
                st.wait()
                end = prefix(n_t, (end, spare), E)
                at = lambda x: x.unsqueeze(1).to_broadcast([128, SLOTS, E])
                past, nts = big[:, 0], big[:, 1]
                st.done(g.tensor_tensor(out=past, in0=tile_no[:, :].unsqueeze(2).to_broadcast([128, SLOTS, E]), in1=at(end), op=ALU.is_ge))
                st.wait()
                st.done(g.tensor_tensor(out=nts, in0=past, in1=at(n_t), op=ALU.mult))
                first, row, gap = (tab[:, k] for k in range(3))
                expert = expert_pad[:, 0:SLOTS]
                st.done(g.memset(expert_pad[:, SLOTS:SLOTS + DIGITS], 0.0))
                st.done(g.tensor_reduce(out=expert, in_=past[:, :, 0:E - 1], axis=AXL.X, op=ALU.add))
                st.wait()
                st.done(g.tensor_reduce(out=first, in_=nts[:, :, 0:E - 1], axis=AXL.X, op=ALU.add))
                st.wait()
                st.done(g.tensor_tensor(out=row, in0=tile_no[:, :], in1=first, op=ALU.subtract))
                st.done(g.tensor_scalar(out=gap, in0=expert, scalar1=float(REG), scalar2=None, op0=ALU.mult))
                st.wait()
                st.done(g.scalar_tensor_tensor(out=row, in0=row, scalar=128.0, in1=gap, op0=ALU.mult, op1=ALU.add))
                st.wait()
                st.done(g.tensor_scalar(out=gap, in0=row, scalar1=-1.0, scalar2=float(NULL), op0=ALU.mult, op1=ALU.add))
                st.wait()
                st.done(g.tensor_tensor(out=gap, in0=gap, in1=past[:, :, E - 1], op=ALU.mult))
                st.wait()
                st.done(g.tensor_tensor(out=row, in0=row, in1=gap, op=ALU.add))
                st.done(g.scalar_tensor_tensor(out=null_off[:, :], in0=tile_no[:, :], scalar=128.0, in1=past[:, :, E - 1], op0=ALU.mult, op1=ALU.mult))
                st.wait()
                g.tensor_copy(tab_i[:, :], row).then_inc(s["r_tab"], 1)
                digit = lambda n: expert_pad[:, n:n + SLOTS].rearrange("p (i j) -> p i j", j=4)[:, :, 0]
                digits = gap[:, 0:SLOTS // 4]
                st.done(g.tensor_copy(digits, digit(DIGITS - 1)))
                for n in reversed(range(DIGITS - 1)):
                    st.wait()
                    st.done(g.scalar_tensor_tensor(out=digits, in0=digits, scalar=float(E), in1=digit(n), op0=ALU.mult, op1=ALU.add))
                st.wait()
                g.tensor_copy(experts_i[:, :], digits).then_inc(s["r_exps"], 1)

            vec.wait_ge(s["moe_consts"], 80)
            vec.wait_ge(s["pads_up"], 1)
            g.tensor_copy(pad_rows[:, :, D:D + 1], pad_at[:, :].unsqueeze(2)).then_inc(s["pads_up"], 1)
            turns_and_routes(vec, turn1, {7: piece(7, route_rows, 0), 9: piece(9, route_gates, 0), 10: piece(10, route_weights, 0),
                                          11: piece(11, route_slots, 0), 13: piece(13, route_rows, 1), 15: piece(15, route_gates, 1)})
            st.at(before(NT))
            route_weights(1)
            route_slots(1)
            output1(NT - 1, 1)
            vec.wait_ge(s["c_x3"], NT)
            stats(NT - 1, 0)
            route_rows(2)
            route_gates(2)
            route_weights(2)
            route_slots(2)
            tables()

            def rows_out(k, j):
                vec.wait_ge(s["e_turn"], k + 1)
                if after(k, 2):
                    vec.wait_ge(s["e_up"], k - 1)
                g.tensor_copy(rT[:, j % 2], bank[j % 2][:, 0:128].bitcast(FP16).rearrange("p (h k) -> p h k", h=2)).then_inc(s["e_xT"], 1)
                if after(k, 4):
                    vec.wait_ge(s["e_out"], k - 3)
                g.tensor_tensor(out=y_row[:, j:j + 1], in0=rows[:, j, D:D + 1], in1=null_off[:, bass.ds(k, 1)], op=ALU.add).then_inc(s["e_ex"], 1)

            def weigh(k, j):
                vec.wait_ge(s["e_ex"], k + 1)
                if after(k, 4):
                    vec.wait_ge(s[f"e_sent{j}"], 16 * (k // 4) if isinstance(k, int) else 4 * (k - j))
                g.tensor_copy(y_at[:, j:j + 1], y_row[:, j:j + 1])
                vec.wait_ge(s["e_y"], k + 1)
                vec.wait_ge(s["e_gate"], k + 1)
                g.tensor_scalar(out=y_out[:, j, :], in0=bank[4 + j % 2][:, 0:D], scalar1=y_gate[:, j:j + 1], scalar2=None, op0=ALU.mult)\
                 .then_inc(s["e_out"], 1)

            def expert_turn(k, j, _):
                if not isinstance(k, int) or k + 3 < SLOTS:
                    rows_out(k + 3, (j + 3) % 4)
                weigh(k, j)

            vec.wait_ge(s["r_tab"], 1)
            rows_out(0, 0)
            rows_out(1, 1)
            rows_out(2, 2)
            slots(vec, expert_turn)
            for gi in range(NG):
                vec.wait_ge(s[f"f_y{gi}"], 32)
                c = slice(gi * GT * D, (gi + 1) * GT * D)
                st.at(0)
                g.tensor_tensor(out=x_res[:, c], in0=x_res[:, c], in1=joint[:, c], op=ALU.add).then_inc(s["f_half"], 1)
                vec.wait_ge(s["f_half"], gi + 1)
                g.tensor_tensor(out=x_res[:, c], in0=x_res[:, c], in1=joint[:, NT * D + gi * GT * D:NT * D + (gi + 1) * GT * D],
                                op=ALU.add).then_inc(s["f_x"], 1)

        @block.tensor
        def _(pe):
            g = nc.tensor
            pe.wait_ge(s["ident_up"], 3)
            pe.wait_ge(s["weights_in"], 48)
            for p in range(NP):
                i = g.transpose(bank[6][:, p * D:(p + 1) * D], wkv_raw[:, INNER + p * 128:INNER + (p + 1) * 128], ident[:, :])
            i.then_inc(s["wv_turned"], 1)
            pe.wait_ge(s["wv_copied"], 1)
            for h in range(H0):
                r = slice(64 * (h % 2), 64 * (h % 2) + 64)
                i = g.matmul(bank[4 + h % 2][:, (h // 2) * D:(h // 2 + 1) * D], wvT[r, h // 2, :], wo_sb[r, h // 2, :], start=True, stop=True)
                if h >= H0 - 2:
                    i.then_inc(s["wvo_mm"], 1)
            pe.wait_ge(s["w_split"], 1)
            pe.wait_ge(s["q_zero"], 1)
            pe.wait_ge(s["select_up"], 1)

            def turn_x(t, u):
                pe.wait_ge(s["a_split"], t + 1)
                for hl in range(2):
                    for b in range(TB):
                        i = g.transpose(bank[2][:, 0:256].bitcast(FP16)[:, (hl * TB + b) * 128:(hl * TB + b + 1) * 128],
                                        x_s[:, u, hl, b, :], ident_h[:, :])
                i.then_inc(s["a_turn"], 1)

            def product(dst, w, x, cols):
                for n, (i, j) in enumerate(((0, 0), (0, 1), (1, 0))):
                    last = g.matmul(dst, w[:, i, cols], x[j], start=n == 0, stop=n == 2)
                return last

            def project_q(t, u):
                for p in range(NP):
                    i = product(bank[2][:, p * 128:(p + 1) * 128], wq_s, [xT[:, u, j, :, 64:128] for j in range(2)],
                                slice(p * 128, (p + 1) * 128))
                i.then_inc(s["a_projq"], 1)

            def project_k(t, u, ns):
                if ns[0] == 0:
                    pe.wait_ge(s["a_xT"], t + 1)
                if not (isinstance(t, int) and t == 0):
                    if ns[0] == 0:
                        pe.wait_ge(s["a_nmax"], TB * t)
                    elif not (isinstance(t, int) and t == 1):
                        pe.wait_ge(s["a_x1"], t - 1)
                for n in ns:
                    p, k = K_PAIRS[n]
                    cols = slice(p * 128, (p + 1) * 128)
                    product(bank[k][:, 0:256], wk_s, [xT[:, u, j].rearrange("p b k -> p (b k)") for j in range(2)], cols)
                    product(bank[k][:, 256:384], wkr_s, [xT[:, u, j, :, 0:64] for j in range(2)], cols).then_inc(s["a_proj"], 1)

            def scores(t, u):
                pe.wait_ge(s["a_q"], t + 1)
                pe.wait_ge(s["a_kb"], t + 1)
                pe.wait_ge(s["a_qk"], NP * (t + 1))
                for b in range(TB):
                    for p in range(NP):
                        i = g.matmul(bank[4 + b][:, p * 128:(p + 1) * 128], qT_b[:, u, p, b].rearrange("p h q -> p (h q)"),
                                     kT_b[:, u, p, b, :], start=True, stop=True)
                    i.then_inc(s["a_s"], 1)

            def turn_max(t, u):
                pe.wait_ge(s["a_nmax"], TB * (t + 1))
                g.transpose(bank[3][0:8, 64:128].bitcast(BF16), nmax[:, u].rearrange("p b a -> p (b a)"), ident_b[:, :]).then_inc(s["a_nturn"], 1)

            def scores_t(t, u):
                pe.wait_ge(s["a_nmaxT"], t + 1)
                pe.wait_ge(s["a_k"], t + 1)
                pe.wait_ge(s["a_q"], t + 1)
                pe.wait_ge(s["a_qk"], NP * (t + 1))
                if not (isinstance(t, int) and t == 0):
                    pe.wait_ge(s["a_axs"], TB * t)
                for b in range(TB):
                    for p in range(NP):
                        d = bank[6 + b][:, p * 128:(p + 1) * 128]
                        g.matmul(d, kT[:, u, p, b, :], qT[:, u, p, b].rearrange("p h q -> p (h q)"), start=True, stop=False)
                        i = g.matmul(d, select[:, b * NP + p, :], nmaxT[:, u, :], start=False, stop=True)
                    i.then_inc(s["a_sT"], 1)

            def attend(t, u):
                for b in range(TB):
                    pe.wait_ge(s["a_pl"], TB * t + b + 1)
                    for n, (i, j) in enumerate(((0, 0), (0, 1), (1, 0))):
                        last = g.matmul(bank[6 + b][:, :], x_s[:, u, i, b, :], prob_s[:, u, j, :, b, :], start=n == 0, stop=n == 2)
                    last.then_inc(s["a_ax"], 1)
                pe.wait_ge(s["a_nmaxT"], t + 1)
                for h in range(H0):
                    for hl in range(2):
                        i = g.matmul(bank[3][:, h:h + 1], prob_s[:, u, hl, h].rearrange("p b q -> p (b q)"), ones_h[:, :],
                                     start=hl == 0, stop=hl == 1)
                i.then_inc(s["a_den"], 1)

            def project_out(t, u, heads):
                if heads[0] == 0:
                    pe.wait_ge(s["a_axs"], TB * (t + 1))
                for h in heads:
                    i = g.matmul(bank[h // 4][:, (h % 4) * D:(h % 4 + 1) * D], ax[:, u, h].rearrange("p b q -> p (b q)"),
                                 wvo[:, h, :], start=True, stop=True)
                if h == H0 - 1:
                    i.then_inc(s["a_y"], 1)

            pe.wait_ge(s["wvo_up"], 2)
            turn_x(0, 0)
            project_k(0, 0, (0, 1))
            project_q(0, 0)
            project_k(0, 0, (2, 3))
            scores(0, 0)
            turn_max(0, 0)
            pe.wait_ge(s["a_q"], 1)
            turn_x(1, 1)

            def turn(t, u, more=2):
                v = 1 - u
                if more:
                    project_k(t + 1, v, (0, 1))
                scores_t(t, u)
                if more:
                    project_q(t + 1, v)
                    project_k(t + 1, v, (2, 3))
                attend(t, u)
                if more:
                    scores(t + 1, v)
                project_out(t, u, range(0, 6))
                if more:
                    pe.wait_ge(s["a_rden"], t + 1)
                    turn_max(t + 1, v)
                if more == 2:
                    pe.wait_ge(s["a_q"], t + 2)
                    turn_x(t + 2, u)
                project_out(t, u, range(6, H0))

            turn(0, 0)
            turn(1, 1)
            with pe.Fori(1, NT // 2 - 1) as i:
                turn(2 * i, 0)
                turn(2 * i + 1, 1)
            turn(NT - 2, 0, 1)
            turn(NT - 1, 1, 0)
            pe.wait_ge(s["ffn_in"], 80)
            pe.wait_ge(s["a_rden"], NT)
            for n in range(3):
                i = g.transpose(bank[3][:, n * D:(n + 1) * D], ffn_raw[:, n, :], ident[:, :])
            pe.wait_ge(s["moe_in"], 48)
            g.transpose(bank[3][:, 384:384 + E * FC], b1_raw[:, :], ident[0:E * FC, 0:E * FC])
            g.transpose(bank[3][:, 416:416 + E], rw_raw[:, :], ident[0:E, 0:E]).then_inc(s["ffn_turned"], 1)
            pe.wait_ge(s["ffn_wT_up"], 1)

            def z_turn(gi, u):
                pe.wait_ge(s["b_z"], gi + 1)
                if gi:
                    pe.wait_ge(s["b_zTs"], gi)
                for j in range(GT):
                    i = g.transpose(bank[2][:, j * D:(j + 1) * D], z[:, u, j * D:(j + 1) * D], ident[:, :])
                i.then_inc(s["b_zT"], 1)

            def keys_receptance(gi, u):
                pe.wait_ge(s["b_mix"], gi + 1)
                if gi:
                    pe.wait_ge(s["b_relu"], gi)
                    pe.wait_ge(s["b_tanh"], gi)
                g.matmul(bank[4][:, :], ffn_wT[:, 1, :], mixed[:, u, 1].rearrange("p b q -> p (b q)"), start=True, stop=True).then_inc(s["b_k"], 1)
                for j in range(GT):
                    i = g.matmul(bank[5][:, j * D:(j + 1) * D], mixed[:, u, 0].rearrange("p b q -> p (b q)")[:, j * D:(j + 1) * D],
                                 ffn_wT[:, 0, :], start=True, stop=True)
                i.then_inc(s["b_r"], 1)

            def values(gi, u):
                pe.wait_ge(s["b_sq"], gi + 1)
                if gi:
                    pe.wait_ge(s["b_x2"], gi)
                else:
                    pe.wait_ge(s["a_axs"], TB * NT)
                for j in range(GT):
                    i = g.matmul(bank[6][:, j * D:(j + 1) * D], act_k[:, u, j * D:(j + 1) * D], ffn_wT[:, 2, :], start=True, stop=True)
                i.then_inc(s["b_v"], 1)

            def weights_turn(k):
                if k >= 2:
                    pe.wait_ge(s["d_ws"], k - 1)
                    if k - 2 < E:
                        pe.wait_ge(s["d_wl"], k - 1)
                for c in range(FC):
                    src = w1_raw[:, FC * k + c, :] if k < E else w2_raw[:, k - E, c * 128:(c + 1) * 128]
                    i = g.transpose(bank[k % 2][:, c * 128:(c + 1) * 128], src, ident[:, :])
                i.then_inc(s["d_w"], 1)

            pe.wait_ge(s["moe_in2"], 32)
            pe.wait_ge(s["a_x1"], NT)
            z_turn(0, 0)
            for gi in range(NG):
                if gi + 1 < NG:
                    z_turn(gi + 1, (gi + 1) % 2)
                weights_turn(4 * gi)
                weights_turn(4 * gi + 1)
                keys_receptance(gi, gi % 2)
                weights_turn(4 * gi + 2)
                weights_turn(4 * gi + 3)
                values(gi, gi % 2)

            def turn_kq(t, u):
                pe.wait_ge(s["c_st"], t + 1)
                pe.wait_ge(s["c_q"], t + 1)
                if not (isinstance(t, int) and t == 0):
                    pe.wait_ge(s["c_q1_out"], t)
                pt = bank[0][:, :].bitcast(FP16)
                for a_, x in enumerate((k_st, q_st)):
                    for k in range(4):
                        i = g.transpose(pt[:, (4 * a_ + k) * 128:(4 * a_ + k + 1) * 128],
                                        x[:, u, 4 * k:4 * k + 4].rearrange("p h c e -> p (h c e)"), ident_h[:, :])
                i.then_inc(s["c_turn"], 1)

            def scores1(t, u):
                pe.wait_ge(s["c_kbd"], t + 1)
                pe.wait_ge(s["c_q1_out"], t + 1)
                if not (isinstance(t, int) and t == 0):
                    pe.wait_ge(s["c_max"], t)
                for b in range(TB):
                    for k in range(4):
                        i = g.matmul(bank[2 + k // 2][64 * b:64 * b + 64, (k % 2) * 256:(k % 2) * 256 + 256],
                                     qT1[:, u, k, 64 * b:64 * b + 64], k_bd[:, u, k, b].rearrange("p i k -> p (i k)"), start=True, stop=True)
                i.then_inc(s["c_s"], 1)

            def turn_q2(t, u):
                pe.wait_ge(s["c_max"], t + 1)
                if not (isinstance(t, int) and t == 0):
                    pe.wait_ge(s["c_q2_out"], t)
                for k in range(4):
                    i = g.transpose(bank[1][:, 0:256].bitcast(FP16)[:, k * 128:(k + 1) * 128],
                                    q_st[:, u, 4 * k:4 * k + 4].rearrange("p h c e -> p (h c e)"), ident_h[:, :])
                i.then_inc(s["c_turn2"], 1)

            def scores1_t(t, u):
                pe.wait_ge(s["c_qbd"], t + 1)
                if not (isinstance(t, int) and t == 0):
                    pe.wait_ge(s["c_exp"], t)
                for b in range(TB):
                    for k in range(4):
                        i = g.matmul(bank[4 + k // 2][64 * b:64 * b + 64, (k % 2) * 256:(k % 2) * 256 + 256],
                                     kT1[:, u, k, 64 * b:64 * b + 64], q_bd[:, u, k, b].rearrange("p i k -> p (i k)"), start=True, stop=True)
                i.then_inc(s["c_sT"], 1)

            def attend1(t, u):
                pe.wait_ge(s["c_pl"], t + 1)
                pe.wait_ge(s["c_v"], t + 1)
                if not (isinstance(t, int) and t == 0):
                    pe.wait_ge(s["c_x3"], t)
                for p in range(H1 // 2):
                    for n, (i, j) in enumerate(((0, 0), (0, 1), (1, 0))):
                        last = g.matmul(bank[6][:, p * 34:p * 34 + 34], p1_s[:, u, i, p * 128:(p + 1) * 128],
                                        v_bd[:, u, j, p].rearrange("p b e -> p (b e)"), start=n == 0, stop=n == 2)
                last.then_inc(s["c_pv"], 1)

            pe.wait_ge(s["b_x2"], NG)
            pe.wait_ge(s["d_ws"], 2 * E)
            turn_kq(0, 0)
            scores1(0, 0)
            turn_q2(0, 0)
            turn_kq(1, 1)
            scores1_t(0, 0)

            def turn1(t, u):
                more = not isinstance(t, int) or t + 1 < NT
                if more:
                    scores1(t + 1, 1 - u)
                if not isinstance(t, int) or t + 2 < NT:
                    turn_kq(t + 2, u)
                if more:
                    turn_q2(t + 1, 1 - u)
                attend1(t, u)
                if more:
                    scores1_t(t + 1, 1 - u)

            zT_chunks = [0]

            def route_logits(r):
                n = ROUTED[r][1]
                pe.wait_ge(s["r_z"], r + 1)
                if r:
                    pe.wait_ge(s["r_slots"], r)
                for at in range(0, n, 4):
                    if at:
                        pe.wait_ge(s["r_zTs"], zT_chunks[0])
                    for j in range(at, min(at + 4, n)):
                        i = g.transpose(bank[7][:, (j - at) * D:(j - at + 1) * D], z[:, :, :].rearrange("p a b -> p (a b)")[:, j * D:(j + 1) * D], ident[:, :])
                    i.then_inc(s["r_zT"], 1)
                    zT_chunks[0] += 1
                pe.wait_ge(s["r_zTs"], zT_chunks[0])
                for j in range(n):
                    i = g.matmul(bank[7][:, j * E:(j + 1) * E], zTr[:, j * D:(j + 1) * D], rwT[:, :], start=True, stop=True)
                i.then_inc(s["r_log"], 1)

            def route_ranks(r):
                n = ROUTED[r][1]
                pe.wait_ge(s["r_pick"], r + 1)
                flat = picked[:, 0:n, :].rearrange("p j e -> p (j e)")
                g.matmul(bank[7][:, 0:n * E], tri[:, :], flat, start=True, stop=False)
                for k in range(1, n):
                    g.matmul(bank[7][:, k * E:n * E], ones_sq[:, :], flat[:, 0:(n - k) * E], start=False, stop=k == n - 1)
                for j in range(n):
                    i = g.matmul(bank[7][:, RT * E:RT * E + E], ones_sq[:, :], picked[:, j, :], start=j == 0, stop=j == n - 1)
                i.then_inc(s["r_rank"], 1)

            turns_and_routes(pe, turn1, {8: lambda: route_logits(0), 10: lambda: route_ranks(0), 14: lambda: route_logits(1)})
            route_ranks(1)
            route_logits(2)
            route_ranks(2)

            def turn_rows(k, j):
                pe.wait_ge(s[f"e_row{j}"], 16 * (k // 4 + 1) if isinstance(k, int) else 4 * (k - j) + 16)
                if after(k, 2):
                    pe.wait_ge(s["e_xT"], k - 1)
                r16 = rows[:, j, 0:D].bitcast(FP16)
                for hl in range(2):
                    i = g.transpose(bank[j % 2][:, 0:128].bitcast(FP16)[:, hl * 128:(hl + 1) * 128], r16[:, hl * 128:(hl + 1) * 128], ident_h[:, :])
                i.then_inc(s["e_turn"], 1)

            def up(k, j, expert):
                pe.wait_ge(s["e_xT"], k + 1)
                if after(k, 4):
                    pe.wait_ge(s["e_hid"], k - 3)
                for c in range(FC):
                    for n, (a_, b_) in enumerate(((0, 0), (0, 1), (1, 0))):
                        i = g.matmul(bank[UP_BANKS[j]][:, c * 128:(c + 1) * 128], w1_s[:, a_, bass.ds(expert * F + c * 128, 128)],
                                     rT[:, j % 2, b_], start=n == 0, stop=n == 2)
                i.then_inc(s["e_up"], 1)

            def down(k, j, expert):
                pe.wait_ge(s["e_hid"], k + 1)
                if after(k, 2):
                    pe.wait_ge(s["e_out"], k - 1)
                dst = bank[4 + j % 2][:, 0:D]
                g.matmul(dst, ones_row[:, :], b2_row[:, bass.ds(expert * D, D)], start=True, stop=False)
                for c in range(FC):
                    i = g.matmul(dst, hid[:, j, c], w2T[:, bass.ds(expert * F + c * 128, 128)], start=False, stop=c == FC - 1)
                i.then_inc(s["e_y"], 1)

            pe.wait_ge(s["r_exps"], 1)
            pe.wait_ge(s["c_x3"], NT)
            turn_rows(0, 0)
            turn_rows(1, 1)
            digits = pe.value_load(experts_i[0:1, 0:1], min_val=0, max_val=E ** DIGITS - 1)
            first_two = [(digits // E ** n) % E for n in range(2)]
            up(0, 0, first_two[0])
            turn_rows(2, 2)
            up(1, 1, first_two[1])

            def expert_turn(k, j, expert):
                if not isinstance(k, int) or k + 3 < SLOTS:
                    turn_rows(k + 3, (j + 3) % 4)
                if not isinstance(k, int) or k + 2 < SLOTS:
                    up(k + 2, (j + 2) % 4, expert[j + 2])
                down(k, j, expert[j])

            slots(pe, expert_turn, experts_i, 2)


_INS = ["x", "ctx_1024", "g_xattn", "g_ffn", "L0_xattn_gamma_x", "L0_xattn_beta_x", "L0_xattn_gamma_l", "L0_xattn_beta_l",
        "L0_xattn_Wq", "L0_xattn_Wkv", "L0_xattn_Wo", "L0_ffn_W_r", "L0_ffn_W_k", "L0_ffn_W_v", "L0_ffn_mu_r", "L0_ffn_mu_k",
        "L1_ffn_router_w", "L1_ffn_w1", "L1_ffn_b1", "L1_ffn_w2", "L1_ffn_b2"]


def _constants():
    f32 = np.float32

    def angles(width):
        inv = (1.0 / f32(10000.0) ** (np.arange(0, width, 2, dtype=f32) / f32(width))).astype(f32)
        return (np.arange(T, dtype=f32)[:, None] * inv[None, :]).astype(f32)

    th = angles(HD0)
    cos, sin = np.cos(th).astype(f32).T, np.sin(th).astype(f32).T
    cos0 = np.ascontiguousarray(np.concatenate([cos, cos, cos, cos], 0))
    sin0 = np.ascontiguousarray(np.concatenate([-sin, sin, -sin, sin], 0))
    th = angles(HD1)
    cos, sin = np.cos(th).astype(f32), np.sin(th).astype(f32)
    cos1 = np.tile(np.concatenate([cos, cos], 1), (2, 1))
    sin1 = np.tile(np.concatenate([-sin, sin], 1), (2, 1))
    slope = np.array([2.0 ** (-8.0 * i / H1) for i in range(1, H1 + 1)]).astype(f32).astype(np.float64) * HD1 ** 0.5
    pos = np.tile(np.arange(T, dtype=np.float64), 2)
    q_ext, k_ext = np.zeros((128, H1, 8), np.float16), np.zeros((128, H1, 8), np.float16)
    shift = -slope[None, :] * pos[:, None]
    q_ext[:, :, 0] = slope
    q_ext[:, :, 1] = slope - slope.astype(np.float16)
    q_ext[:, :, 2] = shift
    q_ext[:, :, 3] = shift - shift.astype(np.float16)
    k_ext[:, :, 0] = k_ext[:, :, 1] = pos[:, None]
    k_ext[:, :, 2:5] = 1.0
    p = np.arange(128)
    tri = (p[:, None] < p[None, :]).astype(np.float16)
    tile_no = np.tile(np.arange(SLOTS, dtype=f32), (128, 1))
    region = np.tile(np.arange(E, dtype=f32) * REG, (128, 1))
    tok_id = (p[:, None] + 128 * np.arange(NT)[None, :]).astype(f32)
    pad_at = (2 * TOK + p[:, None] + 128 * np.arange(E + 1)[None, :]).astype(f32)
    return {"cos0": cos0, "sin0": sin0, "cos1": cos1, "sin1": sin1, "q_ext": q_ext, "k_ext": k_ext,
            "tri": tri, "tile_no": tile_no, "region": region, "tok_id": tok_id, "pad_at": pad_at}


def kernel(**inputs):
    import numpy as _np
    import concourse.bacc as _bacc
    from concourse import mybir as _mybir
    from concourse.bass_utils import run_bass_kernel_spmd as _run

    nc = _bacc.Bacc("TRN2", target_bir_lowering=False, num_devices=1)
    arrays, args = {}, {}
    held = {n: _np.ascontiguousarray(inputs[n]) for n in _INS}
    held.update(_constants())
    for name, v in held.items():
        arrays[f"in_{name}"] = v
        args[name] = nc.dram_tensor(f"in_{name}", v.shape, _mybir.dt.from_np(v.dtype), kind="ExternalInput").ap()
    out = nc.dram_tensor("out_0", (B, T, D), _mybir.dt.float32, kind="ExternalOutput").ap()
    program(nc, args, out)
    r = _run(nc, [arrays], core_ids=[0])
    return r.results[0]["out_0"]
```

```python
from contextlib import ExitStack

import numpy as np

import concourse.bass as bass
from concourse import mybir

FP32, FP16, BF16, I32 = mybir.dt.float32, mybir.dt.float16, mybir.dt.bfloat16, mybir.dt.int32
ALU, ACT, AXL = mybir.AluOpType, mybir.ActivationFunctionType, mybir.AxisListType

B, T, D = 32, 64, 128
TB = 2
NT = B // TB
EPS = 1e-5
H0, HD0 = 8, 64
NP = H0 // 2
INNER = H0 * HD0
H1, HD1 = 16, 8
E, F = 8, 512
FC = F // 128
REG = B * T + 128
NULL = E * REG
TOK = B * T
DIGITS = 6
SLOTS = 40
ROW = D + 2
ROUTED = ((0, 10), (10, 6))
RT = 10
ZT_CHUNKS = sum(-(-n // 4) for _, n in ROUTED)
Q_SHARE = 5
GT = 4
NG = NT // GT
K_PAIRS = ((2, 4), (3, 5), (0, 0), (1, 1))
W1_TURNS = ((0, 1, 2), (3, 4, 5), (6, 7), ())
UP_BANKS = (2, 3, 6, 7)
RSQRT_MAGIC = 0x5F3759DF


class Steps:

    def __init__(self, eng, sem):
        self.eng, self.sem, self.base, self.n = eng, sem, 0, 0

    def at(self, base):
        self.base, self.n = base, 0

    def done(self, instruction):
        self.n += 1
        return instruction.then_inc(self.sem, 1)

    def wait(self, but=0):
        self.eng.wait_ge(self.sem, self.base + self.n - but)


def rotate(g, st, src, tmp, dst, sin, cos):
    hs, ht, hd = (x.rearrange("p (h e) -> p h e", e=HD1) for x in (src, tmp, dst))
    n, half_d = hs.shape[1], HD1 // 2
    for half in range(2):
        o, i = slice(half_d * half, half_d * (half + 1)), slice(half_d * (1 - half), half_d * (2 - half))
        st.done(g.tensor_tensor(out=ht[:, :, o], in0=hs[:, :, i], in1=sin[:, o].unsqueeze(1).to_broadcast([128, n, half_d]), op=ALU.mult))
    st.wait()
    st.done(g.tensor_tensor(out=hd, in0=hs, in1=cos[:, :].unsqueeze(1).to_broadcast([128, n, HD1]), op=ALU.mult))
    st.wait()
    st.done(g.tensor_tensor(out=dst, in0=dst, in1=tmp, op=ALU.add))
    st.wait()


def slots(eng, body, table=None, ahead=0):
    def four(i, last=False):
        experts = None
        if table is not None:
            digits = eng.value_load(table[0:1, bass.ds(i, 1)], min_val=0, max_val=E ** DIGITS - 1)
            experts = [(digits // E ** n) % E for n in range(4 if last else 4 + ahead)]
        for j in range(4):
            body(4 * i + j, j, experts)

    four(0)
    with eng.Fori(1, SLOTS // 4 - 1) as i:
        four(i)
    four(SLOTS // 4 - 1, True)


def turns_and_routes(eng, turn, routes):
    turn(0, 0)
    if 1 in routes:
        routes[1]()
    turn(1, 1)
    if 2 in routes:
        routes[2]()
    with eng.Fori(1, 5) as i:
        turn(2 * i, 0)
        turn(2 * i + 1, 1)
    for t in range(10, NT):
        if t in routes:
            routes[t]()
        turn(t, t % 2)


def after(k, n):
    return not isinstance(k, int) or k >= n


def program(nc, a, out):
    ctx = ExitStack()
    with ctx:
        def sb(name, shape, dt=FP32):
            return ctx.enter_context(nc.sbuf_tensor(name, shape, dt))

        def sem(name):
            return ctx.enter_context(nc.semaphore(name))

        joint = sb("joint", [128, B * D])
        x_res = sb("x_res", [128, NT * D])
        gates = sb("gates", [128, 4])
        tanh_g = sb("tanh_g", [128, 4])
        ident = sb("ident", [128, 128])
        ident_h = sb("ident_h", [128, 128], FP16)
        ident_b = sb("ident_b", [128, 128], BF16)
        ones_f = sb("ones_f", [128, 1])
        warm = sb("warm", [128, 1])
        ones_h = sb("ones_h", [128, 1], FP16)
        stat4 = sb("stat4", [128, 2, NT, 6])
        mv4 = sb("mv4", [128, 2, NT, 2])
        nwt4 = sb("nwt4", [128, 2, 5, NT])
        mix_w = sb("mix_w", [128, 4])
        ffn_raw = sb("ffn_raw", [128, 3, D])
        ffn_wT = sb("ffn_wT", [128, 5, D])
        half_g = sb("half_g", [128, 1])
        z = sb("z", [128, 2, GT * D])
        own_row = sb("own_row", [128, TB], FP16)
        cos1 = sb("cos1", [128, 8])
        sin1 = sb("sin1", [128, 8])
        q_ext = sb("q_ext", [128, H1, 8], FP16)
        k_ext = sb("k_ext", [128, H1, 8], FP16)
        ctx_tok = sb("ctx_tok", [128, NT * D])
        half_w = NT // 2 * D
        zTr, z_all = joint[:, 0:RT * D].bitcast(FP16).rearrange("p (j h k) -> p j h k", j=RT, h=2), joint[:, 2 * half_w:2 * half_w + RT * D]
        k_f, k_tmp, q_f, q_tmp = (joint[:, k * half_w:(k + 1) * half_w] for k in range(4))
        w1_raw = sb("w1_raw", [128, E * FC, D])
        w2_raw = sb("w2_raw", [128, E, F])
        b1_raw = sb("b1_raw", [E * FC, 128])
        b1T = sb("b1T", [128, E * FC])
        b2_row = sb("b2_row", [1, E * D])
        ones_row = sb("ones_row", [1, 128], FP16)
        tri = sb("tri", [128, 128], FP16)
        ones_sq = sb("ones_sq", [128, 128], FP16)
        tile_no = sb("tile_no", [128, SLOTS])
        region = sb("region", [128, E])
        tok_id = sb("tok_id", [128, NT])
        pad_rows = sb("pad_rows", [128, E + 1, ROW])
        pad_at = sb("pad_at", [128, E + 1])
        rw_raw = sb("rw_raw", [E, D])
        rwT = sb("rwT", [128, E])
        rwT_s = sb("rwT_s", [128, 2, E], FP16)

        early = ExitStack()

        def sb0(name, shape, dt=FP32):
            return early.enter_context(nc.sbuf_tensor(name, shape, dt))

        gamma_j = sb0("gamma_j", [128, D])
        beta_j = sb0("beta_j", [128, D])
        wq_raw = sb0("wq_raw", [128, INNER])
        wkv_raw = sb0("wkv_raw", [128, 2 * INNER])
        wo_sb = sb0("wo_sb", [128, NP, D])
        select = sb0("select", [8, 8, 128], BF16)
        cos0 = sb0("cos0", [128, T])
        sin0 = sb0("sin0", [128, T])
        wq_s = sb0("wq_s", [128, 2, INNER], FP16)
        wk_s = sb0("wk_s", [128, 2, INNER], FP16)
        wkr_s = sb0("wkr_s", [128, 2, INNER], FP16)
        wvT = sb0("wvT", [128, NP, D])
        wvo = sb0("wvo", [128, H0, D])
        stat = sb0("stat", [128, B, 6])
        mv = sb0("mv", [128, B, 2])
        nwt = sb0("nwt", [128, 6, B])
        scale_j = sb0("scale_j", [128, B])
        bias_j = sb0("bias_j", [128, B])
        xn = sb0("xn", [128, 2, TB, D])
        x_s = sb0("x_s", [128, 2, 2, TB, D], FP16)
        xT = sb0("xT", [128, 2, 2, TB, 128], FP16)
        kT = sb0("kT", [128, 2, NP, TB, 128])
        kT_b = sb0("kT_b", [128, 2, NP, TB, 128], BF16)
        qT = sb0("qT", [128, 2, NP, TB, 2, T])
        qT_b = sb0("qT_b", [128, 2, NP, TB, 2, T], BF16)
        kcos = sb0("kcos", [128, 2, NP, TB, T])
        ksin = sb0("ksin", [128, 2, NP, TB, T])
        nmax = sb0("nmax", [128, 2, TB, NP], BF16)
        nmaxT = sb0("nmaxT", [8, 2, 128], BF16)
        prob = sb0("prob", [128, 2, H0, TB, T])
        prob_s = sb0("prob_s", [128, 2, 2, H0, TB, T], FP16)
        y_odd = sb0("y_odd", [128, D])
        rden = sb0("rden", [128, 2, H0])
        ax = sb0("ax", [128, 2, H0, TB, T])

        early.close()
        early = ExitStack()
        zT = sb0("zT", [128, 2, 2, GT * TB, T])
        act_k = sb0("act_k", [128, 2, GT * D])
        recept = sb0("recept", [128, 2, GT * D])
        k1_s = sb0("k1_s", [128, 2, NT * D], FP16)
        v1_s = sb0("v1_s", [128, 2, NT * D], FP16)
        q1_s = sb0("q1_s", [128, 2, NT * D], FP16)
        q_st = sb0("q_st", [128, 2, H1, 4, 8], FP16)
        k_st = sb0("k_st", [128, 2, H1, 4, 8], FP16)
        v_bd = sb0("v_bd", [128, 2, 2, H1 // 2, TB, 17], FP16)
        qT1 = sb0("qT1", [128, 2, 4, 128], FP16)
        kT1 = sb0("kT1", [128, 2, 4, 128], FP16)
        q_bd = sb0("q_bd", [128, 2, 4, TB, 4, T], FP16)
        k_bd = sb0("k_bd", [128, 2, 4, TB, 4, T], FP16)
        p1 = sb0("p1", [128, 2, H1 * T])
        p1_s = sb0("p1_s", [128, 2, 2, H1 * T], FP16)
        rden1 = sb0("rden1", [128, 2, H1 // 2, TB])
        o1 = sb0("o1", [128, 2, D])
        w1_s = sb0("w1_s", [128, 2, E * FC * 128], FP16)
        b2_s = sb0("b2_s", [1, 2, E * D], FP16)
        w2T = sb0("w2T", [128, E * FC * D])
        top = sb0("top", [128, RT, 8])
        rs = sb0("rs", [128, 8, RT])
        picked = sb0("picked", [128, RT, E], FP16)
        slot_at = sb0("slot_at", [128, 2, NT], I32)
        count = sb0("count", [128, 2, E])
        per_e = sb0("per_e", [128, 6, E])
        per_ei = sb0("per_ei", [128, 2, E], I32)
        expert_pad = sb0("expert_pad", [128, SLOTS + DIGITS])
        tab_i = sb0("tab_i", [128, SLOTS], I32)
        experts_i = sb0("experts_i", [128, SLOTS // 4], I32)
        null_off = sb0("null_off", [128, SLOTS])
        y_row = sb0("y_row", [128, 4])
        y_at = sb0("y_at", [128, 4], I32)
        y_gate = sb0("y_gate", [128, 4])
        early.close()

        spent = [0, 0]

        def over(k, *shape):
            n = int(np.prod(shape))
            at = spent[k]
            spent[k] += n
            assert spent[k] <= E * FC * D
            axes = "abc"[:len(shape)]
            flat = (w1_raw, w2_raw)[k][:, :, :].rearrange("p a b -> p (a b)")[:, at:at + n]
            return flat.rearrange("p (" + " ".join(axes) + ") -> p " + " ".join(axes), **dict(zip(axes[1:], shape[1:])))

        row_buf = [over(0, 2, ROUTED[0][1], ROW),
                   p1[:, :, :].rearrange("p u c -> p (u c)")[:, 0:2 * ROUTED[1][1] * ROW].rearrange("p (c n w) -> p c n w", c=2, w=ROW)]
        rt = ctx_tok[:, 0:14 * RT * E].rearrange("p (k n e) -> p k n e", k=14, e=E)
        big = over(0, 2, SLOTS, E)
        tab = over(0, 3, SLOTS)
        rows = over(1, 4, ROW)
        hid = w1_raw[:, 0:16, :].rearrange("p (j c) f -> p j c f", c=FC)
        y_out = over(1, 4, D)
        rT = over(1, 2 * 128).bitcast(FP16).rearrange("p (j h k) -> p j h k", j=2, h=2)

        rows_d = nc.dram_tensor("rows_by_expert", (NULL + 128, ROW), FP32, kind="Internal").ap()
        y_d = nc.dram_tensor("results", (2 * TOK + (E + 1) * 128 + SLOTS * 128, D), FP32, kind="Internal").ap()

        bank = [ctx.enter_context(nc.psum_tensor(f"bank{i}", [128, 512], FP32)) for i in range(8)]

        s = {}
        for name in (
            "consts_in weights_in x_in0 x_in1 x_in2 x_in3 x_res_in out_done ident_up select_up vec_step pool_step q_zero tanh_ready "
            "w_split wv_turned wv_copied wvo_mm wvo_up "
            "a_norm a_split a_turn a_xT a_proj a_projq a_q a_qk a_rope a_k a_kb a_s a_nmax a_nturn a_nmaxT "
            "a_sT a_exp a_ph a_pl a_den a_rden a_ax a_axs a_y a_x1 "
            "ffn_in ffn_turned ffn_wT_up mix_up b_ln b_z b_zT b_zTs b_k b_r b_tanh b_relu b_sq b_v b_x2 "
            "c_consts kv_in c_vh c_kv c_own c_ext c_zero c_zero_q c_rstd c_ln c_qs c_qs_g c_q c_st c_v c_turn c_k_out c_q1_out c_kbd c_s c_max c_turn2 c_qbd c_sT "
            "c_exp c_ph c_pl c_pv c_x3 "
            "moe_in moe_in2 small_up d_w d_wl d_ws moe_consts pads_up "
            "r_rstd r_z r_high r_low r_zT r_zTs r_log r_less r_exp r_pick r_rank r_slots r_sent r_tab r_exps r_pad "
            "e_row0 e_row1 e_row2 e_row3 e_turn e_xT e_ex e_gate e_up e_hid e_y e_out e_sent0 e_sent1 e_sent2 e_sent3 "
            "f_first0 f_first1 f_first2 f_first3 f_second0 f_second1 f_second2 f_second3 f_half f_x"
        ).split():
            s[name] = sem(name)

        block = ctx.enter_context(nc.Block())

        @block.sync
        def _(sp):
            ctx_rows = a["ctx_1024"].rearrange("b t d -> t b d")
            x_rows = a["x"].rearrange("b t d -> t b d")
            jt = joint[:, :].rearrange("p (b d) -> p b d", d=D)

            def joint_in(c):
                bs = slice(c * B // 4, (c + 1) * B // 4)
                sp.dma_start(jt[0:64, bs, :], ctx_rows[:, bs, :]).then_inc(s[f"x_in{c}"], 16)
                sp.dma_start(jt[64:128, bs, :], x_rows[:, bs, :]).then_inc(s[f"x_in{c}"], 16)

            joint_in(0)
            for t, dst in ((a["L0_xattn_gamma_x"], gamma_j[0:64, :]), (a["L0_xattn_gamma_l"], gamma_j[64:128, :]),
                           (a["L0_xattn_beta_x"], beta_j[0:64, :]), (a["L0_xattn_beta_l"], beta_j[64:128, :])):
                sp.dma_start(dst, t.partition_broadcast(64)).then_inc(s["consts_in"], 16)
            sp.dma_start(cos0[:, :], a["cos0"]).then_inc(s["consts_in"], 16)
            sp.dma_start(sin0[:, :], a["sin0"]).then_inc(s["consts_in"], 16)
            sp.dma_start(gates[:, 0:2], a["g_xattn"].partition_broadcast(128)).then_inc(s["consts_in"], 16)
            sp.dma_start(gates[:, 2:4], a["g_ffn"].partition_broadcast(128)).then_inc(s["consts_in"], 16)
            for c in range(1, 4):
                joint_in(c)
            tok = a["x"].rearrange("(n b) t d -> (b t) n d", b=TB)
            sp.dma_start(x_res[:, :].rearrange("p (n d) -> p n d", d=D), tok).then_inc(s["x_res_in"], 16)
            for n, name in enumerate(("L0_ffn_W_r", "L0_ffn_W_k", "L0_ffn_W_v")):
                sp.dma_start(ffn_raw[:, n, :], a[name]).then_inc(s["ffn_in"], 16)
            for n, name in enumerate(("L0_ffn_mu_r", "L0_ffn_mu_k")):
                sp.dma_start(mix_w[:, n:n + 1], a[name].rearrange("(d a) -> d a", a=1)).then_inc(s["ffn_in"], 16)
            for t, dst in (("cos1", cos1[:, :]), ("sin1", sin1[:, :]), ("q_ext", q_ext[:, :, :]), ("k_ext", k_ext[:, :, :])):
                sp.dma_start(dst, a[t]).then_inc(s["c_consts"], 16)
            sp.dma_start(ctx_tok[:, :].rearrange("p (n d) -> p n d", d=D),
                         a["ctx_1024"].rearrange("(n b) t d -> (b t) n d", b=TB)).then_inc(s["kv_in"], 16)
            sp.dma_start(b1_raw[:, :], a["L1_ffn_b1"].rearrange("e (c f) -> (e c) f", f=128)).then_inc(s["moe_in"], 16)
            sp.dma_start(b2_row[:, :], a["L1_ffn_b2"].rearrange("(a e) d -> a (e d)", a=1)).then_inc(s["moe_in"], 16)
            sp.dma_start(rw_raw[:, :], a["L1_ffn_router_w"]).then_inc(s["moe_in"], 16)
            sp.dma_start(w1_raw[:, :, :], a["L1_ffn_w1"].rearrange("e (c f) h -> f (e c) h", f=128)).then_inc(s["moe_in2"], 16)
            sp.dma_start(w2_raw[:, :, :], a["L1_ffn_w2"].rearrange("e h f -> h e f")).then_inc(s["moe_in2"], 16)
            for t, dst in (("tri", tri[:, :]), ("tile_no", tile_no[:, :]), ("region", region[:, :]), ("tok_id", tok_id[:, :]),
                           ("pad_at", pad_at[:, :])):
                sp.dma_start(dst, a[t]).then_inc(s["moe_consts"], 16)
            sp.wait_ge(s["pads_up"], 2)
            sp.dma_start(rows_d[NULL:NULL + 128, :], pad_rows[:, E, :]).then_inc(s["r_pad"], 16)
            sp.wait_ge(s["r_tab"], 1)
            for e in range(E):
                at = sp.value_load(per_ei[0:1, 1, e:e + 1], min_val=0, max_val=NULL - 128)
                sp.dma_start(rows_d[bass.ds(at, 128), :], pad_rows[:, e, :]).then_inc(s["r_pad"], 16)

            def load_rows(k, j, _):
                at = sp.value_load(tab_i[0:1, bass.ds(k, 1)], min_val=0, max_val=NULL)
                if isinstance(k, int) and k == 0:
                    sp.wait_ge(s["d_w"], 2 * E)
                    sp.wait_ge(s["r_pad"], (E + 1) * 16)
                    sp.wait_ge(s["r_sent"], 2 * NT * 16)
                if after(k, 4):
                    sp.wait_ge(s["e_turn"], k - 3)
                    sp.wait_ge(s["e_ex"], k - 3)
                    sp.wait_ge(s["e_gate"], k - 3)
                sp.dma_start(rows[:, j, :], rows_d[bass.ds(at, 128), :]).then_inc(s[f"e_row{j}"], 16)

            slots(sp, load_rows)
            for j in range(4):
                sp.wait_ge(s[f"e_sent{j}"], SLOTS // 4 * 16)
            yv = y_d[0:2 * TOK, :].rearrange("(c n p) d -> p c n d", p=128, n=NT)
            for gi in range(NG):
                for c in range(2):
                    sp.dma_start(joint[:, c * NT * D + gi * GT * D:c * NT * D + (gi + 1) * GT * D].rearrange("p (n d) -> p n d", d=D),
                                 yv[:, c, gi * GT:(gi + 1) * GT, :]).then_inc(s[f"f_{('first', 'second')[c]}{gi}"], 16)
            ov = out.rearrange("(n b) t d -> (b t) n d", b=TB)
            for gi in range(NG):
                sp.wait_ge(s["f_x"], gi + 1)
                sp.dma_start(ov[:, gi * GT:(gi + 1) * GT, :],
                             x_res[:, gi * GT * D:(gi + 1) * GT * D].rearrange("p (n d) -> p n d", d=D)).then_inc(s["out_done"], 16)
            sp.wait_ge(s["out_done"], NG * 16)

        @block.gpsimd
        def _(pool):
            g = nc.gpsimd
            st = Steps(pool, s["pool_step"])
            st.done(g.memset(ident[:, :], 0.0))
            st.done(g.memset(qT[:, :, :, :, :, :], 0.0))
            st.done(g.memset(qT_b[:, :, :, :, :, :], 0.0))
            st.done(g.memset(ones_f[:, :], 1.0))
            st.done(g.memset(ones_row[:, :], 1.0))
            st.done(g.memset(ones_sq[:, :], 1.0))
            g.memset(pad_rows[:, :, :], 0.0).then_inc(s["pads_up"], 1)
            g.memset(ones_h[:, :], 1.0).then_inc(s["q_zero"], 1)
            st.wait()
            g.affine_select(out=ident[:, :], in_=ident[:, :], compare_op=ALU.not_equal, fill=1.0,
                            base=0, pattern=[[-1, 128]], channel_multiplier=1).then_inc(s["ident_up"], 1)
            pool.wait_ge(s["ident_up"], 1)
            g.tensor_copy(ident_h[:, :], ident[:, :]).then_inc(s["ident_up"], 1)
            g.tensor_copy(ident_b[:, :], ident[:, :]).then_inc(s["ident_up"], 1)
            for r in range(8):
                i = g.tensor_copy(select[:, r, :], ident[0:8, r:r + 1].to_broadcast([8, 128]))
            i.then_inc(s["select_up"], 1)
            pool.wait_ge(s["consts_in"], 8 * 16)

            def cast(dst, src, shape):
                one = ones_f[:, :]
                for _ in range(len(shape) - 2):
                    one = one.unsqueeze(1)
                return g.tensor_tensor(out=dst, in0=src, in1=one.to_broadcast(shape), op=ALU.mult)

            def affine(t, u):
                pool.wait_ge(s["a_norm"], t + 1)
                x = xn[:, u, :, :]
                st.done(g.tensor_tensor(out=x, in0=x, in1=gamma_j[:, :].unsqueeze(1).to_broadcast([128, TB, D]), op=ALU.mult))
                st.wait()
                st.done(g.tensor_tensor(out=x, in0=x, in1=beta_j[:, :].unsqueeze(1).to_broadcast([128, TB, D]), op=ALU.add))

            def split(t, u):
                st.wait()
                st.done(cast(x_s[:, u, 0], xn[:, u, :, :], [128, TB, D]))
                st.wait()
                g.tensor_tensor(out=x_s[:, u, 1], in0=xn[:, u, :, :], in1=x_s[:, u, 0], op=ALU.subtract).then_inc(s["a_split"], 1)

            def prob_high(t, u):
                for b in range(TB):
                    pool.wait_ge(s["a_exp"], TB * t + b + 1)
                    cast(prob_s[:, u, 0, :, b, :], prob[:, u, :, b, :], [128, H0, T]).then_inc(s["a_ph"], 1)

            n0 = st.n
            per = 3
            for t in range(2):
                affine(t, t)
                split(t, t)

            def turn(t, u, more=True):
                st.at(n0 + 2 * per + per * t)
                if more:
                    affine(t + 2, u)
                if not (isinstance(t, int) and t < 2):
                    pool.wait_ge(s["a_den"], t - 1)
                prob_high(t, u)
                if more:
                    pool.wait_ge(s["a_ax"], TB * (t + 1))
                    split(t + 2, u)

            turn(0, 0)
            turn(1, 1)
            with pool.Fori(1, NT // 2 - 1) as i:
                turn(2 * i, 0)
                turn(2 * i + 1, 1)
            turn(NT - 2, 0, False)
            turn(NT - 1, 1, False)
            st.at(n0 + 2 * per + per * (NT - 2))
            pool.wait_ge(s["a_x1"], NT)
            pool.wait_ge(s["c_consts"], 64)
            g.memset(v_bd[:, :, :, :, :, :], 0.0).then_inc(s["c_zero"], 1)
            g.memset(k_bd[:, :, :, :, :, :], 0.0).then_inc(s["c_zero"], 1)
            for u in range(2):
                g.tensor_copy(q_st[:, u, :, 3, :], q_ext[:, :, :])
                i = g.tensor_copy(k_st[:, u, :, 3, :], k_ext[:, :, :])
            i.then_inc(s["c_ext"], 1)
            pool.wait_ge(s["kv_in"], 16)
            for half in range(2):
                c = slice(half * half_w, (half + 1) * half_w)
                rotate(g, st, ctx_tok[:, c], k_tmp, k_f, sin1, cos1)
                st.done(cast(k1_s[:, 0, c], k_f, [128, half_w]))
                st.wait()
                st.done(g.tensor_tensor(out=k1_s[:, 1, c], in0=k_f, in1=k1_s[:, 0, c], op=ALU.subtract))
                st.wait()
            pool.wait_ge(s["c_kv"], 1)
            pool.wait_ge(s["c_own"], 1)
            pool.wait_ge(s["c_ext"], 1)

            def heads_of(x, t, j):
                return x[:, j, bass.ds(t * D, D)].rearrange("p (h e) -> p h e", e=8)

            def stack_k(t, u):
                if not (isinstance(t, int) and t < 2):
                    pool.wait_ge(s["c_turn"], t - 1)
                for n, j in enumerate((0, 0, 1)):
                    i = cast(k_st[:, u, :, n, :], heads_of(k1_s, t, j), [128, H1, 8])
                i.then_inc(s["c_st"], 1)

            def stack_q(t, u):
                if not (isinstance(t, int) and t < 2):
                    pool.wait_ge(s["c_turn2"], t - 1)
                for n, j in enumerate((0, 1, 0)):
                    cast(q_st[:, u, :, n, :], heads_of(q1_s, t, j), [128, H1, 8])
                g.memset(q_st[:, u, :, 3, 4:5], 0.0).then_inc(s["c_q"], 1)

            def blocks_v(t, u):
                if not (isinstance(t, int) and t < 2):
                    pool.wait_ge(s["c_pv"], t - 1)
                for b in range(TB):
                    own = own_row[:, b:b + 1].unsqueeze(1).to_broadcast([128, H1 // 2, 16])
                    for j in range(2):
                        i = g.tensor_tensor(out=v_bd[:, u, j, :, b, 0:16], in0=v1_s[:, j, bass.ds(t * D, D)].rearrange("p (h e) -> p h e", e=16),
                                            in1=own, op=ALU.mult)
                i.then_inc(s["c_v"], 1)

            stack_k(0, 0)
            stack_k(1, 1)
            blocks_v(0, 0)
            pool.wait_ge(s["c_ln"], 1)
            c = slice(Q_SHARE * D, half_w)
            rotate(g, st, q_f[:, c], q_tmp[:, c], q_f[:, c], sin1, cos1)
            st.done(cast(q1_s[:, 0, c], q_f[:, c], [128, half_w - Q_SHARE * D]))
            st.wait()
            g.tensor_tensor(out=q1_s[:, 1, c], in0=q_f[:, c], in1=q1_s[:, 0, c], op=ALU.subtract).then_inc(s["c_qs_g"], 1)
            pool.wait_ge(s["c_qs_g"], 1)
            pool.wait_ge(s["c_qs"], 1)
            stack_q(0, 0)
            stack_q(1, 1)
            stack_k(2, 0)
            stack_q(2, 0)

            def turn1(t, u):
                if not isinstance(t, int) or t + 3 < NT:
                    stack_k(t + 3, 1 - u)
                if not isinstance(t, int) or t + 1 < NT:
                    blocks_v(t + 1, 1 - u)
                if not isinstance(t, int) or t + 3 < NT:
                    stack_q(t + 3, 1 - u)

            def send_rows(r):
                pool.wait_ge(s["r_slots"], r + 1)
                for j in range(ROUTED[r][1]):
                    for c in range(2):
                        g.indirect_dma_start(rows_d, bass.IndirectOffsetOnAxis(ap=slot_at[:, c, ROUTED[r][0] + j:ROUTED[r][0] + j + 1], axis=0),
                                             row_buf[r][:, c, j, :], None).then_inc(s["r_sent"], 16)

            turn1(0, 0)
            turn1(1, 1)
            pool.wait_ge(s["c_qs"], 2)
            with pool.Fori(1, 6) as i:
                turn1(2 * i, 0)
                turn1(2 * i + 1, 1)
            for t in range(12, NT - 1):
                turn1(t, t % 2)
            send_rows(0)
            send_rows(1)

            def weight_out(k, j):
                g.tensor_tensor(out=y_gate[:, j:j + 1], in0=rows[:, j, D + 1:D + 2], in1=ones_f[:, :], op=ALU.mult).then_inc(s["e_gate"], 1)

            def send(k, j, _):
                pool.wait_ge(s["e_out"], k + 1)
                if not isinstance(k, int) or k + 2 < SLOTS:
                    weight_out(k + 2, (j + 2) % 4)
                g.indirect_dma_start(y_d, bass.IndirectOffsetOnAxis(ap=y_at[:, j:j + 1], axis=0), y_out[:, j, :], None)\
                 .then_inc(s[f"e_sent{j}"], 16)

            for j in range(2):
                pool.wait_ge(s["e_turn"], j + 1)
                weight_out(j, j)
            slots(pool, send)

        @block.scalar
        def _(act):
            g = nc.scalar
            act.dma_start(wq_raw[:, :], a["L0_xattn_Wq"]).then_inc(s["weights_in"], 16)
            act.dma_start(wkv_raw[:, :], a["L0_xattn_Wkv"]).then_inc(s["weights_in"], 16)
            act.dma_start(wo_sb[:, :, :], a["L0_xattn_Wo"].rearrange("(p r) n -> r p n", r=128)).then_inc(s["weights_in"], 16)
            act.wait_ge(s["consts_in"], 8 * 16)
            g.activation(tanh_g[:, :], gates[:, :], ACT.Tanh).then_inc(s["tanh_ready"], 1)
            act.wait_ge(s["wv_turned"], 1)
            g.activation(wvT[:, :, :], bank[6][:, :].rearrange("p (a d) -> p a d", d=D), ACT.Copy).then_inc(s["wv_copied"], 1)
            for half in range(2):
                act.wait_ge(s["wvo_mm"], half + 1)
                g.activation(wvo[:, half:H0:2, :], bank[4 + half][:, :].rearrange("p (a d) -> p a d", d=D),
                             ACT.Copy).then_inc(s["wvo_up"], 1)
            act.wait_ge(s["q_zero"], 1)

            def x_turned(t, u):
                act.wait_ge(s["a_turn"], t + 1)
                g.activation(xT[:, u], bank[2][:, 0:256].bitcast(FP16).rearrange("p (h b k) -> p h b k", h=2, b=TB),
                             ACT.Copy).then_inc(s["a_xT"], 1)

            def queries_out(t, u):
                act.wait_ge(s["a_projq"], t + 1)
                qq = bank[2][:, :].rearrange("p (a b q) -> p a b q", a=NP, b=TB)
                for h in range(2):
                    r = slice(64 * h, 64 * h + 64)
                    g.activation(qT[r, u, :, :, h, :], qq[r], ACT.Copy)
                    i = g.activation(qT_b[r, u, :, :, h, :], qq[r], ACT.Copy)
                i.then_inc(s["a_q"], 1)

            def latent_keys_out(t, u, ns):
                for n in ns:
                    p, k = K_PAIRS[n]
                    act.wait_ge(s["a_rope"], NP * t + n + 1)
                    kk = bank[k][:, 0:256].rearrange("p (b k) -> p b k", b=TB)
                    g.activation(kT[:, u, p, :, 64:128], kk[:, :, 64:128], ACT.Copy)
                    g.activation(kT_b[:, u, p, :, 64:128], kk[:, :, 64:128], ACT.Copy).then_inc(s["a_qk"], 1)

            def exps(t, u, b):
                act.wait_ge(s["a_sT"], TB * t + b + 1)
                g.activation(prob[:, u, :, b, :], bank[6 + b][:, :].rearrange("p (h q) -> p h q", h=H0), ACT.Exp,
                             scale=HD0 ** -0.5).then_inc(s["a_exp"], 1)

            def ax_out(t, u):
                for b in range(TB):
                    act.wait_ge(s["a_ax"], TB * t + b + 1)
                    g.activation(ax[:, u, :, b, :], bank[6 + b][:, :].rearrange("p (h q) -> p h q", h=H0), ACT.Copy).then_inc(s["a_axs"], 1)

            def nmax_out(t, u):
                act.wait_ge(s["a_nturn"], t + 1)
                g.activation(nmaxT[:, u, :], bank[3][0:8, 64:128].bitcast(BF16), ACT.Copy).then_inc(s["a_nmaxT"], 1)

            x_turned(0, 0)
            latent_keys_out(0, 0, (0, 1))
            queries_out(0, 0)
            latent_keys_out(0, 0, (2, 3))
            nmax_out(0, 0)
            x_turned(1, 1)

            def turn(t, u, more=2):
                if not (isinstance(t, int) and t < 2):
                    act.wait_ge(s["a_ph"], TB * (t - 1))
                    act.wait_ge(s["a_pl"], TB * (t - 1))
                exps(t, u, 0)
                if more:
                    if not (isinstance(t, int) and t < 1):
                        act.wait_ge(s["a_sT"], TB * t)
                        act.wait_ge(s["a_s"], TB * t)
                    latent_keys_out(t + 1, 1 - u, (0, 1))
                exps(t, u, 1)
                if more:
                    queries_out(t + 1, 1 - u)
                    latent_keys_out(t + 1, 1 - u, (2, 3))
                if not (isinstance(t, int) and t < 2):
                    act.wait_ge(s["a_y"], t - 1)
                ax_out(t, u)
                if more:
                    nmax_out(t + 1, 1 - u)
                if more == 2:
                    x_turned(t + 2, u)

            turn(0, 0)
            turn(1, 1)
            with act.Fori(1, NT // 2 - 1) as i:
                turn(2 * i, 0)
                turn(2 * i + 1, 1)
            turn(NT - 2, 0, 1)
            turn(NT - 1, 1, 0)
            def normalize(k, first, count, dst):
                for j in range(count):
                    t = first + j
                    i = g.activation(dst[:, j * D:(j + 1) * D], x_res[:, t * D:(t + 1) * D], ACT.Identity,
                                     scale=nwt4[:, k, 1, t:t + 1], bias=nwt4[:, k, 0, t:t + 1])
                return i

            def ffn_head(gi):
                act.wait_ge(s["b_ln"], 1 + gi // (NG - 1))
                if gi >= 2:
                    act.wait_ge(s["b_zT"], gi - 1)
                normalize(0, GT * gi, GT, z[:, gi % 2]).then_inc(s["b_z"], 1)

            ffn_head(0)
            ffn_head(1)
            act.wait_ge(s["ffn_turned"], 1)
            act.wait_ge(s["b_ln"], 1)
            for n in range(4):
                g.activation(ffn_wT[:, n, :], bank[3][:, (n % 2) * D:(n % 2 + 1) * D], ACT.Copy, scale=mix_w[:, n:n + 1])
            g.activation(ffn_wT[:, 4, :], bank[3][:, 2 * D:3 * D], ACT.Copy)
            g.activation(b1T[:, :], bank[3][:, 384:384 + E * FC], ACT.Copy)
            g.activation(rwT_s[:, 0], bank[3][:, 416:416 + E], ACT.Copy)
            g.activation(rwT[:, :], bank[3][:, 416:416 + E], ACT.Copy).then_inc(s["ffn_wT_up"], 1)

            def z_out(gi, u):
                act.wait_ge(s["b_zT"], gi + 1)
                if gi >= 2:
                    act.wait_ge(s["b_r"], gi - 1)
                zz = bank[2][:, :].rearrange("p (b q) -> p b q", q=T)
                g.activation(zT[:, u, 0], zz, ACT.Copy)
                g.activation(zT[:, u, 1, :, 1:T], zz[:, :, 0:T - 1], ACT.Copy).then_inc(s["b_zTs"], 1)

            def weights_out(k):
                act.wait_ge(s["d_w"], k + 1)
                dst = w1_s[:, 0, :] if k < E else w2T[:, :]
                g.activation(dst[:, F * (k % E):F * (k % E + 1)], bank[k % 2][:, :], ACT.Copy).then_inc(s["d_ws"], 1)

            def queries_norm():
                act.wait_ge(s["c_rstd"], 2)
                act.wait_ge(s["c_qs"], 1)
                act.wait_ge(s["c_qs_g"], 1)
                normalize(1, NT // 2, NT // 2, q_f).then_inc(s["c_ln"], 1)

            act.wait_ge(s["mix_up"], 1)
            z_out(0, 0)
            act.wait_ge(s["kv_in"], 16)
            g.activation(v1_s[:, 0], ctx_tok[:, :], ACT.Copy).then_inc(s["c_vh"], 1)
            for gi in range(NG):
                u = gi % 2
                if gi + 1 < NG:
                    z_out(gi + 1, 1 - u)
                if gi + 2 < NG:
                    ffn_head(gi + 2)
                for k in W1_TURNS[gi][:1]:
                    weights_out(k)
                act.wait_ge(s["b_k"], gi + 1)
                if gi >= 2:
                    act.wait_ge(s["b_v"], gi - 1)
                g.activation(act_k[:, u], bank[4][:, :], ACT.Relu).then_inc(s["b_relu"], 1)
                act.wait_ge(s["b_relu"], gi + 1)
                g.activation(act_k[:, u], act_k[:, u], ACT.Square).then_inc(s["b_sq"], 1)
                act.wait_ge(s["b_r"], gi + 1)
                if gi >= 2:
                    act.wait_ge(s["b_x2"], gi - 1)
                g.activation(recept[:, u], bank[5][:, :], ACT.Tanh, scale=0.5).then_inc(s["b_tanh"], 1)
                for k in W1_TURNS[gi][1:]:
                    weights_out(k)

            def k_q1_out(t, u):
                act.wait_ge(s["c_turn"], t + 1)
                pt = bank[0][:, :].bitcast(FP16).rearrange("p (a g k) -> p a g k", a=2, g=4)
                if not (isinstance(t, int) and t < 2):
                    act.wait_ge(s["c_sT"], t - 1)
                    act.wait_ge(s["c_kbd"], t - 1)
                g.activation(kT1[:, u], pt[:, 0], ACT.Copy).then_inc(s["c_k_out"], 1)
                g.activation(qT1[:, u], pt[:, 1], ACT.Copy).then_inc(s["c_q1_out"], 1)

            def q2_out(t, u):
                act.wait_ge(s["c_turn2"], t + 1)
                if not (isinstance(t, int) and t < 2):
                    act.wait_ge(s["c_sT"], t - 1)
                turned = bank[1][:, 0:256].bitcast(FP16).rearrange("p (g b k) -> p (g b) k", g=4, b=TB)
                for i in range(4):
                    r = slice(32 * i, 32 * i + 32)
                    last = g.activation(q_bd[r, u, :, :, i, :].rearrange("p g b k -> p (g b) k"), turned[r], ACT.Copy)
                last.then_inc(s["c_qbd"], 1)

            def exp1(t, u):
                act.wait_ge(s["c_sT"], t + 1)
                if not (isinstance(t, int) and t < 2):
                    act.wait_ge(s["c_pl"], t - 1)
                    act.wait_ge(s["c_pv"], t - 1)
                for half in range(2):
                    c = slice(512 * half, 512 * half + 512)
                    i = g.activation(p1[:, u, c], bank[4 + half][:, :], ACT.Exp, scale=HD1 ** -0.5)
                i.then_inc(s["c_exp"], 1)

            act.wait_ge(s["c_zero_q"], 1)
            k_q1_out(0, 0)
            q2_out(0, 0)
            k_q1_out(1, 1)

            def turn1(t, u):
                exp1(t, u)
                if not isinstance(t, int) or t + 2 < NT:
                    k_q1_out(t + 2, u)
                if not isinstance(t, int) or t + 1 < NT:
                    q2_out(t + 1, 1 - u)

            zT_chunks = [0]

            def route_rows(r):
                first, n = ROUTED[r]
                if r == 0:
                    act.wait_ge(s["r_rstd"], r + 1)
                    act.wait_ge(s["c_qs"], 2)
                    normalize(0, first, n, z_all).then_inc(s["r_z"], 1)
                act.wait_ge(s["r_z"], r + 1)
                g.activation(row_buf[r][:, 0, :, 0:D // 2].bitcast(FP16), z_all[:, 0:n * D].rearrange("p (j d) -> p j d", d=D), ACT.Copy)\
                 .then_inc(s["r_high"], 1)

            def route_turned(r):
                for at in range(0, 4 if r else ROUTED[r][1], 4):
                    n = min(4, ROUTED[r][1] - at)
                    zT_chunks[0] += 1
                    act.wait_ge(s["r_zT"], zT_chunks[0])
                    g.activation(zTr[:, at:at + n].rearrange("p j h k -> p (j h k)"), bank[7][:, :].bitcast(FP16)[:, 0:2 * n * D],
                                 ACT.Copy).then_inc(s["r_zTs"], 1)

            def route_exp(r):
                act.wait_ge(s["r_less"], r + 1)
                x = rt[:, 5, 0:ROUTED[r][1]]
                g.activation(x, x, ACT.Exp).then_inc(s["r_exp"], 1)

            turns_and_routes(act, turn1, {1: queries_norm, 11: lambda: route_rows(0), 12: lambda: route_turned(0), 13: lambda: route_exp(0)})
            route_rows(1)
            route_turned(1)
            route_exp(1)
            for k in range(E, 2 * E):
                weights_out(k)

            def gelus(k, j, expert):
                act.wait_ge(s["e_up"], k + 1)
                if after(k, 4):
                    act.wait_ge(s["e_y"], k - 3)
                for c in range(FC):
                    i = g.activation(hid[:, j, c], bank[UP_BANKS[j]][:, c * 128:(c + 1) * 128], ACT.Gelu,
                                     bias=b1T[:, bass.ds(expert[j] * FC + c, 1)])
                i.then_inc(s["e_hid"], 1)

            g.activation(warm[:, :], ones_f[:, :], ACT.Gelu)
            act.wait_ge(s["r_exps"], 1)
            slots(act, gelus, experts_i)

        @block.vector
        def _(vec):
            g = nc.vector
            st = Steps(vec, s["vec_step"])

            def rsqrt(y, v, tmp, out_sem=None):
                half, sq, bits = tmp
                st.wait()
                st.done(g.tensor_scalar(out=half, in0=v, scalar1=-0.5, scalar2=None, op0=ALU.mult))
                st.done(g.tensor_scalar(out=bits.bitcast(I32), in0=v.bitcast(I32), scalar1=1, scalar2=None, op0=ALU.logical_shift_right))
                st.wait()
                st.done(g.tensor_scalar(out=y.bitcast(I32), in0=bits.bitcast(I32), scalar1=-1.0, scalar2=float(RSQRT_MAGIC),
                                        op0=ALU.mult, op1=ALU.add))
                for k in range(3):
                    st.wait()
                    st.done(g.tensor_tensor(out=sq, in0=y, in1=y, op=ALU.mult))
                    st.wait()
                    st.done(g.tensor_tensor(out=sq, in0=sq, in1=half, op=ALU.mult))
                    st.wait()
                    st.done(g.scalar_tensor_tensor(out=y, in0=sq, scalar=1.5, in1=y, op0=ALU.add, op1=ALU.mult))

            def joint_stats(c):
                vec.wait_ge(s[f"x_in{c}"], 32)
                for b in range(c * B // 4, (c + 1) * B // 4):
                    st.done(g.bn_stats(stat[:, b, :], joint[:, b * D:(b + 1) * D]))

            def joint_scales(first, last):
                st.wait()
                for b in range(first, last):
                    st.done(g.bn_aggr(mv[:, b, :], stat[:, b, :]))
                st.wait()
                var, h, sq, bits = (nwt[:, i, first:last] for i in range(4))
                y = scale_j[:, first:last]
                lo, hi = slice(0, 64), slice(64, 128)
                st.done(g.tensor_scalar(out=var[lo], in0=mv[lo, first:last, 1], scalar1=EPS, scalar2=None, op0=ALU.add))
                st.done(g.tensor_scalar(out=var[hi], in0=mv[hi, first:last, 1], scalar1=1.0 + EPS, scalar2=EPS * EPS, op0=ALU.mult, op1=ALU.add))
                rsqrt(y, var, (h, sq, bits))
                st.wait()
                st.done(g.scalar_tensor_tensor(out=bias_j[:, first:last], in0=mv[:, first:last, 0], scalar=-1.0, in1=y,
                                               op0=ALU.mult, op1=ALU.mult))
                st.wait()

            joint_stats(0)
            joint_scales(0, B // 4)

            def norm(t, u):
                for b in range(TB):
                    i = g.tensor_scalar(out=xn[:, u, b, :], in0=joint[:, bass.ds((TB * t + b) * D, D)],
                                        scalar1=scale_j[:, bass.ds(TB * t + b, 1)], scalar2=bias_j[:, bass.ds(TB * t + b, 1)],
                                        op0=ALU.mult, op1=ALU.add)
                i.then_inc(s["a_norm"], 1)

            norm(0, 0)
            norm(1, 1)
            vec.wait_ge(s["weights_in"], 48)
            wk_raw = wkv_raw[:, 0:INNER]
            for raw, split in ((wq_raw[:, :], wq_s), (wk_raw, wk_s)):
                st.done(g.tensor_copy(split[:, 0, :], raw))
                st.wait()
                st.done(g.tensor_tensor(out=split[:, 1, :], in0=raw, in1=split[:, 0, :], op=ALU.subtract))
            st.wait()
            for hl in range(2):
                src = wk_s[:, hl, :].rearrange("p (h a d) -> p h a d", a=2, d=HD0 // 2)
                dst = wkr_s[:, hl, :].rearrange("p (h a d) -> p h a d", a=2, d=HD0 // 2)
                for half in range(2):
                    i = g.tensor_copy(dst[:, :, half, :], src[:, :, 1 - half, :])
            i.then_inc(s["w_split"], 1)
            vec.wait_ge(s["consts_in"], 8 * 16)
            vec.wait_ge(s["x_res_in"], 16)
            vec.wait_ge(s["tanh_ready"], 1)

            def rope(t, u, n):
                p, k = K_PAIRS[n]
                vec.wait_ge(s["a_proj"], NP * t + n + 1)
                kk = bank[k][:, 0:256].rearrange("p (b k) -> p b k", b=TB)[:, :, 0:64]
                kr = bank[k][:, 256:384].rearrange("p (b k) -> p b k", b=TB)
                g.tensor_tensor(out=kcos[:, u, p], in0=kk, in1=cos0[:, :].unsqueeze(1).to_broadcast([128, TB, T]), op=ALU.mult)
                g.tensor_tensor(out=ksin[:, u, p], in0=kr, in1=sin0[:, :].unsqueeze(1).to_broadcast([128, TB, T]), op=ALU.mult).then_inc(s["a_rope"], 1)

            def rope_sum(t, u):
                vec.wait_ge(s["a_rope"], NP * (t + 1))
                kx = kT[:, u, :, :, 0:64].rearrange("p a b k -> p (a b) k")
                g.tensor_tensor(out=kx, in0=kcos[:, u].rearrange("p a b k -> p (a b) k"),
                                in1=ksin[:, u].rearrange("p a b k -> p (a b) k"), op=ALU.add).then_inc(s["a_k"], 1)
                vec.wait_ge(s["a_k"], t + 1)
                g.tensor_copy(kT_b[:, u, :, :, 0:64].rearrange("p a b k -> p (a b) k"), kx).then_inc(s["a_kb"], 1)

            def prob_low(t, u, b):
                vec.wait_ge(s["a_ph"], TB * t + b + 1)
                g.tensor_tensor(out=prob_s[:, u, 1, :, b, :], in0=prob[:, u, :, b, :], in1=prob_s[:, u, 0, :, b, :],
                                op=ALU.subtract).then_inc(s["a_pl"], 1)

            def maxima(t, u):
                for b in range(TB):
                    vec.wait_ge(s["a_s"], TB * t + b + 1)
                    g.tensor_reduce(out=nmax[:, u, b, :], in_=bank[4 + b][:, :].rearrange("p (a k) -> p a k", a=NP), axis=AXL.X,
                                    op=ALU.max, negate=True).then_inc(s["a_nmax"], 1)

            def denominators(t, u):
                vec.wait_ge(s["a_den"], t + 1)
                st.done(g.reciprocal(rden[:, u, :], bank[3][:, 0:H0]))
                st.wait()
                g.tensor_scalar(out=rden[:, u, :], in0=rden[:, u, :], scalar1=tanh_g[:, 0:1], scalar2=None, op0=ALU.mult).then_inc(s["a_rden"], 1)

            def residual(t, u):
                vec.wait_ge(s["a_y"], t + 1)
                vec.wait_ge(s["a_rden"], t + 1)
                xr = x_res[:, bass.ds(t * D, D)]
                for h in range(H0):
                    if h >= 2:
                        st.wait(1)
                    y, r = bank[h // 4][:, (h % 4) * D:(h % 4 + 1) * D], rden[:, u, h:h + 1]
                    dst = y_odd[:, :] if h % 2 else xr
                    if h == 1:
                        st.done(g.tensor_scalar(out=dst, in0=y, scalar1=r, scalar2=None, op0=ALU.mult))
                    else:
                        st.done(g.scalar_tensor_tensor(out=dst, in0=y, scalar=r, in1=dst, op0=ALU.mult, op1=ALU.add))
                st.wait()
                g.tensor_tensor(out=xr, in0=xr, in1=y_odd[:, :], op=ALU.add).then_inc(s["a_x1"], 1)

            joint_stats(1)
            for n in range(NP):
                rope(0, 0, n)
            rope_sum(0, 0)
            maxima(0, 0)
            joint_stats(2)
            joint_stats(3)
            joint_scales(B // 4, B)
            n0 = st.n
            vec.wait_ge(s["a_split"], 1)
            norm(2, 0)
            per = H0 + 1 + 1

            def stats(t, k):
                st.done(g.bn_stats(stat4[:, :, :, :].rearrange("p a n s -> p (a n s)")[:, bass.ds(k * NT * 6 + t * 6, 6)], x_res[:, bass.ds(t * D, D)]))

            def mean_var(first, count, k):
                st.wait()
                for t in range(first, first + count):
                    st.done(g.bn_aggr(mv4[:, k, t, :], stat4[:, k, t, :]))

            def rstd(k, first, count):
                st.wait()
                var, y, h, sq, bits = (nwt4[:, k, n, first:first + count] for n in range(5))
                st.done(g.tensor_scalar(out=var, in0=mv4[:, k, first:first + count, 1], scalar1=EPS, scalar2=None, op0=ALU.add))
                rsqrt(y, var, (h, sq, bits))
                st.wait()
                return g.scalar_tensor_tensor(out=var, in0=mv4[:, k, first:first + count, 0], scalar=-1.0, in1=y, op0=ALU.mult, op1=ALU.mult)

            late = [0]

            def turn(t, u, more=2):
                st.at(n0 + per * t - (0 if isinstance(t, int) and t == 0 else 1))
                v = 1 - u
                if more and not (isinstance(t, int) and t < 1):
                    vec.wait_ge(s["a_sT"], TB * t)
                    vec.wait_ge(s["a_s"], TB * t)
                for n in range(NP):
                    if more:
                        rope(t + 1, v, n)
                    if n % 2:
                        prob_low(t, u, n // 2)
                if more:
                    rope_sum(t + 1, v)
                if more == 0:
                    before = st.n
                    vec.wait_ge(s["ffn_in"], 80)
                    st.done(g.tensor_scalar(out=mix_w[:, 2:4], in0=mix_w[:, 0:2], scalar1=-1.0, scalar2=1.0, op0=ALU.mult, op1=ALU.add))
                    st.done(g.tensor_scalar(out=half_g[:, :], in0=tanh_g[:, 2:3], scalar1=0.5, scalar2=None, op0=ALU.mult))
                    mean_var(0, NT - GT, 0)
                    rstd(0, 0, NT - GT).then_inc(s["b_ln"], 1)
                    late[0] = st.n - before
                denominators(t, u)
                if not (isinstance(t, int) and t == 0):
                    vec.wait_ge(s["a_x1"], t)
                    stats(t - 1, 0)
                if more:
                    if not (isinstance(t, int) and t < 1):
                        vec.wait_ge(s["a_nturn"], t)
                    maxima(t + 1, v)
                if more == 2:
                    vec.wait_ge(s["a_split"], t + 2)
                    norm(t + 3, v)
                residual(t, u)

            turn(0, 0)
            turn(1, 1)
            with vec.Fori(1, NT // 2 - 2) as i:
                turn(2 * i, 0)
                turn(2 * i + 1, 1)
            turn(NT - 4, 0)
            turn(NT - 3, 1, 1)
            turn(NT - 2, 0, 1)
            turn(NT - 1, 1, 0)
            st.at(n0 + late[0] + per * NT - 1)
            vec.wait_ge(s["a_x1"], NT)
            for u in range(2):
                i = g.memset(zT[:, u, 1, :, 0:1], 0.0)
            i.then_inc(s["mix_up"], 1)
            stats(NT - 1, 0)
            mean_var(NT - GT, GT, 0)
            rstd(0, NT - GT, GT).then_inc(s["b_ln"], 1)

            def ffn_tail(gi, u):
                vec.wait_ge(s["b_v"], gi + 1)
                vec.wait_ge(s["b_tanh"], gi + 1)
                st.done(g.scalar_tensor_tensor(out=recept[:, u], in0=recept[:, u], scalar=1.0, in1=bank[6][:, :], op0=ALU.add, op1=ALU.mult))
                st.wait()
                xr = x_res[:, gi * GT * D:(gi + 1) * GT * D]
                g.scalar_tensor_tensor(out=xr, in0=recept[:, u], scalar=half_g[:, 0:1], in1=xr, op0=ALU.mult, op1=ALU.add).then_inc(s["b_x2"], 1)

            def weights_low(k):
                vec.wait_ge(s["d_ws"], k + 1)
                c = slice(F * k, F * (k + 1))
                g.tensor_tensor(out=w1_s[:, 1, c], in0=bank[k % 2][:, :], in1=w1_s[:, 0, c], op=ALU.subtract).then_inc(s["d_wl"], 1)

            def queries_stats(half):
                first = half * (NT // 2)
                vec.wait_ge(s["b_x2"], (half + 1) * NG // 2)
                for t in range(first, first + NT // 2):
                    stats(t, 1)
                mean_var(first, NT // 2, 1)

            def queries_rstd(half):
                rstd(1, half * (NT // 2), NT // 2).then_inc(s["c_rstd"], 1)

            def queries_norm():
                vec.wait_ge(s["c_rstd"], 1)
                for t in range(NT // 2):
                    i = g.tensor_scalar(out=q_f[:, t * D:(t + 1) * D], in0=x_res[:, t * D:(t + 1) * D], scalar1=nwt4[:, 1, 1, t:t + 1],
                                        scalar2=nwt4[:, 1, 0, t:t + 1], op0=ALU.mult, op1=ALU.add)
                i.then_inc(s["c_ln"], 1)

            def queries_rotate(half):
                n = half_w if half else Q_SHARE * D
                x, tmp = q_f[:, 0:n], q_tmp[:, 0:n]
                c = slice(half * half_w, half * half_w + n)
                vec.wait_ge(s["c_ln"], half + 1)
                rotate(g, st, x, tmp, x, sin1, cos1)
                st.done(g.tensor_copy(q1_s[:, 0, c], x))
                st.wait()
                g.tensor_tensor(out=q1_s[:, 1, c], in0=x, in1=q1_s[:, 0, c], op=ALU.subtract).then_inc(s["c_qs"], 1)
                vec.wait_ge(s["c_qs"], half + 1)

            vec.wait_ge(s["c_consts"], 64)
            vec.wait_ge(s["ffn_wT_up"], 1)
            g.tensor_tensor(out=rwT_s[:, 1], in0=rwT[:, :], in1=rwT_s[:, 0], op=ALU.subtract).then_inc(s["small_up"], 1)
            vec.wait_ge(s["moe_in"], 48)
            g.tensor_copy(b2_s[:, 0], b2_row[:, :]).then_inc(s["small_up"], 1)
            vec.wait_ge(s["small_up"], 2)
            g.tensor_tensor(out=b2_s[:, 1], in0=b2_row[:, :], in1=b2_s[:, 0], op=ALU.subtract).then_inc(s["small_up"], 1)
            vec.wait_ge(s["c_zero"], 1)
            st.done(g.memset(own_row[:, :], 0.0))
            st.wait()
            for b in range(TB):
                r = slice(64 * b, 64 * b + 64)
                i = g.memset(own_row[r, b:b + 1], 1.0)
                for u in range(2):
                    st.done(g.memset(v_bd[r, u, 0, :, b, 16], 1.0))
            i.then_inc(s["c_own"], 1)
            g.memset(q_bd[:, :, :, :, :, :], 0.0).then_inc(s["c_zero_q"], 1)
            vec.wait_ge(s["c_vh"], 1)
            g.tensor_tensor(out=v1_s[:, 1], in0=ctx_tok[:, :], in1=v1_s[:, 0], op=ALU.subtract).then_inc(s["c_kv"], 1)
            for gi in range(NG):
                if gi == 2:
                    ffn_tail(1, 1)
                    queries_stats(0)
                    queries_rstd(0)
                    queries_norm()
                for k in W1_TURNS[gi]:
                    weights_low(k)
                if gi in (1, 3):
                    ffn_tail(gi - 1, (gi - 1) % 2)
            queries_rotate(0)
            ffn_tail(NG - 1, (NG - 1) % 2)
            queries_stats(1)

            vec.wait_ge(s["c_zero"], 2)

            def blocks(t, u, src, dst, ready):
                for i in range(4):
                    r = slice(32 * i, 32 * i + 32)
                    last = g.tensor_copy(dst[r, u, :, :, i, :].rearrange("p g b k -> p (g b) k"),
                                         src[r, u].rearrange("p g (b k) -> p (g b) k", b=TB))
                last.then_inc(ready, 1)

            def k_blocks(t, u):
                vec.wait_ge(s["c_k_out"], t + 1)
                blocks(t, u, kT1, k_bd, s["c_kbd"])

            def max1(t, u):
                vec.wait_ge(s["c_s"], t + 1)
                vec.wait_ge(s["c_turn"], t + 1)
                for half in range(2):
                    i = g.tensor_reduce(out=q_st[:, u, 8 * half:8 * half + 8, 3, 4], in_=bank[2 + half][:, :].rearrange("p (h k) -> p h k", k=T),
                                        axis=AXL.X, op=ALU.max, negate=True)
                i.then_inc(s["c_max"], 1)

            def p_split(t, u):
                vec.wait_ge(s["c_exp"], t + 1)
                if not (isinstance(t, int) and t < 2):
                    vec.wait_ge(s["c_pv"], t - 1)
                g.tensor_copy(p1_s[:, u, 0], p1[:, u]).then_inc(s["c_ph"], 1)
                vec.wait_ge(s["c_ph"], t + 1)
                g.tensor_tensor(out=p1_s[:, u, 1], in0=p1[:, u], in1=p1_s[:, u, 0], op=ALU.subtract).then_inc(s["c_pl"], 1)

            def output1(t, u):
                vec.wait_ge(s["c_pv"], t + 1)
                pv = bank[6][:, 0:272].rearrange("p (a b e) -> p a b e", a=H1 // 2, b=TB)
                st.done(g.reciprocal(rden1[:, u], pv[:, :, :, 16]))
                st.wait()
                for hh in range(2):
                    for b in range(TB):
                        r = slice(64 * hh, 64 * hh + 64)
                        st.done(g.tensor_tensor(out=o1[64 * b:64 * b + 64, u].rearrange("p (a h e) -> p a h e", a=8, h=2)[:, :, hh, :],
                                                in0=pv[r, :, b, 8 * hh:8 * hh + 8],
                                                in1=rden1[r, u, :, b:b + 1].to_broadcast([64, 8, 8]), op=ALU.mult))
                st.wait()
                xr = x_res[:, bass.ds(t * D, D)]
                g.scalar_tensor_tensor(out=xr, in0=o1[:, u], scalar=tanh_g[:, 1:2], in1=xr, op0=ALU.mult, op1=ALU.add).then_inc(s["c_x3"], 1)

            k_blocks(0, 0)
            max1(0, 0)
            queries_rstd(1)
            k_blocks(1, 1)
            n1 = st.base + st.n
            per1 = 5 + 1
            extra = [0]

            def before(t):
                return n1 + extra[0] + (per1 * t - per1 if not isinstance(t, int) or t else 0)

            def turn1(t, u):
                st.at(before(t))
                more = not isinstance(t, int) or t + 1 < NT
                if not isinstance(t, int) or t:
                    output1(t - 1, 1 - u)
                if more:
                    max1(t + 1, 1 - u)
                if not isinstance(t, int) or t:
                    vec.wait_ge(s["c_x3"], t)
                    stats(t - 1, 0)
                p_split(t, u)
                if not isinstance(t, int) or t + 2 < NT:
                    k_blocks(t + 2, u)


            def piece(t, f, *args):
                def run():
                    st.at(before(t))
                    f(*args)
                    extra[0] += st.n
                return run

            def route_stats(r):
                first, n = ROUTED[r]
                mean_var(first, n, 0)
                rstd(0, first, n).then_inc(s["r_rstd"], 1)
                if r:
                    vec.wait_ge(s["r_rstd"], r + 1)
                    vec.wait_ge(s["r_high"], r)
                    for j in range(n):
                        t = first + j
                        i = g.tensor_scalar(out=z_all[:, j * D:(j + 1) * D], in0=x_res[:, t * D:(t + 1) * D], scalar1=nwt4[:, 0, 1, t:t + 1],
                                            scalar2=nwt4[:, 0, 0, t:t + 1], op0=ALU.mult, op1=ALU.add)
                    i.then_inc(s["r_z"], 1)

            def route_rows(r):
                n = ROUTED[r][1]
                vec.wait_ge(s["r_high"], r + 1)
                zz = z_all[:, 0:n * D].rearrange("p (j d) -> p j d", d=D)
                hi, lo = (row_buf[r][:, 0, :, k * (D // 2):(k + 1) * (D // 2)].bitcast(FP16) for k in range(2))
                g.tensor_tensor(out=lo, in0=zz, in1=hi, op=ALU.subtract).then_inc(s["r_low"], 1)
                vec.wait_ge(s["r_low"], r + 1)
                st.done(g.tensor_copy(row_buf[r][:, 1, :, 0:D], row_buf[r][:, 0, :, 0:D]))
                if r:
                    vec.wait_ge(s["r_zT"], ZT_CHUNKS)
                    g.tensor_copy(zTr[:, 4:n].rearrange("p j h k -> p (j h k)"), bank[6][:, :].bitcast(FP16)[:, 0:2 * (n - 4) * D]).then_inc(s["r_zTs"], 1)

            def prefix(src, spare, n):
                dst, other = spare
                cols = lambda x, lo, hi: x[:, :, lo:hi] if len(x.shape) == 3 else x[:, lo:hi]
                step = 1
                while step < n:
                    st.done(g.tensor_copy(cols(dst, 0, step), cols(src, 0, step)))
                    st.done(g.tensor_tensor(out=cols(dst, step, n), in0=cols(src, step, n), in1=cols(src, 0, n - step), op=ALU.add))
                    st.wait()
                    src, dst, other = dst, other, dst
                    step *= 2
                return src

            def route_gates(r):
                first, n = ROUTED[r]
                vec.wait_ge(s["r_log"], r + 1)
                lg, above, equal, run, run2, ex, gates_ = (rt[:, k, 0:ROUTED[r][1]] for k in range(7))
                st.done(g.tensor_copy(lg, bank[7][:, 0:n * E].rearrange("p (j e) -> p j e", e=E)))
                st.wait()
                for j in range(n):
                    st.done(g.max(top[:, j], lg[:, j]))
                st.wait()
                m1 = top[:, 0:n, 0:1].to_broadcast([128, n, E])
                m2 = top[:, 0:n, 1:2].to_broadcast([128, n, E])
                g.tensor_tensor(out=ex, in0=lg, in1=m1, op=ALU.subtract).then_inc(s["r_less"], 1)
                st.done(g.tensor_tensor(out=above, in0=lg, in1=m2, op=ALU.is_gt))
                st.done(g.tensor_tensor(out=equal, in0=lg, in1=m2, op=ALU.is_equal))
                st.wait()
                counted = prefix(equal, (run, run2), E)
                st.done(g.tensor_reduce(out=rs[:, 0, 0:n], in_=above, axis=AXL.X, op=ALU.add))
                st.wait()
                st.done(g.tensor_scalar(out=rs[:, 0, 0:n], in0=rs[:, 0, 0:n], scalar1=-1.0, scalar2=2.0, op0=ALU.mult, op1=ALU.add))
                st.wait()
                st.done(g.tensor_tensor(out=counted, in0=counted, in1=rs[:, 0, 0:n].unsqueeze(2).to_broadcast([128, n, E]), op=ALU.is_le))
                st.wait()
                st.done(g.tensor_tensor(out=equal, in0=equal, in1=counted, op=ALU.mult))
                st.wait()
                st.done(g.tensor_tensor(out=above, in0=above, in1=equal, op=ALU.add))
                st.wait()
                g.tensor_copy(picked[:, 0:n, :], above).then_inc(s["r_pick"], 1)

            def route_weights(r):
                above, ex, gates_ = (rt[:, k, 0:ROUTED[r][1]] for k in (1, 5, 6))
                n = ROUTED[r][1]
                vec.wait_ge(s["r_pick"], r + 1)
                vec.wait_ge(s["r_exp"], r + 1)
                st.done(g.tensor_tensor(out=ex, in0=ex, in1=above, op=ALU.mult))
                st.wait()
                st.done(g.tensor_reduce(out=rs[:, 1, 0:n], in_=ex, axis=AXL.X, op=ALU.add))
                st.wait()
                st.done(g.reciprocal(rs[:, 2, 0:n], rs[:, 1, 0:n]))
                st.wait()
                st.done(g.tensor_scalar(out=rs[:, 2, 0:n], in0=rs[:, 2, 0:n], scalar1=tanh_g[:, 3:4], scalar2=None, op0=ALU.mult))
                st.wait()
                st.done(g.tensor_tensor(out=gates_, in0=ex, in1=rs[:, 2, 0:n].unsqueeze(2).to_broadcast([128, n, E]), op=ALU.mult))

            def route_slots(r):
                at, n = ROUTED[r]
                vec.wait_ge(s["r_rank"], r + 1)
                above, gates_, pos, is_a, ga, gb = (rt[:, k, 0:ROUTED[r][1]] for k in (1, 6, 7, 8, 9, 10))
                rank = bank[7][:, 0:n * E].rearrange("p (j e) -> p j e", e=E)
                first, total = region[:, :], count[:, (r + 1) % 2]
                here = bank[7][:, RT * E:RT * E + E]
                if r:
                    first = per_e[:, 0]
                    st.done(g.tensor_tensor(out=first, in0=region[:, :], in1=count[:, r % 2], op=ALU.add))
                    st.done(g.tensor_tensor(out=total, in0=count[:, r % 2], in1=here, op=ALU.add))
                else:
                    st.done(g.tensor_copy(total, here))
                st.wait()
                st.done(g.tensor_tensor(out=pos, in0=rank, in1=first.unsqueeze(1).to_broadcast([128, n, E]), op=ALU.add))
                st.wait()
                st.done(g.tensor_tensor(out=pos, in0=pos, in1=above, op=ALU.mult))
                st.wait()
                st.done(g.tensor_reduce(out=rs[:, 3, 0:n], in_=pos, axis=AXL.X, op=ALU.max))
                st.done(g.tensor_reduce(out=rs[:, 4, 0:n], in_=pos, axis=AXL.X, op=ALU.add))
                st.wait()
                st.done(g.tensor_tensor(out=rs[:, 5, 0:n], in0=rs[:, 4, 0:n], in1=rs[:, 3, 0:n], op=ALU.subtract))
                st.done(g.tensor_tensor(out=is_a, in0=pos, in1=rs[:, 3, 0:n].unsqueeze(2).to_broadcast([128, n, E]), op=ALU.is_equal))
                st.wait()
                st.done(g.tensor_tensor(out=ga, in0=gates_, in1=is_a, op=ALU.mult))
                st.wait()
                st.done(g.tensor_tensor(out=gb, in0=gates_, in1=ga, op=ALU.subtract))
                st.wait()
                st.done(g.tensor_reduce(out=row_buf[r][:, 0, :, D + 1], in_=ga, axis=AXL.X, op=ALU.add))
                st.done(g.tensor_reduce(out=row_buf[r][:, 1, :, D + 1], in_=gb, axis=AXL.X, op=ALU.add))
                st.done(g.tensor_copy(row_buf[r][:, 0, :, D], tok_id[:, at:at + n]))
                st.done(g.tensor_scalar(out=row_buf[r][:, 1, :, D], in0=tok_id[:, at:at + n], scalar1=float(TOK), scalar2=None, op0=ALU.add))
                st.done(g.tensor_copy(slot_at[:, 0, at:at + n], rs[:, 3, 0:n]))
                g.tensor_copy(slot_at[:, 1, at:at + n], rs[:, 5, 0:n]).then_inc(s["r_slots"], 1)

            def tables():
                total = count[:, len(ROUTED) % 2]
                n_t, end, spare, start = (per_e[:, k] for k in (1, 2, 3, 4))
                st.wait()
                st.done(g.tensor_scalar(out=per_ei[:, 0], in0=total, scalar1=127.0, scalar2=None, op0=ALU.add))
                st.done(g.tensor_tensor(out=per_ei[:, 1], in0=total, in1=region[:, :], op=ALU.add))
                st.wait()
                st.done(g.tensor_scalar(out=per_ei[:, 0], in0=per_ei[:, 0], scalar1=7, scalar2=None, op0=ALU.logical_shift_right))
                st.wait()
                st.done(g.tensor_copy(n_t, per_ei[:, 0]))
                st.wait()
                end = prefix(n_t, (end, spare), E)
                at = lambda x: x.unsqueeze(1).to_broadcast([128, SLOTS, E])
                past, nts = big[:, 0], big[:, 1]
                st.done(g.tensor_tensor(out=past, in0=tile_no[:, :].unsqueeze(2).to_broadcast([128, SLOTS, E]), in1=at(end), op=ALU.is_ge))
                st.wait()
                st.done(g.tensor_tensor(out=nts, in0=past, in1=at(n_t), op=ALU.mult))
                first, row, gap = (tab[:, k] for k in range(3))
                expert = expert_pad[:, 0:SLOTS]
                st.done(g.memset(expert_pad[:, SLOTS:SLOTS + DIGITS], 0.0))
                st.done(g.tensor_reduce(out=expert, in_=past[:, :, 0:E - 1], axis=AXL.X, op=ALU.add))
                st.wait()
                st.done(g.tensor_reduce(out=first, in_=nts[:, :, 0:E - 1], axis=AXL.X, op=ALU.add))
                st.wait()
                st.done(g.tensor_tensor(out=row, in0=tile_no[:, :], in1=first, op=ALU.subtract))
                st.done(g.tensor_scalar(out=gap, in0=expert, scalar1=float(REG), scalar2=None, op0=ALU.mult))
                st.wait()
                st.done(g.scalar_tensor_tensor(out=row, in0=row, scalar=128.0, in1=gap, op0=ALU.mult, op1=ALU.add))
                st.wait()
                st.done(g.tensor_scalar(out=gap, in0=row, scalar1=-1.0, scalar2=float(NULL), op0=ALU.mult, op1=ALU.add))
                st.wait()
                st.done(g.tensor_tensor(out=gap, in0=gap, in1=past[:, :, E - 1], op=ALU.mult))
                st.wait()
                st.done(g.tensor_tensor(out=row, in0=row, in1=gap, op=ALU.add))
                st.done(g.scalar_tensor_tensor(out=null_off[:, :], in0=tile_no[:, :], scalar=128.0, in1=past[:, :, E - 1], op0=ALU.mult, op1=ALU.mult))
                st.wait()
                g.tensor_copy(tab_i[:, :], row).then_inc(s["r_tab"], 1)
                digit = lambda n: expert_pad[:, n:n + SLOTS].rearrange("p (i j) -> p i j", j=4)[:, :, 0]
                digits = gap[:, 0:SLOTS // 4]
                st.done(g.tensor_copy(digits, digit(DIGITS - 1)))
                for n in reversed(range(DIGITS - 1)):
                    st.wait()
                    st.done(g.scalar_tensor_tensor(out=digits, in0=digits, scalar=float(E), in1=digit(n), op0=ALU.mult, op1=ALU.add))
                st.wait()
                g.tensor_copy(experts_i[:, :], digits).then_inc(s["r_exps"], 1)

            vec.wait_ge(s["moe_consts"], 80)
            vec.wait_ge(s["pads_up"], 1)
            g.tensor_copy(pad_rows[:, :, D:D + 1], pad_at[:, :].unsqueeze(2)).then_inc(s["pads_up"], 1)
            turns_and_routes(vec, turn1, {2: piece(2, queries_rotate, 1), 11: piece(11, route_stats, 0), 12: piece(12, route_rows, 0),
                                          13: piece(13, route_gates, 0), 14: piece(14, route_weights, 0), 15: piece(15, route_slots, 0)})
            st.at(before(NT))
            output1(NT - 1, 1)
            vec.wait_ge(s["c_x3"], NT)
            stats(NT - 1, 0)
            route_stats(1)
            route_rows(1)
            route_gates(1)
            route_weights(1)
            route_slots(1)
            tables()

            def rows_out(k, j):
                vec.wait_ge(s["e_turn"], k + 1)
                if after(k, 2):
                    vec.wait_ge(s["e_up"], k - 1)
                g.tensor_copy(rT[:, j % 2], bank[j % 2][:, 0:128].bitcast(FP16).rearrange("p (h k) -> p h k", h=2)).then_inc(s["e_xT"], 1)
                if after(k, 4):
                    vec.wait_ge(s["e_out"], k - 3)
                g.tensor_tensor(out=y_row[:, j:j + 1], in0=rows[:, j, D:D + 1], in1=null_off[:, bass.ds(k, 1)], op=ALU.add).then_inc(s["e_ex"], 1)

            def weigh(k, j):
                vec.wait_ge(s["e_ex"], k + 1)
                if after(k, 4):
                    vec.wait_ge(s[f"e_sent{j}"], 16 * (k // 4) if isinstance(k, int) else 4 * (k - j))
                g.tensor_copy(y_at[:, j:j + 1], y_row[:, j:j + 1])
                vec.wait_ge(s["e_y"], k + 1)
                vec.wait_ge(s["e_gate"], k + 1)
                g.tensor_scalar(out=y_out[:, j, :], in0=bank[4 + j % 2][:, 0:D], scalar1=y_gate[:, j:j + 1], scalar2=None, op0=ALU.mult)\
                 .then_inc(s["e_out"], 1)

            def expert_turn(k, j, _):
                if not isinstance(k, int) or k + 3 < SLOTS:
                    rows_out(k + 3, (j + 3) % 4)
                weigh(k, j)

            vec.wait_ge(s["r_tab"], 1)
            rows_out(0, 0)
            rows_out(1, 1)
            rows_out(2, 2)
            slots(vec, expert_turn)
            for gi in range(NG):
                vec.wait_ge(s[f"f_first{gi}"], 16)
                c = slice(gi * GT * D, (gi + 1) * GT * D)
                st.at(0)
                g.tensor_tensor(out=x_res[:, c], in0=x_res[:, c], in1=joint[:, c], op=ALU.add).then_inc(s["f_half"], 1)
                vec.wait_ge(s["f_half"], gi + 1)
                vec.wait_ge(s[f"f_second{gi}"], 16)
                g.tensor_tensor(out=x_res[:, c], in0=x_res[:, c], in1=joint[:, NT * D + gi * GT * D:NT * D + (gi + 1) * GT * D],
                                op=ALU.add).then_inc(s["f_x"], 1)

        @block.tensor
        def _(pe):
            g = nc.tensor
            pe.wait_ge(s["ident_up"], 3)
            pe.wait_ge(s["weights_in"], 48)
            for p in range(NP):
                i = g.transpose(bank[6][:, p * D:(p + 1) * D], wkv_raw[:, INNER + p * 128:INNER + (p + 1) * 128], ident[:, :])
            i.then_inc(s["wv_turned"], 1)
            pe.wait_ge(s["wv_copied"], 1)
            for h in range(H0):
                r = slice(64 * (h % 2), 64 * (h % 2) + 64)
                i = g.matmul(bank[4 + h % 2][:, (h // 2) * D:(h // 2 + 1) * D], wvT[r, h // 2, :], wo_sb[r, h // 2, :], start=True, stop=True)
                if h >= H0 - 2:
                    i.then_inc(s["wvo_mm"], 1)
            pe.wait_ge(s["w_split"], 1)
            pe.wait_ge(s["q_zero"], 1)
            pe.wait_ge(s["select_up"], 1)

            def turn_x(t, u):
                pe.wait_ge(s["a_split"], t + 1)
                for hl in range(2):
                    for b in range(TB):
                        i = g.transpose(bank[2][:, 0:256].bitcast(FP16)[:, (hl * TB + b) * 128:(hl * TB + b + 1) * 128],
                                        x_s[:, u, hl, b, :], ident_h[:, :])
                i.then_inc(s["a_turn"], 1)

            def product(dst, w, x, cols):
                for n, (i, j) in enumerate(((0, 0), (0, 1), (1, 0))):
                    last = g.matmul(dst, w[:, i, cols], x[j], start=n == 0, stop=n == 2)
                return last

            def project_q(t, u):
                for p in range(NP):
                    i = product(bank[2][:, p * 128:(p + 1) * 128], wq_s, [xT[:, u, j, :, 64:128] for j in range(2)],
                                slice(p * 128, (p + 1) * 128))
                i.then_inc(s["a_projq"], 1)

            def project_k(t, u, ns):
                if ns[0] == 0:
                    pe.wait_ge(s["a_xT"], t + 1)
                if not (isinstance(t, int) and t == 0):
                    if ns[0] == 0:
                        pe.wait_ge(s["a_nmax"], TB * t)
                    elif not (isinstance(t, int) and t == 1):
                        pe.wait_ge(s["a_x1"], t - 1)
                for n in ns:
                    p, k = K_PAIRS[n]
                    cols = slice(p * 128, (p + 1) * 128)
                    product(bank[k][:, 0:256], wk_s, [xT[:, u, j].rearrange("p b k -> p (b k)") for j in range(2)], cols)
                    product(bank[k][:, 256:384], wkr_s, [xT[:, u, j, :, 0:64] for j in range(2)], cols).then_inc(s["a_proj"], 1)

            def scores(t, u):
                pe.wait_ge(s["a_q"], t + 1)
                pe.wait_ge(s["a_kb"], t + 1)
                pe.wait_ge(s["a_qk"], NP * (t + 1))
                for b in range(TB):
                    for p in range(NP):
                        i = g.matmul(bank[4 + b][:, p * 128:(p + 1) * 128], qT_b[:, u, p, b].rearrange("p h q -> p (h q)"),
                                     kT_b[:, u, p, b, :], start=True, stop=True)
                    i.then_inc(s["a_s"], 1)

            def turn_max(t, u):
                pe.wait_ge(s["a_nmax"], TB * (t + 1))
                g.transpose(bank[3][0:8, 64:128].bitcast(BF16), nmax[:, u].rearrange("p b a -> p (b a)"), ident_b[:, :]).then_inc(s["a_nturn"], 1)

            def scores_t(t, u):
                pe.wait_ge(s["a_nmaxT"], t + 1)
                pe.wait_ge(s["a_k"], t + 1)
                pe.wait_ge(s["a_q"], t + 1)
                pe.wait_ge(s["a_qk"], NP * (t + 1))
                if not (isinstance(t, int) and t == 0):
                    pe.wait_ge(s["a_axs"], TB * t)
                for b in range(TB):
                    for p in range(NP):
                        d = bank[6 + b][:, p * 128:(p + 1) * 128]
                        g.matmul(d, kT[:, u, p, b, :], qT[:, u, p, b].rearrange("p h q -> p (h q)"), start=True, stop=False)
                        i = g.matmul(d, select[:, b * NP + p, :], nmaxT[:, u, :], start=False, stop=True)
                    i.then_inc(s["a_sT"], 1)

            def attend(t, u):
                for b in range(TB):
                    pe.wait_ge(s["a_pl"], TB * t + b + 1)
                    for n, (i, j) in enumerate(((0, 0), (0, 1), (1, 0))):
                        last = g.matmul(bank[6 + b][:, :], x_s[:, u, i, b, :], prob_s[:, u, j, :, b, :], start=n == 0, stop=n == 2)
                    last.then_inc(s["a_ax"], 1)
                pe.wait_ge(s["a_nmaxT"], t + 1)
                for h in range(H0):
                    for hl in range(2):
                        i = g.matmul(bank[3][:, h:h + 1], prob_s[:, u, hl, h].rearrange("p b q -> p (b q)"), ones_h[:, :],
                                     start=hl == 0, stop=hl == 1)
                i.then_inc(s["a_den"], 1)

            def project_out(t, u, heads):
                if heads[0] == 0:
                    pe.wait_ge(s["a_axs"], TB * (t + 1))
                for h in heads:
                    i = g.matmul(bank[h // 4][:, (h % 4) * D:(h % 4 + 1) * D], ax[:, u, h].rearrange("p b q -> p (b q)"),
                                 wvo[:, h, :], start=True, stop=True)
                if h == H0 - 1:
                    i.then_inc(s["a_y"], 1)

            pe.wait_ge(s["wvo_up"], 2)
            turn_x(0, 0)
            project_k(0, 0, (0, 1))
            project_q(0, 0)
            project_k(0, 0, (2, 3))
            scores(0, 0)
            turn_max(0, 0)
            pe.wait_ge(s["a_q"], 1)
            turn_x(1, 1)

            def turn(t, u, more=2):
                v = 1 - u
                if more:
                    project_k(t + 1, v, (0, 1))
                scores_t(t, u)
                if more:
                    project_q(t + 1, v)
                    project_k(t + 1, v, (2, 3))
                attend(t, u)
                if more:
                    scores(t + 1, v)
                project_out(t, u, range(0, 6))
                if more:
                    pe.wait_ge(s["a_rden"], t + 1)
                    turn_max(t + 1, v)
                if more == 2:
                    pe.wait_ge(s["a_q"], t + 2)
                    turn_x(t + 2, u)
                project_out(t, u, range(6, H0))

            turn(0, 0)
            turn(1, 1)
            with pe.Fori(1, NT // 2 - 1) as i:
                turn(2 * i, 0)
                turn(2 * i + 1, 1)
            turn(NT - 2, 0, 1)
            turn(NT - 1, 1, 0)
            pe.wait_ge(s["ffn_in"], 80)
            pe.wait_ge(s["a_rden"], NT)
            for n in range(3):
                i = g.transpose(bank[3][:, n * D:(n + 1) * D], ffn_raw[:, n, :], ident[:, :])
            pe.wait_ge(s["moe_in"], 48)
            g.transpose(bank[3][:, 384:384 + E * FC], b1_raw[:, :], ident[0:E * FC, 0:E * FC])
            g.transpose(bank[3][:, 416:416 + E], rw_raw[:, :], ident[0:E, 0:E]).then_inc(s["ffn_turned"], 1)

            def z_turn(gi, u):
                pe.wait_ge(s["b_z"], gi + 1)
                if gi:
                    pe.wait_ge(s["b_zTs"], gi)
                for j in range(GT):
                    i = g.transpose(bank[2][:, j * D:(j + 1) * D], z[:, u, j * D:(j + 1) * D], ident[:, :])
                i.then_inc(s["b_zT"], 1)

            def keys_receptance(gi, u):
                pe.wait_ge(s["ffn_wT_up"], 1)
                pe.wait_ge(s["b_zTs"], gi + 1)
                if gi:
                    pe.wait_ge(s["b_relu"], gi)
                    pe.wait_ge(s["b_tanh"], gi)
                now, before = (zT[:, u, n].rearrange("p b q -> p (b q)") for n in range(2))
                g.matmul(bank[4][:, :], ffn_wT[:, 1, :], now, start=True, stop=False)
                g.matmul(bank[4][:, :], ffn_wT[:, 3, :], before, start=False, stop=True).then_inc(s["b_k"], 1)
                for j in range(GT):
                    for n, x in enumerate((now, before)):
                        i = g.matmul(bank[5][:, j * D:(j + 1) * D], x[:, j * 128:(j + 1) * 128], ffn_wT[:, 2 * n, :], start=n == 0, stop=n == 1)
                i.then_inc(s["b_r"], 1)

            def values(gi, u):
                pe.wait_ge(s["b_sq"], gi + 1)
                if gi:
                    pe.wait_ge(s["b_x2"], gi)
                else:
                    pe.wait_ge(s["a_axs"], TB * NT)
                for j in range(GT):
                    i = g.matmul(bank[6][:, j * D:(j + 1) * D], act_k[:, u, j * D:(j + 1) * D], ffn_wT[:, 4, :], start=True, stop=True)
                i.then_inc(s["b_v"], 1)

            def weights_turn(k):
                if k >= 2:
                    pe.wait_ge(s["d_ws"], k - 1)
                    if k - 2 < E:
                        pe.wait_ge(s["d_wl"], k - 1)
                for c in range(FC):
                    src = w1_raw[:, FC * k + c, :] if k < E else w2_raw[:, k - E, c * 128:(c + 1) * 128]
                    i = g.transpose(bank[k % 2][:, c * 128:(c + 1) * 128], src, ident[:, :])
                i.then_inc(s["d_w"], 1)

            pe.wait_ge(s["moe_in2"], 32)
            pe.wait_ge(s["a_x1"], NT)
            z_turn(0, 0)
            for gi in range(NG):
                if gi + 1 < NG:
                    z_turn(gi + 1, (gi + 1) % 2)
                for k in W1_TURNS[gi][:1]:
                    weights_turn(k)
                keys_receptance(gi, gi % 2)
                for k in W1_TURNS[gi][1:]:
                    weights_turn(k)
                values(gi, gi % 2)

            def turn_kq(t, u):
                pe.wait_ge(s["c_st"], t + 1)
                pe.wait_ge(s["c_q"], t + 1)
                if not (isinstance(t, int) and t == 0):
                    pe.wait_ge(s["c_q1_out"], t)
                pt = bank[0][:, :].bitcast(FP16)
                for a_, x in enumerate((k_st, q_st)):
                    for k in range(4):
                        i = g.transpose(pt[:, (4 * a_ + k) * 128:(4 * a_ + k + 1) * 128],
                                        x[:, u, 4 * k:4 * k + 4].rearrange("p h c e -> p (h c e)"), ident_h[:, :])
                i.then_inc(s["c_turn"], 1)

            def scores1(t, u):
                pe.wait_ge(s["c_kbd"], t + 1)
                pe.wait_ge(s["c_q1_out"], t + 1)
                if not (isinstance(t, int) and t == 0):
                    pe.wait_ge(s["c_max"], t)
                for b in range(TB):
                    for k in range(4):
                        i = g.matmul(bank[2 + k // 2][64 * b:64 * b + 64, (k % 2) * 256:(k % 2) * 256 + 256],
                                     qT1[:, u, k, 64 * b:64 * b + 64], k_bd[:, u, k, b].rearrange("p i k -> p (i k)"), start=True, stop=True)
                i.then_inc(s["c_s"], 1)

            def turn_q2(t, u):
                pe.wait_ge(s["c_max"], t + 1)
                if not (isinstance(t, int) and t == 0):
                    pe.wait_ge(s["c_qbd"], t)
                for k in range(4):
                    i = g.transpose(bank[1][:, 0:256].bitcast(FP16)[:, k * 128:(k + 1) * 128],
                                    q_st[:, u, 4 * k:4 * k + 4].rearrange("p h c e -> p (h c e)"), ident_h[:, :])
                i.then_inc(s["c_turn2"], 1)

            def scores1_t(t, u):
                pe.wait_ge(s["c_qbd"], t + 1)
                if not (isinstance(t, int) and t == 0):
                    pe.wait_ge(s["c_exp"], t)
                for b in range(TB):
                    for k in range(4):
                        i = g.matmul(bank[4 + k // 2][64 * b:64 * b + 64, (k % 2) * 256:(k % 2) * 256 + 256],
                                     kT1[:, u, k, 64 * b:64 * b + 64], q_bd[:, u, k, b].rearrange("p i k -> p (i k)"), start=True, stop=True)
                i.then_inc(s["c_sT"], 1)

            def attend1(t, u):
                pe.wait_ge(s["c_pl"], t + 1)
                pe.wait_ge(s["c_v"], t + 1)
                if not (isinstance(t, int) and t == 0):
                    pe.wait_ge(s["c_x3"], t)
                for p in range(H1 // 2):
                    for n, (i, j) in enumerate(((0, 0), (0, 1), (1, 0))):
                        last = g.matmul(bank[6][:, p * 34:p * 34 + 34], p1_s[:, u, i, p * 128:(p + 1) * 128],
                                        v_bd[:, u, j, p].rearrange("p b e -> p (b e)"), start=n == 0, stop=n == 2)
                last.then_inc(s["c_pv"], 1)

            pe.wait_ge(s["d_ws"], E)
            pe.wait_ge(s["d_wl"], E)
            turn_kq(0, 0)
            scores1(0, 0)
            turn_q2(0, 0)
            turn_kq(1, 1)
            scores1(1, 1)
            pe.wait_ge(s["b_x2"], NG)
            scores1_t(0, 0)

            def turn1(t, u):
                more = not isinstance(t, int) or t + 1 < NT
                more2 = not isinstance(t, int) or t + 2 < NT
                if more2:
                    turn_kq(t + 2, u)
                if more:
                    turn_q2(t + 1, 1 - u)
                attend1(t, u)
                if more2:
                    scores1(t + 2, u)
                if more:
                    scores1_t(t + 1, 1 - u)

            zT_chunks = [0]

            def route_logits(r):
                n = ROUTED[r][1]
                pe.wait_ge(s["r_low"], r + 1)
                if r:
                    pe.wait_ge(s["r_slots"], r)
                for at in range(0, n, 4):
                    zb = bank[6 if r and at else 7][:, :].bitcast(FP16)
                    if at and not r:
                        pe.wait_ge(s["r_zTs"], zT_chunks[0])
                    for j in range(at, min(at + 4, n)):
                        for hl in range(2):
                            k = 2 * (j - at) + hl
                            i = g.transpose(zb[:, k * D:(k + 1) * D],
                                            row_buf[r][:, 0, j, hl * (D // 2):(hl + 1) * (D // 2)].bitcast(FP16), ident_h[:, :])
                    i.then_inc(s["r_zT"], 1)
                    zT_chunks[0] += 1
                pe.wait_ge(s["r_zTs"], zT_chunks[0])
                for j in range(n):
                    for m, (a_, b_) in enumerate(((0, 0), (0, 1), (1, 0))):
                        i = g.matmul(bank[7][:, j * E:(j + 1) * E], zTr[:, j, a_], rwT_s[:, b_], start=m == 0, stop=m == 2)
                i.then_inc(s["r_log"], 1)

            def route_ranks(r):
                n = ROUTED[r][1]
                pe.wait_ge(s["r_pick"], r + 1)
                flat = picked[:, 0:n, :].rearrange("p j e -> p (j e)")
                g.matmul(bank[7][:, 0:n * E], tri[:, :], flat, start=True, stop=False)
                for k in range(1, n):
                    g.matmul(bank[7][:, k * E:n * E], ones_sq[:, :], flat[:, 0:(n - k) * E], start=False, stop=k == n - 1)
                for j in range(n):
                    i = g.matmul(bank[7][:, RT * E:RT * E + E], ones_sq[:, :], picked[:, j, :], start=j == 0, stop=j == n - 1)
                i.then_inc(s["r_rank"], 1)

            turns_and_routes(pe, turn1, {12: lambda: route_logits(0), 14: lambda: route_ranks(0)})
            route_logits(1)
            route_ranks(1)
            for k in range(E, 2 * E):
                weights_turn(k)

            def turn_rows(k, j):
                pe.wait_ge(s[f"e_row{j}"], 16 * (k // 4 + 1) if isinstance(k, int) else 4 * (k - j) + 16)
                if after(k, 2):
                    pe.wait_ge(s["e_xT"], k - 1)
                r16 = rows[:, j, 0:D].bitcast(FP16)
                for hl in range(2):
                    i = g.transpose(bank[j % 2][:, 0:128].bitcast(FP16)[:, hl * 128:(hl + 1) * 128], r16[:, hl * 128:(hl + 1) * 128], ident_h[:, :])
                i.then_inc(s["e_turn"], 1)

            def up(k, j, expert):
                pe.wait_ge(s["e_xT"], k + 1)
                if after(k, 4):
                    pe.wait_ge(s["e_hid"], k - 3)
                for c in range(FC):
                    for n, (a_, b_) in enumerate(((0, 0), (0, 1), (1, 0))):
                        i = g.matmul(bank[UP_BANKS[j]][:, c * 128:(c + 1) * 128], w1_s[:, a_, bass.ds(expert * F + c * 128, 128)],
                                     rT[:, j % 2, b_], start=n == 0, stop=n == 2)
                i.then_inc(s["e_up"], 1)

            def down(k, j, expert):
                pe.wait_ge(s["e_hid"], k + 1)
                if after(k, 2):
                    pe.wait_ge(s["e_out"], k - 1)
                dst = bank[4 + j % 2][:, 0:D]
                for hl in range(2):
                    g.matmul(dst, ones_row[:, :], b2_s[:, hl, bass.ds(expert * D, D)], start=hl == 0, stop=False)
                for c in range(FC):
                    i = g.matmul(dst, hid[:, j, c], w2T[:, bass.ds(expert * F + c * 128, 128)], start=False, stop=c == FC - 1)
                i.then_inc(s["e_y"], 1)

            pe.wait_ge(s["r_exps"], 1)
            pe.wait_ge(s["d_ws"], 2 * E)
            pe.wait_ge(s["small_up"], 3)
            pe.wait_ge(s["c_x3"], NT)
            turn_rows(0, 0)
            turn_rows(1, 1)
            digits = pe.value_load(experts_i[0:1, 0:1], min_val=0, max_val=E ** DIGITS - 1)
            first_two = [(digits // E ** n) % E for n in range(2)]
            up(0, 0, first_two[0])
            turn_rows(2, 2)
            up(1, 1, first_two[1])

            def expert_turn(k, j, expert):
                if not isinstance(k, int) or k + 3 < SLOTS:
                    turn_rows(k + 3, (j + 3) % 4)
                if not isinstance(k, int) or k + 2 < SLOTS:
                    up(k + 2, (j + 2) % 4, expert[j + 2])
                down(k, j, expert[j])

            slots(pe, expert_turn, experts_i, 2)


_INS = ["x", "ctx_1024", "g_xattn", "g_ffn", "L0_xattn_gamma_x", "L0_xattn_beta_x", "L0_xattn_gamma_l", "L0_xattn_beta_l",
        "L0_xattn_Wq", "L0_xattn_Wkv", "L0_xattn_Wo", "L0_ffn_W_r", "L0_ffn_W_k", "L0_ffn_W_v", "L0_ffn_mu_r", "L0_ffn_mu_k",
        "L1_ffn_router_w", "L1_ffn_w1", "L1_ffn_b1", "L1_ffn_w2", "L1_ffn_b2"]


def _constants():
    f32 = np.float32

    def angles(width):
        inv = (1.0 / f32(10000.0) ** (np.arange(0, width, 2, dtype=f32) / f32(width))).astype(f32)
        return (np.arange(T, dtype=f32)[:, None] * inv[None, :]).astype(f32)

    th = angles(HD0)
    cos, sin = np.cos(th).astype(f32).T, np.sin(th).astype(f32).T
    cos0 = np.ascontiguousarray(np.concatenate([cos, cos, cos, cos], 0))
    sin0 = np.ascontiguousarray(np.concatenate([-sin, sin, -sin, sin], 0))
    th = angles(HD1)
    cos, sin = np.cos(th).astype(f32), np.sin(th).astype(f32)
    cos1 = np.tile(np.concatenate([cos, cos], 1), (2, 1))
    sin1 = np.tile(np.concatenate([-sin, sin], 1), (2, 1))
    slope = np.array([2.0 ** (-8.0 * i / H1) for i in range(1, H1 + 1)]).astype(f32).astype(np.float64) * HD1 ** 0.5
    pos = np.tile(np.arange(T, dtype=np.float64), 2)
    q_ext, k_ext = np.zeros((128, H1, 8), np.float16), np.zeros((128, H1, 8), np.float16)
    shift = -slope[None, :] * pos[:, None]
    q_ext[:, :, 0] = slope
    q_ext[:, :, 1] = slope - slope.astype(np.float16)
    q_ext[:, :, 2] = shift
    q_ext[:, :, 3] = shift - shift.astype(np.float16)
    k_ext[:, :, 0] = k_ext[:, :, 1] = pos[:, None]
    k_ext[:, :, 2:5] = 1.0
    p = np.arange(128)
    tri = (p[:, None] < p[None, :]).astype(np.float16)
    tile_no = np.tile(np.arange(SLOTS, dtype=f32), (128, 1))
    region = np.tile(np.arange(E, dtype=f32) * REG, (128, 1))
    tok_id = (p[:, None] + 128 * np.arange(NT)[None, :]).astype(f32)
    pad_at = (2 * TOK + p[:, None] + 128 * np.arange(E + 1)[None, :]).astype(f32)
    return {"cos0": cos0, "sin0": sin0, "cos1": cos1, "sin1": sin1, "q_ext": q_ext, "k_ext": k_ext,
            "tri": tri, "tile_no": tile_no, "region": region, "tok_id": tok_id, "pad_at": pad_at}


def kernel(**inputs):
    import numpy as _np
    import concourse.bacc as _bacc
    from concourse import mybir as _mybir
    from concourse.bass_utils import run_bass_kernel_spmd as _run

    nc = _bacc.Bacc("TRN2", target_bir_lowering=False, num_devices=1)
    arrays, args = {}, {}
    held = {n: _np.ascontiguousarray(inputs[n]) for n in _INS}
    held.update(_constants())
    for name, v in held.items():
        arrays[f"in_{name}"] = v
        args[name] = nc.dram_tensor(f"in_{name}", v.shape, _mybir.dt.from_np(v.dtype), kind="ExternalInput").ap()
    out = nc.dram_tensor("out_0", (B, T, D), _mybir.dt.float32, kind="ExternalOutput").ap()
    program(nc, args, out)
    r = _run(nc, [arrays], core_ids=[0])
    return r.results[0]["out_0"]
```
